# Optimizing a Trainium2 kernel written in Bass

```python
import numpy as np
import jax
import jax.numpy as jnp

def _softmax(x, axis=-1):
    return jax.nn.softmax(x, axis=axis)

def _gelu(x):
    return jax.nn.gelu(x, approximate=True)

def _silu(x):
    return jax.nn.silu(x)

def _sigmoid(x):
    return jax.nn.sigmoid(x)

def _layernorm(x, axis=-1, eps=1e-05):
    m = jnp.mean(x, axis=axis, keepdims=True)
    v = jnp.var(x, axis=axis, keepdims=True)
    return (x - m) / jnp.sqrt(v + eps)

def _scatter_add(tgt, idx, src, axis=0):
    return tgt.at[idx].add(src)

def _segment_sum(src, seg, n):
    return jax.ops.segment_sum(src, seg, n)
kernel_name = 'mk_audio_tower_d1_tok_audfeat1024_r4_abd26c'

def setup_inputs(seed: int=0):
    np.random.seed(seed)
    _w = jnp.asarray

    def _rec_inputs():
        import jax
        import jax.numpy as jnp
        _rk = jax.random.key(seed)
        x = -0.000125008 + 0.999885 * jax.random.normal(jax.random.fold_in(_rk, 1), (16, 2048, 64), jnp.float32)
        return x
    x = _rec_inputs()

    def _L0_tok_setup():
        import jax, jax.numpy as jnp
        import numpy as np
        PATCH_LEN = 16
        STRIDE = 8
        D_MODEL = 256
        INPUT_DIM = 64
        B, L = (64, 2048)
        PATCH_DIM = INPUT_DIM * PATCH_LEN
        EPS = 1e-05

        def _patchify(x):
            n_patches = (L - PATCH_LEN) // STRIDE + 1
            starts = jnp.arange(n_patches) * STRIDE
            idx = starts[:, None] + jnp.arange(PATCH_LEN)
            patches = x[:, idx, :]
            patches = jnp.transpose(patches, (0, 1, 3, 2))
            return patches.reshape(x.shape[0], n_patches, PATCH_DIM)
        key = jax.random.key(seed)
        k1, k2, k3 = jax.random.split(key, 3)
        x = jax.random.normal(k1, (B, L, INPUT_DIM), dtype=jnp.float32)
        W = jax.random.normal(k2, (PATCH_DIM, D_MODEL), dtype=jnp.float32) / np.sqrt(PATCH_DIM)
        b = jnp.zeros((D_MODEL,), dtype=jnp.float32)
        gamma = jnp.ones((PATCH_DIM,), dtype=jnp.float32)
        beta = jnp.zeros((PATCH_DIM,), dtype=jnp.float32)
        return {'x': x, 'W': W, 'b': b, 'gamma': gamma, 'beta': beta}
    _L0_tok_all = _L0_tok_setup()
    _L0_tok_in = {k: v for k, v in _L0_tok_all.items() if k in ('W', 'b', 'gamma', 'beta')}
    del _L0_tok_all

    def _L0_attn_setup():
        import jax, jax.numpy as jnp
        import numpy as np
        import math
        B, S, D, H, DH = (4, 512, 256, 8, 64)
        SCALE = 1.0 / math.sqrt(DH)
        EPS = 1e-08

        def _xavier(key, shape, gain):
            std = gain * np.sqrt(2.0 / (shape[0] + shape[1]))
            return (jax.random.normal(key, shape, jnp.float32) * std).astype(jnp.float32)

        def _stable_lse(a, b):
            m = jnp.maximum(a, b)
            return m + jnp.log1p(jnp.exp(-jnp.abs(a - b)))
        key = jax.random.key(seed)
        ks = jax.random.split(key, 7)
        return {'x': jax.random.normal(ks[0], (B, S, D), jnp.float32), 'W_q': _xavier(ks[1], (H * DH, D), 0.1), 'W_k': _xavier(ks[2], (H * DH, D), 0.1), 'W_v': _xavier(ks[3], (D, D), 1.0), 'W_alpha_w': jax.random.normal(ks[4], (H * DH, D), jnp.float32) * 0.01, 'W_alpha_b': jnp.ones((H * DH,), jnp.float32), 'W_o': _xavier(ks[5], (D, D), 0.1)}
    _L0_attn_all = _L0_attn_setup()
    _L0_attn_in = {k: v for k, v in _L0_attn_all.items() if k in ('W_q', 'W_k', 'W_v', 'W_alpha_w', 'W_alpha_b', 'W_o')}
    del _L0_attn_all

    def _L0_ffn_setup():
        import jax, jax.numpy as jnp
        import numpy as np
        B, T, E, C, H, G = (2, 512, 8, 256, 512, 16)
        key = jax.random.key(seed)
        ks = jax.random.split(key, 7)
        return {'hidden_states': jax.random.normal(ks[0], (B, T, C), jnp.float32), 'w_red': jax.random.normal(ks[1], (C, G), jnp.float32) * 0.02, 'wg': jax.random.normal(ks[2], (E, G), jnp.float32), 'W1': jax.random.normal(ks[3], (E, C, H), jnp.float32) * 0.02, 'b1': jax.random.normal(ks[4], (E, H), jnp.float32) * 0.02, 'W2': jax.random.normal(ks[5], (E, H, C), jnp.float32) * 0.02, 'b2': jax.random.normal(ks[6], (E, C), jnp.float32) * 0.02}
    _L0_ffn_all = _L0_ffn_setup()
    _L0_ffn_in = {k: v for k, v in _L0_ffn_all.items() if k in ('w_red', 'wg', 'W1', 'b1', 'W2', 'b2')}
    del _L0_ffn_all
    return {'x': x, 'L0_tok_W': _L0_tok_in['W'], 'L0_tok_b': _L0_tok_in['b'], 'L0_tok_gamma': _L0_tok_in['gamma'], 'L0_tok_beta': _L0_tok_in['beta'], 'L0_attn_W_q': _L0_attn_in['W_q'], 'L0_attn_W_k': _L0_attn_in['W_k'], 'L0_attn_W_v': _L0_attn_in['W_v'], 'L0_attn_W_alpha_w': _L0_attn_in['W_alpha_w'], 'L0_attn_W_alpha_b': _L0_attn_in['W_alpha_b'], 'L0_attn_W_o': _L0_attn_in['W_o'], 'L0_ffn_w_red': _L0_ffn_in['w_red'], 'L0_ffn_wg': _L0_ffn_in['wg'], 'L0_ffn_W1': _L0_ffn_in['W1'], 'L0_ffn_b1': _L0_ffn_in['b1'], 'L0_ffn_W2': _L0_ffn_in['W2'], 'L0_ffn_b2': _L0_ffn_in['b2']}

def reference(x, L0_tok_W, L0_tok_b, L0_tok_gamma, L0_tok_beta, L0_attn_W_q, L0_attn_W_k, L0_attn_W_v, L0_attn_W_alpha_w, L0_attn_W_alpha_b, L0_attn_W_o, L0_ffn_w_red, L0_ffn_wg, L0_ffn_W1, L0_ffn_b1, L0_ffn_W2, L0_ffn_b2):
    import jax
    import jax.numpy as jnp

    def _L0_tok_ref(x, W, b, gamma, beta):
        import jax, jax.numpy as jnp
        import numpy as np
        PATCH_LEN = 16
        STRIDE = 8
        D_MODEL = 256
        INPUT_DIM = 64
        B, L = (64, 2048)
        PATCH_DIM = INPUT_DIM * PATCH_LEN
        EPS = 1e-05

        def _patchify(x):
            n_patches = (L - PATCH_LEN) // STRIDE + 1
            starts = jnp.arange(n_patches) * STRIDE
            idx = starts[:, None] + jnp.arange(PATCH_LEN)
            patches = x[:, idx, :]
            patches = jnp.transpose(patches, (0, 1, 3, 2))
            return patches.reshape(x.shape[0], n_patches, PATCH_DIM)
        p = _patchify(x)
        mu = jnp.mean(p, axis=-1, keepdims=True)
        var = jnp.mean(jnp.square(p - mu), axis=-1, keepdims=True)
        p_norm = (p - mu) * jax.lax.rsqrt(var + EPS) * gamma + beta
        return jnp.einsum('bnk,kd->bnd', p_norm, W) + b

    def _L0_attn_ref(x, W_q, W_k, W_v, W_alpha_w, W_alpha_b, W_o):
        import jax, jax.numpy as jnp
        import numpy as np
        import math
        B, S, D, H, DH = (4, 512, 256, 8, 64)
        SCALE = 1.0 / math.sqrt(DH)
        EPS = 1e-08

        def _xavier(key, shape, gain):
            std = gain * np.sqrt(2.0 / (shape[0] + shape[1]))
            return (jax.random.normal(key, shape, jnp.float32) * std).astype(jnp.float32)

        def _stable_lse(a, b):
            m = jnp.maximum(a, b)
            return m + jnp.log1p(jnp.exp(-jnp.abs(a - b)))
        Bx, Sx, _ = x.shape
        q = (x @ W_q.T).reshape(Bx, Sx, H, DH)
        k = (x @ W_k.T).reshape(Bx, Sx, H, DH)
        v = x @ W_v.T
        b = (q * k).sum(-1) * SCALE
        alpha = (x @ W_alpha_w.T + W_alpha_b).reshape(Bx, Sx, H, DH)
        a = -jax.nn.softplus(alpha).sum(-1)
        vs = jnp.sign(v)
        vs = jnp.where(vs == 0, jnp.ones_like(vs), vs)
        vl = jnp.log(jnp.abs(v) + EPS)
        ln0 = b[:, 0]
        nm0 = b[:, 0, :, None] + vl[:, 0, None, :]
        sg0 = jnp.broadcast_to(vs[:, 0, None, :], nm0.shape)
        y0 = (sg0 * jnp.exp(nm0 - ln0[..., None])).sum(-2)

        def step(carry, inp):
            ln, nm, sg = carry
            a_t, b_t, vl_t, vs_t = inp
            ln = _stable_lse(a_t + ln, b_t)
            dec = a_t[..., None] + nm
            new = b_t[..., None] + vl_t[:, None, :]
            m = jnp.maximum(dec, new)
            ssum = sg * jnp.exp(dec - m) + vs_t[:, None, :] * jnp.exp(new - m)
            nsg = jnp.sign(ssum)
            nsg = jnp.where(nsg == 0, jnp.ones_like(nsg), nsg)
            nm = m + jnp.log(jnp.abs(ssum) + EPS)
            y = (nsg * jnp.exp(nm - ln[..., None])).sum(-2)
            return ((ln, nm, nsg), y)
        xs = (jnp.moveaxis(a[:, 1:], 1, 0), jnp.moveaxis(b[:, 1:], 1, 0), jnp.moveaxis(vl[:, 1:], 1, 0), jnp.moveaxis(vs[:, 1:], 1, 0))
        _, ys = jax.lax.scan(step, (ln0, nm0, sg0), xs)
        y = jnp.concatenate([y0[:, None, :], jnp.moveaxis(ys, 0, 1)], axis=1)
        return y @ W_o.T

    def _L0_ffn_ref(hidden_states, w_red, wg, W1, b1, W2, b2):
        import jax, jax.numpy as jnp
        import numpy as np
        B, T, E, C, H, G = (2, 512, 8, 256, 512, 16)
        b, t, c = hidden_states.shape
        x = hidden_states.reshape(-1, c)
        x_red = x @ w_red
        wg_n = wg / jnp.maximum(jnp.linalg.norm(wg, axis=1, keepdims=True), 0.0001)
        logits = x_red @ wg_n.T
        gates = jax.nn.softmax(logits, axis=1)
        scores = jnp.max(gates, axis=1)
        idx = jnp.argmax(gates, axis=1)
        h = jnp.einsum('nc,ech->neh', x, W1) + b1[None]
        h = jnp.take_along_axis(h, idx[:, None, None], axis=1)[:, 0, :]
        h = jax.nn.gelu(h, approximate=False)
        o = jnp.einsum('nh,ehc->nec', h, W2) + b2[None]
        o = jnp.take_along_axis(o, idx[:, None, None], axis=1)[:, 0, :]
        o = o * scores[:, None]
        return o.reshape(b, t, c)
    h = _L0_tok_ref(x, L0_tok_W, L0_tok_b, L0_tok_gamma, L0_tok_beta)
    h = h + _L0_attn_ref(_layernorm(h, axis=-1), L0_attn_W_q, L0_attn_W_k, L0_attn_W_v, L0_attn_W_alpha_w, L0_attn_W_alpha_b, L0_attn_W_o)
    h = h + _L0_ffn_ref(_layernorm(h, axis=-1), L0_ffn_w_red, L0_ffn_wg, L0_ffn_W1, L0_ffn_b1, L0_ffn_W2, L0_ffn_b2)
    return h

_drawn_inputs = setup_inputs


def setup_inputs(seed=0):
    import zlib

    import numpy as np

    out = dict(_drawn_inputs(seed))
    spreads = {'L0_tok_b': (0.0, 0.1),
     'L0_tok_gamma': (1.0, 0.2),
     'L0_tok_beta': (0.0, 0.1),
     'L0_attn_W_alpha_b': (1.0, 0.6)}
    factors = {'L0_attn_W_q': 64.0,
     'L0_attn_W_k': 64.0,
     'L0_ffn_w_red': 5.156,
     'L0_ffn_wg': 5.201,
     'L0_ffn_W1': 5.155,
     'L0_ffn_b1': 8.0,
     'L0_ffn_W2': 5.01,
     'L0_ffn_b2': 8.0,
     'L0_attn_W_alpha_w': 4.801}
    for name, (base, spread) in spreads.items():
        noise = np.random.default_rng([zlib.crc32(name.encode()), seed]).standard_normal(out[name].shape)
        drawn = base * np.exp(spread * noise) if base else spread * noise
        out[name] = jnp.asarray(drawn.astype(out[name].dtype))
    for name, factor in factors.items():
        out[name] = (out[name] * factor).astype(out[name].dtype)
    return out
```

```python
from contextlib import ExitStack

import numpy as np

import concourse.bass as bass
from concourse import mybir

F32 = mybir.dt.float32
F16 = mybir.dt.float16
I32 = mybir.dt.int32
U32 = mybir.dt.uint32
ALU = mybir.AluOpType
ACT = mybir.ActivationFunctionType
AX = mybir.AxisListType.X

P = 128
B, L, DIN = 16, 2048, 64
STRIDE, PATCH = 8, 16
GROUP = STRIDE * DIN
NG = L // STRIDE
NTOK = (L - PATCH) // STRIDE + 1
KG = GROUP // P
KC = 2 * KG
D = 256
DC = D // P
HEADS, DH = 8, 64
HD = HEADS * DH
E, FF = 8, 512
FC = FF // P
TILES = 2 * B
CH = 32
NCH = 2 * P // CH
CT = P // CH
ROWC = D + 4
SLOTS = (B * NTOK + E * (P - 1)) // P
RING = 6
ROUNDS, REST = divmod(SLOTS, RING)
LN_EPS = 1e-5
V_EPS = 1e-8
NEG = -1.0e30
OUT_OF_RANGE = 1 << 20
WS = 64.0
SPAN = CH + 1


class Steps:

    def __init__(self, engine, sem, per):
        self.engine, self.sem, self.per = engine, sem, per

    def begin(self, n):
        self.base, self.done = n * self.per, 0

    def step(self, instruction):
        instruction.then_inc(self.sem, 1)
        self.done += 1

    def settle(self, hold=lambda engine, value: value):
        self.engine.wait_ge(self.sem, hold(self.engine, self.base + self.done))

    def end(self):
        assert self.done == self.per, (self.done, self.per)


def build(nc, x, tok_W, tok_b, tok_gamma, tok_beta, W_q, W_k, W_v, W_aw, W_ab, W_o,
          w_red, wg, W1, b1, W2, b2, out):
    with ExitStack() as ctx:
        def sb(name, shape, dt=F32):
            return ctx.enter_context(nc.sbuf_tensor(name, shape, dt))

        def sem(name):
            return ctx.enter_context(nc.semaphore(name))

        routed = nc.dram_tensor("routed_rows", [SLOTS * P, ROWC], F32, kind="Internal").ap()
        routed_tiles = routed.rearrange("(i p) c -> i p c", p=P)
        out_rows = out.rearrange("b n d -> (b n) d")

        banks = ctx.enter_context(nc.psum_tensor("banks", [P, 8, 512], F32))

        rows = sb("rows", [P, TILES, ROWC])
        vo = sb("vo", [P, TILES, D])
        w1h = sb("w1h", [P, E * DC, FF], F16)
        w1l = sb("w1l", [P, E * DC, FF], F16)
        w2h = sb("w2h", [P, E * FC, D], F16)
        w2l = sb("w2l", [P, E * FC, D], F16)
        bsum = sb("bsum", [P, 2, B * HEADS])
        asum = sb("asum", [P, 2, B * HEADS])
        wrg = sb("wrg", [P, DC, E])
        ident = sb("ident", [P, P])
        shift = sb("shift", [P, P])
        corner = sb("corner", [P, P])
        ones = sb("ones", [P, P])
        before = sb("before", [P, P])
        chunk_mask = sb("chunk_mask", [P, CT, CH])
        mask4 = sb("mask4", [P, CT, HEADS])
        last_row = sb("last_row", [P, 1])
        decay_in = sb("decay_in", [P, HEADS, SPAN])
        head_state_in = sb("head_state_in", [P, 2 * P])
        sel_chunk = sb("sel_chunk", [NCH, 2, P])
        sel_head = sb("sel_head", [16, P])
        one_col = sb("one_col", [P, 1])
        minus_half = sb("minus_half", [P, 1])
        plus_half = sb("plus_half", [E, 1])
        minus_veps = sb("minus_veps", [P, 1])
        init_rows = sb("init_rows", [P, ROWC])
        colsum = sb("colsum", [P, D])
        tok_bias = sb("tok_bias", [P, D])
        alpha_bias = sb("alpha_bias", [P, HD])
        b1t = sb("b1t", [P, E, FC])

        early = sb("early", [P, 6272])
        wtok = early[:, 0:2048].rearrange("p (k d) -> p k d", k=KC)
        gT = early[:, 2048:3076].rearrange("p (k g) -> p k g", k=KG)
        xg = early[:, 3076:4100].rearrange("p (j r) -> p j r", j=2)
        q_sb = early[:, 4100:4612]
        qk = early[:, 4612:5124]
        al = early[:, 5124:5636]
        sp = early[:, 5636:6148]
        beta_wide = early[:, 4100:5124].rearrange("p (k m) -> p k m", k=KC)
        proj = sb("proj", [P, 3072])
        wqka_h = proj[:, 0:1536].bitcast(F16).rearrange("p (c o) -> p c o", c=DC)
        wqka_l = proj[:, 1536:3072].bitcast(F16).rearrange("p (c o) -> p c o", c=DC)
        wv_h = sb("wv_h", [P, DC, D], F16)
        wv_l = sb("wv_l", [P, DC, D], F16)
        wo_h = sb("wo_h", [P, DC, D], F16)
        wo_l = sb("wo_l", [P, DC, D], F16)
        xn = sb("xn", [P, 2, D])
        xnT_h = sb("xnT_h", [P, DC, 2 * P], F16)
        xnT_l = sb("xnT_l", [P, DC, 2 * P], F16)
        u = sb("u", [P, DC, 2 * P])
        vT_h = sb("vT_h", [P, DC, 2 * P], F16)
        vT_l = sb("vT_l", [P, DC, 2 * P], F16)
        gst6 = sb("gst6", [P, 2, 6])
        gst = sb("gst", [P, 2, 2])
        lst6 = sb("lst6", [P, 6])
        sm = sb("sm", [P, 12])
        stage1 = sb("stage1", [P, 512])
        stage2 = sb("stage2", [P, 512])
        gam_raw = sb("gam_raw", [P, PATCH])
        bet_raw = sb("bet_raw", [P, PATCH])
        b1_sb = sb("b1_sb", [E * FC, P])
        gam = sb("gam", [P, KC])
        bet = sb("bet", [P, KC])

        late = {}
        at = 0
        for name, cols in (("bT", 256), ("aT", 256), ("m", 257), ("ea", 256), ("eb", 256), ("r", 257), ("lam", 256)):
            late[name] = proj[:, at:at + cols]
            at += cols
        lamB = early[0:NCH, 0:B * HEADS * SPAN].rearrange("p (b h s) -> p b h s", b=B, h=HEADS)
        lamQ = early[0:16, 4224:4224 + 8 * 256].rearrange("p (r t) -> p r t", r=8)
        resp = sb("resp", [P, HEADS + 1, SPAN])
        wsum = sb("wsum", [P, CH])
        wbd = sb("wbd", [P, 4, P])
        ends = sb("ends", [P, 4, P])
        qst = sb("qst", [P, 2 * P])
        lst = sb("lst", [P, D])
        xn2 = xn
        xT2 = u

        flat = vo[:].rearrange("p t d -> p (t d)")
        at = 0

        def over(cols):
            nonlocal at
            at += cols
            assert at <= TILES * D
            return flat[:, at - cols:at]

        lg = over(256).rearrange("p (t e) -> p t e", e=E)
        oh = over(256).rearrange("p (t e) -> p t e", e=E)
        t8 = over(256).rearrange("p (t e) -> p t e", e=E)
        tot = over(256).rearrange("p (t e) -> p t e", e=E)
        cum = over(256).rearrange("p (t e) -> p t e", e=E)
        zer = over(256)
        cmp8 = over(SLOTS * E).rearrange("p (i e) -> p i e", e=E)
        rt = over(32 * 4)
        mx, mw, sumexp, posf = (rt[:, 32 * i:32 * i + 32] for i in range(4))
        r8 = over(8 * 4)
        ntile, tend, tstart, _ = (r8[:, 8 * i:8 * i + 8] for i in range(4))
        slotf = over(SLOTS)
        posi = over(32).bitcast(I32)
        sloti = over(SLOTS).bitcast(I32)
        b2w = over(E * D).rearrange("p (e d) -> p e d", e=E)
        xr = over(RING * ROWC).rearrange("p (w c) -> p w c", w=RING)
        xnD = over(D)
        xh = over(D // 2).bitcast(F16).rearrange("p (c t) -> p c t", c=DC)
        xl = over(D // 2).bitcast(F16).rearrange("p (c t) -> p c t", c=DC)
        gel = over(FF).rearrange("p (f t) -> p f t", f=FC)
        gh = over(FF // 2).bitcast(F16).rearrange("p (f t) -> p f t", f=FC)
        gl = over(FF // 2).bitcast(F16).rearrange("p (f t) -> p f t", f=FC)
        yt = over(D)
        yo = proj[:, 0:RING * D].rearrange("p (w d) -> p w d", w=RING)
        valid = sb("valid", [P, TILES])
        pad_pos = sb("pad_pos", [P, TILES])
        rank_w = sb("rank_w", [P, E])
        thr = sb("thr", [P, 32])
        slot_no = sb("slot_no", [P, SLOTS])
        ii = sb("ii", [P, 64], I32)
        oid = sb("oid", [P, RING], I32)
        wred_sb = sb("wred_sb", [P, DC, 16])
        wg_sb = sb("wg_sb", [E, 16])
        wg_sq = sb("wg_sq", [E, 16])
        wg_norm = sb("wg_norm", [E, 2])
        router_T = sb("router_T", [16, D + E])
        tokc = sb("tokc", [P, D])
        tok_b_wide = sb("tok_b_wide", [P, D])

        raw = flat[:, 0:16 * D].rearrange("p (o c) -> p o c", c=D)

        names = """consts consts2 const_steps const_steps_p init_out wload wraw_ready misc_in tok_w_in wsplit_hi wsplit_lo
            beta_wide_ready bias_ready gamma_done colsum_ready tokprep
            router_norm router_root router_steps router_prep router_t router_weights router_mm router_done
            x_in xt_ready xt_evac gst_done gst_steps tok_done h_done ln_steps var_ready rstd_ready xn_ready
            xnt_ready xhi_done xlo_done q_ready k_ready al_ready q_copied qk_done al_copied act_steps
            ln_done sp_steps sp_done vt_ready u_steps u_done vh_done vl_done vo_ready vo_copied
            w_in w_hi w_lo
            ba_ready gate_steps gate_exp gate_args lam_done lam_b lam_q lb_zero
            lb_ready lb_used es_steps es_ready l_ready l_copied out_ready h2_done h2_steps var2_ready rstd2_ready
            xn2_ready t2_ready t2_evac lg_done qb_ready q_done
            r_steps r_args r_exp oh_ready counts route_ready b2_in scattered
            row_in_0 row_in_1 row_in_2 row_in_3 row_in_4 row_in_5 xd_ready xdt_ready xdh_done xdl_done m1_ready gelu_done g_steps g_done
            m2_ready yt_done y_steps y_done y_out_0 y_out_1 y_out_2 y_out_3 y_out_4 y_out_5""".split()
        s = {n: sem(n) for n in names}

        def bank(i, n=512):
            return banks[:, i, 0:n]

        def apart(engine, value):
            if not isinstance(value, int):
                value = engine.snap(engine.to_reg(value))
            engine.wait_ge(s["consts"], 1)
            return value

        block = ctx.enter_context(nc.Block())

        @block.sync
        def _(sp_):
            for m, w in enumerate((W_q, W_k, W_aw)):
                sp_.dma_start(raw[:, 4 * m:4 * m + 4, :], w.rearrange("(o p) c -> p o c", p=P)).then_inc(s["wraw_ready"], 16)
            sp_.dma_start(raw[:, 12:14, :], W_v.rearrange("(o p) c -> p o c", p=P)).then_inc(s["wraw_ready"], 16)
            sp_.dma_start(raw[:, 14:16, :], W_o.rearrange("(o p) c -> p o c", p=P)).then_inc(s["wraw_ready"], 16)

            def load_x(b):
                if not (isinstance(b, int) and b == 0):
                    sp_.wait_ge(s["xt_ready"], 2 * b)
                    sp_.wait_ge(s["gst_done"], b)
                sp_.dma_start(xg, x[b].rearrange("(j g r) c -> g j (r c)", j=2, r=STRIDE)).then_inc(s["x_in"], 16)

            def load_expert_part(n):
                if not (isinstance(n, int) and n == 0):
                    sp_.wait_ge(s["w_lo"], 2 * n)
                sp_.dma_start(stage1[:], W1.rearrange("e (c p) f -> (e c) p f", p=P)[n]).then_inc(s["w_in"], 16)
                sp_.dma_start(stage2[:].rearrange("p (q d) -> p q d", q=2),
                              W2.rearrange("e (n q p) d -> (e n) p q d", q=2, p=P)[n]).then_inc(s["w_in"], 16)

            for t2 in range(2):
                half = slice(DIN * t2, DIN * t2 + DIN)
                sp_.dma_start(wtok[half], tok_W.rearrange("(d k t) o -> t d k o", k=KC, t=2)[t2]).then_inc(s["tok_w_in"], 16)
                sp_.dma_start(gam_raw[half, :], tok_gamma.rearrange("(d t) -> d t", t=PATCH)).then_inc(s["tok_w_in"], 16)
                sp_.dma_start(bet_raw[half, :], tok_beta.rearrange("(d t) -> d t", t=PATCH)).then_inc(s["tok_w_in"], 16)
            sp_.dma_start(tok_b_wide[:], tok_b.partition_broadcast(P)).then_inc(s["misc_in"], 16)
            sp_.dma_start(alpha_bias[:], W_ab.partition_broadcast(P)).then_inc(s["misc_in"], 16)
            sp_.dma_start(wred_sb[:], w_red.rearrange("(c p) g -> p c g", p=P)).then_inc(s["misc_in"], 16)
            sp_.dma_start(wg_sb[:], wg).then_inc(s["misc_in"], 16)
            sp_.dma_start(b1_sb[:], b1.rearrange("e (q p) -> (e q) p", p=P)).then_inc(s["misc_in"], 16)

            load_x(0)
            load_expert_part(0)
            load_x(1)
            load_x(2)
            sp_.wait_ge(s["consts2"], 1)
            per = SLOTS // (B - 3)
            assert per * (B - 3) == SLOTS
            with sp_.Fori(3, B) as b:
                load_expert_part(b - 2)
                load_x(b)
                for n in range(per):
                    sp_.dma_start(routed_tiles[per * (b - 3) + n], init_rows[:]).then_inc(s["init_out"], 16)
            load_expert_part(B - 2)
            load_expert_part(B - 1)

            sp_.wait_ge(s["lam_done"], 1)
            sp_.wait_ge(s["lb_zero"], 1)
            for c in range(NCH):
                sp_.dma_start(lamB[c:c + 1, :, :, 1:SPAN], late["lam"][:, CH * c:CH * c + CH]).then_inc(s["lam_b"], 16)

            sp_.wait_ge(s["lg_done"], TILES)
            sp_.dma_start(b2w, b2.partition_broadcast(P)).then_inc(s["b2_in"], 16)
            sp_.wait_ge(s["scattered"], 16 * TILES)

            def load_rows(i, w, first=False):
                if not first:
                    sp_.wait_ge(s["y_done"], i - RING + 1)
                sp_.dma_start(xr[:, w, :], routed_tiles[i]).then_inc(s[f"row_in_{w}"], 16)

            for w in range(RING):
                load_rows(w, w, True)
            with sp_.Fori(1, ROUNDS) as g:
                for w in range(RING):
                    load_rows(RING * g + w, w)
            for w in range(REST):
                load_rows(RING * ROUNDS + w, w)

        @block.tensor
        def _(pe):
            mm, tr = nc.tensor.matmul, nc.tensor.transpose

            pe.wait_ge(s["consts"], 1)
            pe.wait_ge(s["wraw_ready"], 80)
            for m in range(3):
                for c in range(DC):
                    for o in range(4):
                        last = tr(bank(2 * m + c)[:, o * P:o * P + P], raw[:, 4 * m + o, c * P:c * P + P], ident[:])
                    last.then_inc(s["wload"], 1)
            for m in range(2):
                for c in range(DC):
                    for o in range(2):
                        last = tr(bank(6 + m)[:, c * D + o * P:c * D + o * P + P], raw[:, 12 + 2 * m + o, c * P:c * P + P], ident[:])
                last.then_inc(s["wload"], 1)

            pe.wait_ge(s["beta_wide_ready"], 1)
            pe.wait_ge(s["wsplit_lo"], 2)
            for k in range(KC):
                last = mm(bank(0, D), beta_wide[:, k, :], wtok[:, k, :], start=(k == 0), stop=(k == KC - 1))
            last.then_inc(s["bias_ready"], 1)
            pe.wait_ge(s["gamma_done"], 1)
            for k in range(KC):
                last = mm(bank(1, D), ones[:], wtok[:, k, :], start=(k == 0), stop=(k == KC - 1))
            last.then_inc(s["colsum_ready"], 1)

            pe.wait_ge(s["router_prep"], 1)
            pe.wait_ge(s["wsplit_lo"], 4)
            for c in range(DC):
                tr(banks[0:16, 2, c * P:c * P + P], wred_sb[:, c, :], ident[:])
            tr(banks[0:16, 2, D:D + E], wg_sb[:, :], ident[0:E, 0:E]).then_inc(s["router_t"], 1)
            pe.wait_ge(s["router_weights"], 1)
            for c in range(DC):
                mm(banks[:, 3, c * E:c * E + E], router_T[:, c * P:c * P + P], router_T[:, D:D + E], start=True, stop=True)
            tr(banks[:, 3, 64:64 + E * FC], b1_sb[:], ident[0:E * FC, 0:E * FC]).then_inc(s["router_mm"], 1)

            def transpose_x(b, j):
                if j == 0:
                    pe.wait_ge(s["x_in"], 16 * (b + 1))
                if isinstance(b, int) and b == 0 and j == 0:
                    pe.wait_ge(s["tokprep"], 1)
                    pe.wait_ge(s["router_done"], 1)
                    pe.wait_ge(s["wsplit_lo"], 8)
                else:
                    pe.wait_ge(s["xt_evac"], 2 * b + j)
                for k in range(KG):
                    last = tr(bank(0)[:, k * P:k * P + P], xg[:, j, k * P:k * P + P], ident[:])
                last.then_inc(s["xt_ready"], 1)

            def tokenise(b, j):
                if j == 0:
                    pe.wait_ge(s["xt_evac"], 2 * b + 2)
                if not (isinstance(b, int) and b == 0):
                    pe.wait_ge(s["h_done"], 2 * b + j - 1)
                for k in range(KG):
                    mm(bank(2 + j, D), gT[:, k, j * P:j * P + P], wtok[:, k, :], start=(k == 0), stop=False)
                for k in range(KG):
                    mm(bank(2 + j, D), gT[:, k, j * P + 1:j * P + 1 + P], wtok[:, KG + k, :], start=False, stop=(k == KG - 1))
                if j == 0:
                    pe.wait_ge(s["gst_done"], b + 1)
                last = mm(banks[:, 2 + j, D:D + 2], shift[:], gst[:, j, :], start=True, stop=(j == 1))
                if j == 0:
                    last = mm(banks[:, 2 + j, D:D + 2], corner[:], gst[:, 1, :], start=False, stop=True)
                last.then_inc(s["tok_done"], 1)

            def transpose_xn(b):
                if not (isinstance(b, int) and b == 0):
                    pe.wait_ge(s["xlo_done"], b)
                for j in range(2):
                    pe.wait_ge(s["xn_ready"], 2 * b + j + 1)
                    for c in range(DC):
                        last = tr(bank(1)[:, c * D + j * P:c * D + j * P + P], xn[:, j, c * P:c * P + P], ident[:])
                last.then_inc(s["xnt_ready"], 1)

            def three(dst, pairs):
                n = 3 * len(pairs)
                i = 0
                for lh, ll, rh, rl in pairs:
                    for a, c in ((lh, rh), (lh, rl), (ll, rh)):
                        last = mm(dst, a, c, start=(i == 0), stop=(i == n - 1))
                        i += 1
                return last

            def project(b, j, first=False):
                if j == 0:
                    pe.wait_ge(s["xlo_done"], b + 1)
                for m in ((1, 2, 0), (2, 0, 1))[j]:
                    rdy, free = (("q_ready", "q_copied"), ("k_ready", "qk_done"), ("al_ready", "al_copied"))[m]
                    if m == 0 and j == 0 and not first:
                        pe.wait_ge(s["vo_copied"], b)
                    if not (first and j == 0):
                        pe.wait_ge(s[free], 2 * b + j)
                    three(bank(4 + m), [(xnT_h[:, c, j * P:j * P + P], xnT_l[:, c, j * P:j * P + P],
                                         wqka_h[:, c, m * HD:m * HD + HD], wqka_l[:, c, m * HD:m * HD + HD])
                                        for c in range(DC)]).then_inc(s[rdy], 1)

            def project_v(b, first=False):
                if not first:
                    pe.wait_ge(s["u_done"], b)
                for o in range(DC):
                    last = three(bank(7)[:, o * D:o * D + D],
                                 [(wv_h[:, c, o * P:o * P + P], wv_l[:, c, o * P:o * P + P], xnT_h[:, c, :], xnT_l[:, c, :])
                                  for c in range(DC)])
                last.then_inc(s["vt_ready"], 1)

            def project_out(b):
                pe.wait_ge(s["vl_done"], b + 1)
                pe.wait_ge(s["q_copied"], 2 * b + 2)
                for j in range(2):
                    last = three(bank(4)[:, j * D:j * D + D],
                                 [(vT_h[:, c, j * P:j * P + P], vT_l[:, c, j * P:j * P + P], wo_h[:, c, :], wo_l[:, c, :])
                                  for c in range(DC)])
                last.then_inc(s["vo_ready"], 1)

            def step(b, first=False, ahead=2):
                if ahead >= 1:
                    tokenise(b + 1, 0)
                    tokenise(b + 1, 1)
                if not first:
                    project_out(b - 1)
                project(b, 0, first)
                if ahead >= 2:
                    transpose_x(b + 2, 0)
                project(b, 1, first)
                if ahead >= 2:
                    transpose_x(b + 2, 1)
                project_v(b, first)
                if ahead >= 1:
                    transpose_xn(b + 1)

            transpose_x(0, 0)
            transpose_x(0, 1)
            tokenise(0, 0)
            tokenise(0, 1)
            transpose_x(1, 0)
            transpose_x(1, 1)
            transpose_xn(0)
            step(0, first=True)
            with pe.Fori(1, B - 2) as b:
                step(b)
            step(B - 2, ahead=1)
            step(B - 1, ahead=0)
            project_out(B - 1)

            pe.wait_ge(s["sp_done"], TILES)
            pe.wait_ge(s["xt_evac"], TILES)
            pe.wait_ge(s["xlo_done"], B)
            for k, src in enumerate((bsum, asum)):
                for j in range(2):
                    last = tr(banks[:, k, j * P:j * P + P], src[:, j, :], ident[:])
            last.then_inc(s["ba_ready"], 1)

            def spread_chunk(p, k):
                t = 4 * p + k
                if not (isinstance(p, int) and t < 2):
                    pe.wait_ge(s["lb_used"], apart(pe, t - 1))
                mm(banks[:, k % 2, 0:HEADS * SPAN], sel_chunk[:, k % 2, :],
                   lamB[:, 2 * p + k // 2].rearrange("p h s -> p (h s)"), start=True, stop=True).then_inc(s["lb_ready"], 1)

            def spread_heads(p):
                if not (isinstance(p, int) and p == 0):
                    pe.wait_ge(s["q_done"], apart(pe, p))
                mm(bank(5, 2 * P), sel_head[:], lamQ[:, p, :], start=True, stop=True).then_inc(s["qb_ready"], 1)

            def chunk_ends(p):
                pe.wait_ge(s["es_ready"], 4 * p + 4)
                if not (isinstance(p, int) and p == 0):
                    pe.wait_ge(s["l_copied"], p)
                for k in range(4):
                    last = mm(bank(4, D), ends[:, k, :], vo[:, 4 * p + k, :], start=(k == 0), stop=(k == 3))
                last.then_inc(s["l_ready"], 1)

            def mix(p, k):
                t = 4 * p + k
                b2_, j = k // 2, k % 2
                if not (isinstance(p, int) and t < 2):
                    pe.wait_ge(s["h2_done"], t - 1)
                if k == 0:
                    pe.wait_ge(s["q_done"], p + 1)
                    pe.wait_ge(s["l_copied"], p + 1)
                mm(bank(2 + k % 2, D), wbd[:, k, :], vo[:, t, :], start=True, stop=False)
                mm(bank(2 + k % 2, D), qst[64 * b2_:64 * b2_ + 64, j * P:j * P + P], lst[64 * b2_:64 * b2_ + 64, :],
                   start=False, stop=True).then_inc(s["out_ready"], 1)

            def transpose_xn2(t, w):
                pe.wait_ge(s["xn2_ready"], t + 1)
                if not (isinstance(t, int) and t == 0):
                    pe.wait_ge(s["t2_evac"], t)
                for c in range(DC):
                    last = tr(bank(6)[:, c * P:c * P + P], xn2[:, w, c * P:c * P + P], ident[:])
                last.then_inc(s["t2_ready"], 1)

            def logits(t, w):
                pe.wait_ge(s["t2_evac"], t + 1)
                for c in range(DC):
                    last = mm(banks[:, 7, bass.ds(t * E, E)], xT2[:, w, c * P:c * P + P], wrg[:, c, :],
                              start=(c == 0), stop=(c == DC - 1))
                last.then_inc(s["lg_done"], 1)

            def pair(p, ahead=True):
                chunk_ends(p)
                for k in range(4):
                    if ahead:
                        spread_chunk(p + 1, k)
                    mix(p, k)
                    t = 4 * p + k
                    if not (isinstance(p, int) and t < 2):
                        logits(t - 2, k % 2)
                    if not (isinstance(p, int) and t < 1):
                        transpose_xn2(t - 1, (k + 1) % 2)
                if ahead:
                    spread_heads(p + 1)

            pe.wait_ge(s["consts2"], 1)
            pe.wait_ge(s["lam_b"], 16 * NCH)
            pe.wait_ge(s["lam_q"], 16 * 8)
            pe.wait_ge(s["gate_steps"], 2)
            pe.wait_ge(s["vo_copied"], B)
            pe.wait_ge(s["qk_done"], TILES)
            pe.wait_ge(s["al_copied"], TILES)
            pe.wait_ge(s["u_done"], B)
            spread_heads(0)
            for k in range(4):
                spread_chunk(0, k)
            pair(0)
            with pe.Fori(1, 7) as p:
                pair(p)
            pair(7, ahead=False)
            logits(TILES - 2, 0)
            transpose_xn2(TILES - 1, 1)
            logits(TILES - 1, 1)

            pe.wait_ge(s["oh_ready"], 1)
            ohf = oh.rearrange("p t e -> p (t e)")
            mm(bank(0, 256), before[:], ohf, start=True, stop=True)
            mm(bank(1, 256), ones[:], ohf, start=True, stop=True).then_inc(s["counts"], 1)

            def transpose_rows(i):
                pe.wait_ge(s["xd_ready"], i + 1)
                if not (isinstance(i, int) and i == 0):
                    pe.wait_ge(s["xdl_done"], i)
                for c in range(DC):
                    last = tr(bank(2)[:, c * P:c * P + P], xnD[:, c * P:c * P + P], ident[:])
                last.then_inc(s["xdt_ready"], 1)

            def up(i):
                e = pe.value_load(sloti[0:1, bass.ds(i, 1)], min_val=0, max_val=E - 1)
                pe.wait_ge(s["xdl_done"], i + 1)
                for f in range(FC):
                    if f % 2 == 0 and not (isinstance(i, int) and i == 0):
                        pe.wait_ge(s["gelu_done"], FC * i - 2 + f)
                    n = 0
                    for c in range(DC):
                        for a, r_ in ((w1h, xh), (w1l, xh), (w1h, xl)):
                            last = mm(banks[:, f // 2, (f % 2) * P:(f % 2) * P + P],
                                      a[:, bass.ds(e * DC + c, 1), f * P:f * P + P].rearrange("p a b -> p (a b)"),
                                      r_[:, c, :], start=(n == 0), stop=(n == 5))
                            n += 1
                    if f % 2:
                        last.then_inc(s["m1_ready"], 1)
                return e

            def down(i):
                e = pe.value_load(sloti[0:1, bass.ds(i, 1)], min_val=0, max_val=E - 1)
                pe.wait_ge(s["g_done"], i + 1)
                if not (isinstance(i, int) and i == 0):
                    pe.wait_ge(s["yt_done"], i)
                n = 0
                for f in range(FC):
                    for a, r_ in ((gh, w2h), (gh, w2l), (gl, w2h)):
                        last = mm(bank(3, D), a[:, f, :], r_[:, bass.ds(e * FC + f, 1), :].rearrange("p a b -> p (a b)"),
                                  start=(n == 0), stop=(n == 3 * FC - 1))
                        n += 1
                last.then_inc(s["m2_ready"], 1)

            pe.wait_ge(s["route_ready"], 1)
            transpose_rows(0)
            up(0)
            transpose_rows(1)
            up(1)
            transpose_rows(2)
            down(0)
            with pe.Fori(1, SLOTS - 2) as i:
                up(i + 1)
                transpose_rows(i + 2)
                down(i)
            up(SLOTS - 1)
            down(SLOTS - 2)
            down(SLOTS - 1)

        @block.scalar
        def _(act):
            af = nc.scalar.activation
            act.wait_ge(s["consts"], 1)
            for m in range(3):
                for c in range(DC):
                    act.wait_ge(s["wload"], 2 * m + c + 1)
                    af(wqka_h[:, c, m * HD:m * HD + HD], bank(2 * m + c), ACT.Copy, scale=WS).then_inc(s["wsplit_hi"], 1)
            for m, dst in enumerate((wv_h, wo_h)):
                act.wait_ge(s["wload"], 7 + m)
                af(dst[:].rearrange("p c o -> p (c o)"), bank(6 + m), ACT.Copy, scale=WS).then_inc(s["wsplit_hi"], 1)

            act.preload_act_table_set("natural_log_exp_and_others")
            steps = Steps(act, s["act_steps"], 2)

            def keep_xT(b, j):
                act.wait_ge(s["xt_ready"], 2 * b + j + 1)
                if not (isinstance(b, int) and b == 0):
                    act.wait_ge(s["tok_done"], 2 * b)
                af(gT[:, :, j * P:j * P + P], bank(0).rearrange("p (k g) -> p k g", k=KG), ACT.Copy).then_inc(s["xt_evac"], 1)

            def split_xn(b):
                act.wait_ge(s["xnt_ready"], b + 1)
                if not (isinstance(b, int) and b == 0):
                    act.wait_ge(s["vt_ready"], b)
                af(xnT_h[:].rearrange("p c t -> p (c t)"), bank(1), ACT.Copy).then_inc(s["xhi_done"], 1)

            def copy_q(b, j, first=False):
                act.wait_ge(s["q_ready"], 2 * b + j + 1)
                if not (first and j == 0):
                    act.wait_ge(s["qk_done"], 2 * b + j)
                af(q_sb, bank(4), ACT.Copy).then_inc(s["q_copied"], 1)

            def log_part(b, j, first=False):
                t = 2 * b + j
                steps.begin(t)
                act.wait_ge(s["al_copied"], t + 1)
                if not (first and j == 0):
                    act.wait_ge(s["sp_done"], t)
                steps.step(af(sp, al, ACT.Abs))
                steps.settle()
                steps.step(af(sp, sp, ACT.Exp, scale=-1.0))
                steps.settle()
                steps.end()
                af(sp, sp, ACT.Ln, bias=one_col[:]).then_inc(s["ln_done"], 1)

            def split_v(b):
                act.wait_ge(s["u_done"], b + 1)
                if not (isinstance(b, int) and b == 0):
                    act.wait_ge(s["vo_ready"], b)
                af(vT_h[:].rearrange("p c t -> p (c t)"), u[:].rearrange("p c t -> p (c t)"), ACT.Identity,
                   bias=minus_veps[:]).then_inc(s["vh_done"], 1)

            def keep_vo(b):
                act.wait_ge(s["vo_ready"], b + 1)
                if isinstance(b, int) and b == 0:
                    act.wait_ge(s["wsplit_lo"], 8)
                af(vo[:, bass.ds(2 * b, 2), :].rearrange("p t d -> p (t d)"), bank(4), ACT.Copy,
                   scale=1.0 / WS).then_inc(s["vo_copied"], 1)

            def split_expert(n):
                act.wait_ge(s["w_in"], 32 * n + 32)
                af(w1h[:, n, :], stage1[:], ACT.Copy).then_inc(s["w_hi"], 1)
                af(w2h[:, bass.ds(2 * n, 2), :].rearrange("p q d -> p (q d)"), stage2[:], ACT.Copy).then_inc(s["w_hi"], 1)

            def step(b, first=False, ahead=2):
                if not first:
                    split_v(b - 1)
                    keep_vo(b - 1)
                copy_q(b, 0, first)
                log_part(b, 0, first)
                if ahead >= 2:
                    keep_xT(b + 2, 0)
                copy_q(b, 1)
                if ahead >= 2:
                    keep_xT(b + 2, 1)
                log_part(b, 1)
                split_expert(b)
                if ahead >= 1:
                    split_xn(b + 1)

            for j in range(2):
                keep_xT(0, j)
            for j in range(2):
                keep_xT(1, j)
            split_xn(0)
            step(0, first=True)
            with act.Fori(1, B - 2) as b:
                step(b)
            step(B - 2, ahead=1)
            step(B - 1, ahead=0)
            split_v(B - 1)
            keep_vo(B - 1)

            act.wait_ge(s["gate_args"], 1)
            af(late["ea"], late["ea"], ACT.Exp).then_inc(s["gate_exp"], 1)
            act.wait_ge(s["gate_args"], 2)
            af(late["eb"], late["eb"], ACT.Exp).then_inc(s["gate_exp"], 1)
            act.wait_ge(s["lam_done"], 1)
            for r in range(8):
                act.dma_start(lamQ[:, r, :], late["lam"][16 * r:16 * r + 16, :]).then_inc(s["lam_q"], 16)

            def keep_ends(p):
                act.wait_ge(s["l_ready"], p + 1)
                af(lst[:], bank(4, D), ACT.Copy).then_inc(s["l_copied"], 1)

            def keep_xT2(t, w):
                act.wait_ge(s["t2_ready"], t + 1)
                if not (isinstance(t, int) and t < 2):
                    act.wait_ge(s["lg_done"], t - 1)
                af(xT2[:, w, :], bank(6, D), ACT.Copy).then_inc(s["t2_evac"], 1)

            keep_ends(0)
            for k in range(1, 4):
                keep_xT2(k - 1, (k + 1) % 2)
            with act.Fori(1, 8) as p:
                keep_ends(p)
                for k in range(4):
                    keep_xT2(4 * p + k - 1, (k + 1) % 2)
            keep_xT2(TILES - 1, 1)

            act.wait_ge(s["r_args"], 1)
            af(t8.rearrange("p t e -> p (t e)"), t8.rearrange("p t e -> p (t e)"), ACT.Exp).then_inc(s["r_exp"], 1)
            act.wait_ge(s["route_ready"], 1)

            def split_rows(i):
                act.wait_ge(s["xdt_ready"], i + 1)
                if not (isinstance(i, int) and i == 0):
                    act.wait_ge(s["m1_ready"], 2 * i)
                af(xh.rearrange("p c t -> p (c t)"), bank(2, D), ACT.Copy).then_inc(s["xdh_done"], 1)

            split_rows(0)

            def slot(i, last=False):
                e = act.value_load(sloti[0:1, bass.ds(i, 1)], min_val=0, max_val=E - 1)
                if not (isinstance(i, int) and i == 0):
                    act.wait_ge(s["g_done"], i)
                for f in range(FC):
                    if f == FC - 1 and not last:
                        split_rows(i + 1)
                    if f % 2 == 0:
                        act.wait_ge(s["m1_ready"], 2 * i + 1 + f // 2)
                    af(gel[:, f, :], banks[:, f // 2, (f % 2) * P:(f % 2) * P + P], ACT.Gelu,
                       bias=b1t[:, bass.ds(e, 1), f:f + 1].rearrange("p a b -> p (a b)")).then_inc(s["gelu_done"], 1)

            slot(0)
            with act.Fori(1, SLOTS - 1) as i:
                slot(i)
            slot(SLOTS - 1, last=True)

        @block.vector
        def _(dve):
            tt, ts, stt = nc.vector.tensor_tensor, nc.vector.tensor_scalar, nc.vector.scalar_tensor_tensor
            copy, reduce, scan = nc.vector.tensor_copy, nc.vector.tensor_reduce, nc.vector.tensor_tensor_scan

            def wide(ap, shape):
                return ap.unsqueeze(2).to_broadcast(shape)

            def repeated(ap, shape):
                return ap.unsqueeze(1).to_broadcast(shape)

            def weights_lo(n, dst):
                dve.wait_ge(s["wsplit_hi"], n + 1)
                hi, lo = dst
                stt(lo, bank(n), WS, hi, ALU.mult, ALU.subtract).then_inc(s["wsplit_lo"], 1)

            dve.wait_ge(s["consts"], 1)
            dve.wait_ge(s["tok_w_in"], 96)
            prep = Steps(dve, s["router_steps"], 8)
            prep.begin(0)
            for t2 in range(2):
                half = slice(DIN * t2, DIN * t2 + DIN)
                prep.step(copy(gam[half, :], gam_raw[half, t2::2]))
                prep.step(copy(bet[half, :], bet_raw[half, t2::2]))
            prep.settle()
            copy(beta_wide, wide(bet[:], [P, KC, P])).then_inc(s["beta_wide_ready"], 1)
            dve.wait_ge(s["misc_in"], 16 * 5)
            prep.step(tt(wg_sq[:], wg_sb[:], wg_sb[:], ALU.mult))
            prep.settle()
            reduce(wg_norm[:, 0:1], wg_sq[:], AX, ALU.add).then_inc(s["router_norm"], 1)
            for n in range(8):
                m, c = n // 2, n % 2
                if n < 6:
                    weights_lo(n, (wqka_h[:, c, m * HD:m * HD + HD], wqka_l[:, c, m * HD:m * HD + HD]))
                else:
                    hi, lo = ((wv_h, wv_l), (wo_h, wo_l))[n - 6]
                    weights_lo(n, (hi[:].rearrange("p c o -> p (c o)"), lo[:].rearrange("p c o -> p (c o)")))
            dve.wait_ge(s["router_root"], 1)
            prep.step(ts(wg_norm[:, 1:2], wg_norm[:, 1:2], 1e-4, None, ALU.max))
            prep.settle()
            prep.step(nc.vector.reciprocal(wg_norm[:, 0:1], wg_norm[:, 1:2]))
            prep.settle()
            ts(wg_sb[:], wg_sb[:], wg_norm[:, 0:1], None, ALU.mult).then_inc(s["router_prep"], 1)
            dve.wait_ge(s["bias_ready"], 1)
            tt(wtok, wtok, wide(gam[:], [P, KC, D]), ALU.mult).then_inc(s["gamma_done"], 1)
            dve.wait_ge(s["router_t"], 1)
            copy(router_T[:], banks[0:16, 2, 0:D + E]).then_inc(s["router_weights"], 1)
            tt(tok_bias[:], bank(0, D), tok_b_wide[:], ALU.add).then_inc(s["const_steps"], 1)
            nc.vector.memset(gT[:, :, 2 * P:2 * P + 1], 0.0).then_inc(s["const_steps"], 1)
            dve.wait_ge(s["router_mm"], 1)
            copy(b1t[:].rearrange("p e f -> p (e f)"), banks[:, 3, 64:64 + E * FC]).then_inc(s["const_steps"], 1)
            copy(wrg[:].rearrange("p c e -> p (c e)"), banks[:, 3, 0:DC * E]).then_inc(s["router_done"], 1)
            dve.wait_ge(s["colsum_ready"], 1)
            copy(colsum[:], bank(1, D)).then_inc(s["tokprep"], 1)
            prep.step(nc.vector.memset(ends[:], 0.0))
            prep.end()

            gsteps = Steps(dve, s["gst_steps"], 3)
            lsteps = Steps(dve, s["ln_steps"], 7)
            ssteps = Steps(dve, s["sp_steps"], 1)
            usteps = Steps(dve, s["u_steps"], 1)

            def group_stats(b):
                gsteps.begin(b)
                dve.wait_ge(s["x_in"], 16 * (b + 1))
                if not (isinstance(b, int) and b == 0):
                    dve.wait_ge(s["tok_done"], 2 * b)
                for j in range(2):
                    gsteps.step(nc.vector.bn_stats(gst6[:, j, :], xg[:, j, :]))
                gsteps.settle(apart)
                gsteps.step(nc.vector.bn_aggr(gst[:, 0, :], gst6[:, 0, :]))
                nc.vector.bn_aggr(gst[:, 1, :], gst6[:, 1, :]).then_inc(s["gst_done"], 1)
                gsteps.end()

            def normalise(b, j):
                t = 2 * b + j
                lsteps.begin(t)
                dve.wait_ge(s["tok_done"], t + 1)
                nxt = banks[:, 2 + j, D:D + 2]
                lsteps.step(tt(sm[:, 0:2], gst[:, j, :], nxt, ALU.add))
                lsteps.settle()
                lsteps.step(stt(sm[:, 3:4], sm[:, 0:1], -0.5, gst[:, j, 0:1], ALU.mult, ALU.add))
                lsteps.step(ts(sm[:, 2:3], sm[:, 1:2], 0.5, LN_EPS, ALU.mult, ALU.add))
                lsteps.settle()
                stt(sm[:, 4:5], sm[:, 3:4], sm[:, 3:4], sm[:, 2:3], ALU.mult, ALU.add).then_inc(s["var_ready"], 1)
                dve.wait_ge(s["rstd_ready"], 2 * t + 1)
                lsteps.step(stt(sm[:, 6:7], sm[:, 0:1], -0.5, sm[:, 5:6], ALU.mult, ALU.mult))
                lsteps.settle()
                lsteps.step(stt(tokc[:], colsum[:], sm[:, 6:7], tok_bias[:], ALU.mult, ALU.add))
                lsteps.settle()
                h = rows[:, bass.ds(t, 1), 0:D].rearrange("p a b -> p (a b)")
                stt(h, bank(2 + j, D), sm[:, 5:6], tokc[:], ALU.mult, ALU.add).then_inc(s["h_done"], 1)
                dve.wait_ge(s["h_done"], apart(dve, t + 1))
                lsteps.step(nc.vector.bn_stats(lst6[:], h))
                lsteps.settle(apart)
                lsteps.step(nc.vector.bn_aggr(sm[:, 9:11], lst6[:]))
                lsteps.settle()
                lsteps.end()
                ts(sm[:, 7:8], sm[:, 10:11], LN_EPS, None, ALU.add).then_inc(s["var_ready"], 1)
                dve.wait_ge(s["rstd_ready"], 2 * t + 2)
                if not (isinstance(b, int) and b == 0):
                    dve.wait_ge(s["xnt_ready"], b)
                ts(xn[:, j, :], h, sm[:, 9:10], sm[:, 8:9], ALU.subtract, ALU.mult).then_inc(s["xn_ready"], 1)

            def split_xn(b):
                dve.wait_ge(s["xhi_done"], b + 1)
                if not (isinstance(b, int) and b == 0):
                    dve.wait_ge(s["vt_ready"], b)
                tt(xnT_l[:].rearrange("p c t -> p (c t)"), bank(1), xnT_h[:].rearrange("p c t -> p (c t)"),
                   ALU.subtract).then_inc(s["xlo_done"], 1)

            def gate_b(b, j):
                t = 2 * b + j
                dve.wait_ge(s["k_ready"], t + 1)
                dve.wait_ge(s["q_copied"], t + 1)
                stt(qk, bank(5), DH ** -0.5 / (WS * WS), q_sb, ALU.mult, ALU.mult).then_inc(s["qk_done"], 1)
                dve.wait_ge(s["qk_done"], t + 1)
                reduce(bsum[:, j, bass.ds(b * HEADS, HEADS)], qk.rearrange("p (h d) -> p h d", h=HEADS), AX, ALU.add)

            def alpha(b, j, first=False):
                t = 2 * b + j
                dve.wait_ge(s["al_ready"], t + 1)
                if not (first and j == 0):
                    dve.wait_ge(s["sp_done"], t)
                stt(al, bank(6), 1.0 / WS, alpha_bias[:], ALU.mult, ALU.add).then_inc(s["al_copied"], 1)

            def gate_a(b, j):
                t = 2 * b + j
                ssteps.begin(t)
                dve.wait_ge(s["ln_done"], t + 1)
                dve.wait_ge(s["al_copied"], t + 1)
                ssteps.step(stt(al, al, 0.0, sp, ALU.max, ALU.add))
                ssteps.settle()
                ssteps.end()
                reduce(asum[:, j, bass.ds(b * HEADS, HEADS)], al.rearrange("p (h d) -> p h d", h=HEADS), AX,
                       ALU.add).then_inc(s["sp_done"], 1)

            flat_u = u[:].rearrange("p c t -> p (c t)")

            def guard_v(b):
                usteps.begin(b)
                dve.wait_ge(s["vt_ready"], b + 1)
                if not (isinstance(b, int) and b == 0):
                    dve.wait_ge(s["vh_done"], b)
                usteps.step(ts(flat_u, bank(7), 0.0, 2 * V_EPS, ALU.is_ge, ALU.mult))
                usteps.settle()
                usteps.end()
                stt(flat_u, bank(7), 1.0 / WS, flat_u, ALU.mult, ALU.add).then_inc(s["u_done"], 1)

            def split_v(b):
                dve.wait_ge(s["vh_done"], b + 1)
                dve.wait_ge(s["u_done"], b + 1)
                if not (isinstance(b, int) and b == 0):
                    dve.wait_ge(s["vo_ready"], b)
                stt(vT_l[:].rearrange("p c t -> p (c t)"), flat_u, V_EPS, vT_h[:].rearrange("p c t -> p (c t)"),
                    ALU.subtract, ALU.subtract).then_inc(s["vl_done"], 1)

            def step(b, first=False, ahead=2):
                if not first:
                    split_v(b - 1)
                if ahead >= 1:
                    normalise(b + 1, 0)
                    normalise(b + 1, 1)
                alpha(b, 0, first)
                if ahead >= 2:
                    group_stats(b + 2)
                gate_b(b, 0)
                gate_a(b, 0)
                alpha(b, 1)
                gate_b(b, 1)
                guard_v(b)
                gate_a(b, 1)
                if ahead >= 1:
                    split_xn(b + 1)

            group_stats(0)
            normalise(0, 0)
            normalise(0, 1)
            group_stats(1)
            split_xn(0)
            step(0, first=True)
            with dve.Fori(1, B - 2) as b:
                step(b)
            step(B - 2, ahead=1)
            step(B - 1, ahead=0)
            split_v(B - 1)

            T = 2 * P
            gate = Steps(dve, s["gate_steps"], 9)
            gate.begin(0)
            dve.wait_ge(s["ba_ready"], 1)
            dve.wait_ge(s["tok_done"], TILES)
            dve.wait_ge(s["al_ready"], TILES)
            gate.step(copy(late["bT"], bank(0, T)))
            gate.step(ts(late["aT"], bank(1, T), -1.0, None, ALU.mult))
            gate.step(nc.vector.memset(late["m"][:, 0:1], NEG))
            gate.step(nc.vector.memset(late["r"][:, 0:1], 0.0))
            nc.vector.memset(lamB[:, :, :, 0:1], 0.0).then_inc(s["lb_zero"], 1)
            gate.settle()
            gate.step(scan(late["m"][:, 1:T + 1], late["aT"], late["bT"], NEG, ALU.add, ALU.max))
            gate.settle()
            gate.step(tt(late["ea"], late["aT"], late["m"][:, 0:T], ALU.add))
            gate.settle()
            tt(late["ea"], late["ea"], late["m"][:, 1:T + 1], ALU.subtract).then_inc(s["gate_args"], 1)
            tt(late["eb"], late["bT"], late["m"][:, 1:T + 1], ALU.subtract).then_inc(s["gate_args"], 1)
            dve.wait_ge(s["gate_exp"], 2)
            gate.step(scan(late["r"][:, 1:T + 1], late["ea"], late["eb"], 0.0, ALU.mult, ALU.add))
            gate.settle()
            gate.step(nc.vector.reciprocal(late["bT"], late["r"][:, 1:T + 1]))
            gate.step(tt(late["ea"], late["ea"], late["r"][:, 0:T], ALU.mult))
            gate.settle()
            gate.end()
            tt(late["lam"], late["ea"], late["bT"], ALU.mult).then_inc(s["lam_done"], 1)

            esteps = Steps(dve, s["es_steps"], 2)
            hsteps = Steps(dve, s["h2_steps"], 3)

            class Chunk:

                def __init__(self, p, k):
                    self.p, self.k, self.t = p, k, 4 * p + k
                    self.first = isinstance(p, int) and p == 0

                def scan(self):
                    esteps.begin(self.t)
                    dve.wait_ge(s["lb_ready"], self.t + 1)
                    scan(resp[:, 0:HEADS, :].rearrange("p h s -> p (h s)"), decay_in[:].rearrange("p h s -> p (h s)"),
                         banks[:, self.k % 2, 0:HEADS * SPAN], 0.0, ALU.add, ALU.mult).then_inc(s["lb_used"], 1)

                def sum_heads(self):
                    dve.wait_ge(s["lb_used"], self.t + 1)
                    esteps.step(reduce(wsum[:], resp[:, :, 1:SPAN].rearrange("p h s -> p s h"), AX, ALU.add))

                def keep_ends(self):
                    k = self.k
                    if not self.first:
                        dve.wait_ge(s["l_ready"], self.p)
                    col = 64 * (k // 2) + CH * (k % 2)
                    end = resp[:, 0:HEADS, CH:SPAN].rearrange("p h s -> p (h s)")
                    esteps.step(stt(ends[:, k, col:col + CH].rearrange("p (c h) -> p c h", c=CT),
                                    repeated(end, [P, CT, HEADS]), last_row[:], mask4[:], ALU.add, ALU.mult))

                def spread(self):
                    esteps.settle()
                    esteps.end()
                    if not self.first:
                        dve.wait_ge(s["out_ready"], self.t - 3)
                    tt(wbd[:, self.k, :].rearrange("p (c s) -> p c s", c=CT), repeated(wsum[:], [P, CT, CH]),
                       chunk_mask[:], ALU.mult).then_inc(s["es_ready"], 1)

            def head_decays(p):
                dve.wait_ge(s["qb_ready"], p + 1)
                if not (isinstance(p, int) and p == 0):
                    dve.wait_ge(s["out_ready"], 4 * p)
                scan(qst[:], head_state_in[:], bank(5, T), 0.0, ALU.add, ALU.mult).then_inc(s["q_done"], 1)

            def slot(p, k, ahead):
                t = 4 * p + k
                chunk = Chunk(p + 1, k)
                hsteps.begin(t)
                row = rows[:, bass.ds(t, 1), :].rearrange("p a b -> p (a b)")
                stats = sm[:, 2 * (k % 2):2 * (k % 2) + 2]
                mean, rstd = stats[:, 0:1], stats[:, 1:2]
                if ahead:
                    chunk.scan()
                dve.wait_ge(s["out_ready"], t + 1)
                tt(row[:, 0:D], bank(2 + k % 2, D), row[:, 0:D], ALU.add).then_inc(s["h2_done"], 1)
                if ahead:
                    chunk.sum_heads()
                dve.wait_ge(s["h2_done"], apart(dve, t + 1))
                hsteps.step(nc.vector.bn_stats(lst6[:], row[:, 0:D]))
                if ahead:
                    chunk.keep_ends()
                hsteps.settle(apart)
                hsteps.step(nc.vector.bn_aggr(stats, lst6[:]))
                if ahead:
                    chunk.spread()
                hsteps.settle()
                hsteps.step(ts(rstd, rstd, LN_EPS, None, ALU.add))
                hsteps.end()

            def normalise2(t, k):
                row = rows[:, bass.ds(t, 1), :].rearrange("p a b -> p (a b)")
                stats = sm[:, 2 * (k % 2):2 * (k % 2) + 2]
                dve.wait_ge(s["rstd2_ready"], t + 1)
                if not (isinstance(t, int) and t < 2):
                    dve.wait_ge(s["t2_ready"], t - 1)
                ts(xn2[:, k % 2, :], row[:, 0:D], stats[:, 0:1], stats[:, 1:2], ALU.subtract,
                   ALU.mult).then_inc(s["xn2_ready"], 1)
                copy(row[:, D + 1:D + 3], stats)

            def pair(p, ahead=True):
                for k in range(4):
                    slot(p, k, ahead)
                    normalise2(4 * p + k, k)
                if ahead:
                    head_decays(p + 1)

            dve.wait_ge(s["router_steps"], 8)
            dve.wait_ge(s["consts2"], 1)
            head_decays(0)
            for k in range(4):
                chunk = Chunk(0, k)
                chunk.scan()
                chunk.sum_heads()
                chunk.keep_ends()
                chunk.spread()
            pair(0)
            with dve.Fori(1, 7) as p:
                pair(p)
            pair(7, ahead=False)

            T8 = [P, TILES, E]
            r = Steps(dve, s["r_steps"], 32)
            r.begin(0)
            dve.wait_ge(s["lg_done"], TILES)
            r.step(copy(lg.rearrange("p t e -> p (t e)"), bank(7, TILES * E)))
            r.step(nc.vector.memset(zer, 0.0))
            r.settle()
            r.step(reduce(mx, lg, AX, ALU.max))
            r.settle()
            tt(t8, lg, wide(mx, T8), ALU.subtract).then_inc(s["r_args"], 1)
            r.step(tt(oh, lg, wide(mx, T8), ALU.is_ge))
            r.settle()
            r.step(tt(oh, oh, repeated(rank_w[:], T8), ALU.mult))
            r.settle()
            r.step(reduce(mw, oh, AX, ALU.max))
            r.settle()
            r.step(tt(oh, repeated(rank_w[:], T8), wide(mw, T8), ALU.is_equal))
            r.settle()
            tt(oh, oh, wide(valid[:], T8), ALU.mult).then_inc(s["oh_ready"], 1)
            dve.wait_ge(s["r_exp"], 1)
            r.step(reduce(sumexp, t8, AX, ALU.add))
            r.settle()
            r.step(nc.vector.reciprocal(rows[:, :, D:D + 1].rearrange("p t c -> p (t c)"), sumexp))
            dve.wait_ge(s["counts"], 1)
            r.step(copy(tot.rearrange("p t e -> p (t e)"), bank(1, TILES * E)))
            r.settle()
            for e in range(E):
                r.step(scan(cum[:, :, e], tot[:, :, e], zer[:, 0:TILES], 0.0, ALU.add, ALU.add))
            r.settle()
            r.step(tt(t8, cum, tot, ALU.subtract))
            over_thr = lg.rearrange("p t e -> p (t e)").rearrange("p (e t) -> p e t", e=E)
            r.step(tt(over_thr, wide(cum[:, TILES - 1, :], [P, E, 32]), repeated(thr[:], [P, E, 32]), ALU.is_gt))
            r.settle()
            r.step(reduce(ntile, over_thr, AX, ALU.add))
            r.settle()
            r.step(scan(tend, ntile, zer[:, 0:E], 0.0, ALU.add, ALU.add))
            r.settle()
            r.step(tt(tstart, tend, ntile, ALU.subtract))
            r.settle()
            r.step(ts(tstart, tstart, float(P), None, ALU.mult))
            flat8 = t8.rearrange("p t e -> p (t e)")
            r.step(tt(flat8, bank(0, TILES * E), flat8, ALU.add))
            r.settle()
            r.step(tt(t8, t8, repeated(tstart, T8), ALU.add))
            r.settle()
            r.step(tt(t8, t8, oh, ALU.mult))
            r.settle()
            r.step(reduce(posf, t8, AX, ALU.add))
            r.settle()
            r.step(tt(posf, posf, pad_pos[:], ALU.add))
            r.settle()
            r.step(copy(posi, posf))
            S7 = [P, SLOTS, E - 1]
            r.step(tt(cmp8[:, :, 0:E - 1], wide(slot_no[:], S7), repeated(tend[:, 0:E - 1], S7), ALU.is_ge))
            r.settle()
            r.step(reduce(slotf, cmp8[:, :, 0:E - 1], AX, ALU.add))
            r.settle()
            r.end()
            copy(sloti, slotf).then_inc(s["route_ready"], 1)
            dve.wait_ge(s["route_ready"], 1)
            dve.wait_ge(s["b2_in"], 16)

            gsplit = Steps(dve, s["g_steps"], 1)
            ysteps = Steps(dve, s["y_steps"], 1)

            def norm_rows(i, w, g):
                dve.wait_ge(s[f"row_in_{w}"], 16 * g + 16)
                if not (isinstance(i, int) and i == 0):
                    dve.wait_ge(s["xdt_ready"], i)
                ts(xnD, xr[:, w, 0:D], xr[:, w, D + 1:D + 2], xr[:, w, D + 2:D + 3], ALU.subtract,
                   ALU.mult).then_inc(s["xd_ready"], 1)

            def split_rows(i):
                dve.wait_ge(s["xdh_done"], i + 1)
                if not (isinstance(i, int) and i == 0):
                    dve.wait_ge(s["m1_ready"], 2 * i)
                tt(xl.rearrange("p c t -> p (c t)"), bank(2, D), xh.rearrange("p c t -> p (c t)"),
                   ALU.subtract).then_inc(s["xdl_done"], 1)

            def split_gelu(i):
                gsplit.begin(i)
                dve.wait_ge(s["gelu_done"], FC * (i + 1))
                if not (isinstance(i, int) and i == 0):
                    dve.wait_ge(s["m2_ready"], i)
                gsplit.step(copy(gh.rearrange("p f t -> p (f t)"), gel.rearrange("p f t -> p (f t)")))
                gsplit.settle()
                gsplit.end()
                tt(gl.rearrange("p f t -> p (f t)"), gel.rearrange("p f t -> p (f t)"),
                   gh.rearrange("p f t -> p (f t)"), ALU.subtract).then_inc(s["g_done"], 1)

            def finish(i, w, g):
                e = dve.value_load(sloti[0:1, bass.ds(i, 1)], min_val=0, max_val=E - 1)
                ysteps.begin(i)
                dve.wait_ge(s["m2_ready"], i + 1)
                if not (isinstance(i, int) and i == 0):
                    dve.wait_ge(s["y_steps"], i)
                tt(yt, bank(3, D), b2w[:, bass.ds(e, 1), :].rearrange("p a b -> p (a b)"), ALU.add).then_inc(s["yt_done"], 1)
                dve.wait_ge(s["yt_done"], i + 1)
                if not (isinstance(i, int) and i < RING):
                    dve.wait_ge(s[f"y_out_{w}"], 16 * g)
                ysteps.step(stt(yo[:, w, :], yt, xr[:, w, D:D + 1], xr[:, w, 0:D], ALU.mult, ALU.add))
                ysteps.end()
                copy(oid[:, w:w + 1], xr[:, w, D + 3:D + 4].bitcast(I32)).then_inc(s["y_done"], 1)

            def slots(g, count=RING, first=False, last=False):
                for w in range(count):
                    i = RING * g + w
                    if not (last and w == count - 1):
                        split_rows(i + 1)
                    if not (last and w >= count - 2):
                        norm_rows(i + 2, (w + 2) % RING, g if w + 2 < RING else g + 1)
                    split_gelu(i)
                    if not (first and w == 0):
                        finish(i - 1, (w - 1) % RING, g - 1 if w == 0 else g)

            norm_rows(0, 0, 0)
            split_rows(0)
            norm_rows(1, 1, 0)
            slots(0, first=True)
            with dve.Fori(1, ROUNDS) as g:
                slots(g)
            slots(ROUNDS, REST, last=True)
            finish(SLOTS - 1, REST - 1, ROUNDS)

        @block.gpsimd
        def _(pool):
            g = nc.gpsimd
            ptt = g.tensor_tensor
            made = Steps(pool, s["const_steps_p"], 1000)
            made.begin(0)

            def clear(ap, value=0.0):
                made.step(g.memset(ap, value))

            def select(ap, pattern, base, cm, op, fill):
                made.settle()
                made.step(g.affine_select(out=ap, in_=ap, pattern=pattern, compare_op=op, fill=fill, base=base,
                                          channel_multiplier=cm))

            NE, GE = ALU.not_equal, ALU.is_ge
            for ap in (ident, shift, corner):
                clear(ap[:])
            select(ident[:], [[-1, P]], 0, 1, NE, 1.0)
            select(shift[:], [[-1, P]], -1, 1, NE, 1.0)
            for ap in (ones, one_col):
                clear(ap[:], 1.0)
            clear(minus_half[:], -0.5)
            clear(plus_half[:], 0.5)
            clear(minus_veps[:], -V_EPS)
            made.settle()
            g.memset(corner[0:1, P - 1:P], 1.0).then_inc(s["consts"], 1)

            for ap in (chunk_mask, mask4, last_row, decay_in, sel_chunk, sel_head, resp, init_rows, pad_pos,
                       head_state_in, wsum):
                clear(ap[:])
            for ap in (before, valid):
                clear(ap[:], 1.0)
            for e in range(E):
                clear(rank_w[:, e:e + 1], float(E - e))
            select(before[:], [[1, P]], -1, -1, GE, 0.0)
            select(sel_head[:], [[-HEADS, 2], [0, NCH], [-1, HEADS]], 0, 1, NE, 1.0)
            select(sel_chunk[:], [[-CT, 2], [-1, CT], [0, CH]], 0, 1, NE, 1.0)
            for q in range(CT):
                quad = slice(CH * q, CH * q + CH)
                clear(chunk_mask[quad, q, :], 1.0)
                clear(mask4[quad, q, :], 1.0)
                select(last_row[quad, :], [[0, 1]], -(CH - 1), 1, NE, 1.0)
                select(decay_in[quad], [[0, HEADS], [-1, SPAN]], 1, 1, NE, -1.0)
                select(decay_in[quad], [[0, HEADS], [-1, SPAN]], 2, 1, NE, 1.0)
                select(resp[quad, HEADS, :], [[-1, SPAN]], 1, 1, NE, float(HEADS))
            made.settle()
            for q in range(2):
                half = head_state_in[64 * q:64 * q + 64, CH::CH]
                clear(half, 1.0)
                select(half, [[-HEADS, NCH - 1]], 0, 1, GE, 0.0)
                select(half, [[HEADS, NCH - 1]], HEADS - 1, -1, GE, 0.0)
            select(valid[:], [[0, B], [1, 2]], -P, 1, NE, 0.0)
            select(pad_pos[:], [[0, B], [1, 2]], -P, 1, NE, float(OUT_OF_RANGE))
            made.step(g.iota(ii[:, 0:32], pattern=[[P, 32]], base=0, channel_multiplier=0))
            made.settle()
            made.step(g.tensor_copy(thr[:], ii[:, 0:32]))
            made.settle()
            made.step(g.iota(ii[:, 0:SLOTS], pattern=[[1, SLOTS]], base=0, channel_multiplier=0))
            made.settle()
            made.step(g.tensor_copy(slot_no[:], ii[:, 0:SLOTS]))
            made.step(g.iota(rows[:, :, D + 3:D + 4].bitcast(I32), pattern=[[NTOK, B], [P, 2]], base=0, channel_multiplier=1))
            made.settle()
            g.iota(init_rows[:, D + 3:D + 4].bitcast(I32), pattern=[[0, 1]], base=OUT_OF_RANGE,
                   channel_multiplier=0).then_inc(s["consts2"], 1)

            pool.wait_ge(s["router_norm"], 1)
            ptt(wg_norm[:, 1:2], wg_norm[:, 0:1], plus_half[:], ALU.pow).then_inc(s["router_root"], 1)

            def roots(b, j):
                t = 2 * b + j
                for n, (src, dst) in enumerate(((4, 5), (7, 8))):
                    pool.wait_ge(s["var_ready"], 2 * t + n + 1)
                    ptt(sm[:, dst:dst + 1], sm[:, src:src + 1], minus_half[:], ALU.pow).then_inc(s["rstd_ready"], 1)

            def expert_lo(n):
                pool.wait_ge(s["w_hi"], apart(pool, 2 * n + 1))
                ptt(w1l[:, n, :], stage1[:], w1h[:, n, :], ALU.subtract).then_inc(s["w_lo"], 1)
                pool.wait_ge(s["w_hi"], apart(pool, 2 * n + 2))
                two = lambda w: w[:, bass.ds(2 * n, 2), :].rearrange("p q d -> p (q d)")
                ptt(two(w2l), stage2[:], two(w2h), ALU.subtract).then_inc(s["w_lo"], 1)

            roots(0, 0)
            roots(0, 1)
            with pool.Fori(0, B - 1) as b:
                roots(b + 1, 0)
                roots(b + 1, 1)
                expert_lo(b)
            expert_lo(B - 1)

            def root2(t, w):
                pool.wait_ge(s["h2_steps"], 3 * t + 3)
                ptt(sm[:, 2 * w + 1:2 * w + 2], sm[:, 2 * w + 1:2 * w + 2], minus_half[:], ALU.pow).then_inc(s["rstd2_ready"], 1)

            with pool.Fori(0, TILES // 2) as h:
                root2(2 * h, 0)
                root2(2 * h + 1, 1)

            pool.wait_ge(s["route_ready"], 1)
            pool.wait_ge(s["init_out"], 16 * SLOTS)
            for t in range(TILES):
                pool.indirect_dma_start(routed, bass.IndirectOffsetOnAxis(ap=posi[:, t:t + 1].bitcast(U32), axis=0),
                                        rows[:, t, :], None, bounds_check=SLOTS * P - 1,
                                        oob_is_err=False).then_inc(s["scattered"], 16)
            def store(i, w):
                pool.wait_ge(s["y_done"], apart(pool, i + 1))
                pool.indirect_dma_start(out_rows, bass.IndirectOffsetOnAxis(ap=oid[:, w:w + 1].bitcast(U32), axis=0),
                                        yo[:, w, :], None, bounds_check=B * NTOK - 1,
                                        oob_is_err=False).then_inc(s[f"y_out_{w}"], 16)

            with pool.Fori(0, ROUNDS) as g_:
                for w in range(RING):
                    store(RING * g_ + w, w)
            for w in range(REST):
                store(RING * ROUNDS + w, w)
            for w in range(RING):
                pool.wait_ge(s[f"y_out_{w}"], 16 * (ROUNDS + (w < REST)))


def kernel(x, L0_tok_W, L0_tok_b, L0_tok_gamma, L0_tok_beta, L0_attn_W_q, L0_attn_W_k, L0_attn_W_v,
           L0_attn_W_alpha_w, L0_attn_W_alpha_b, L0_attn_W_o, L0_ffn_w_red, L0_ffn_wg, L0_ffn_W1,
           L0_ffn_b1, L0_ffn_W2, L0_ffn_b2):
    import concourse.bacc as bacc
    from concourse.bass_utils import run_bass_kernel_spmd

    given = dict(x=x, tok_W=L0_tok_W, tok_b=L0_tok_b, tok_gamma=L0_tok_gamma, tok_beta=L0_tok_beta,
                 W_q=L0_attn_W_q, W_k=L0_attn_W_k, W_v=L0_attn_W_v, W_aw=L0_attn_W_alpha_w,
                 W_ab=L0_attn_W_alpha_b, W_o=L0_attn_W_o, w_red=L0_ffn_w_red, wg=L0_ffn_wg,
                 W1=L0_ffn_W1, b1=L0_ffn_b1, W2=L0_ffn_W2, b2=L0_ffn_b2)
    nc = bacc.Bacc("TRN2", target_bir_lowering=False, num_devices=1)
    arrays, args = {}, []
    for name, value in given.items():
        a = np.ascontiguousarray(value)
        arrays["in_" + name] = a
        args.append(nc.dram_tensor("in_" + name, a.shape, mybir.dt.from_np(a.dtype), kind="ExternalInput").ap())
    args.append(nc.dram_tensor("out", (B, NTOK, D), F32, kind="ExternalOutput").ap())
    build(nc, *args)
    return run_bass_kernel_spmd(nc, [arrays], core_ids=[0]).results[0]["out"]
```

```python
from contextlib import ExitStack

import numpy as np

import concourse.bass as bass
from concourse import mybir

F32 = mybir.dt.float32
F16 = mybir.dt.float16
I32 = mybir.dt.int32
U32 = mybir.dt.uint32
ALU = mybir.AluOpType
ACT = mybir.ActivationFunctionType
AX = mybir.AxisListType.X

P = 128
B, L, DIN = 16, 2048, 64
STRIDE, PATCH = 8, 16
GROUP = STRIDE * DIN
NG = L // STRIDE
NTOK = (L - PATCH) // STRIDE + 1
KG = GROUP // P
KC = 2 * KG
D = 256
DC = D // P
HEADS, DH = 8, 64
HD = HEADS * DH
E, FF = 8, 512
FC = FF // P
TILES = 2 * B
CH = 32
NCH = 2 * P // CH
CT = P // CH
ROWC = D + 4
SLOTS = (B * NTOK + E * (P - 1)) // P
RING = 6
ROUNDS, REST = divmod(SLOTS, RING)
LN_EPS = 1e-5
V_EPS = 1e-8
NEG = -1.0e30
OUT_OF_RANGE = 1 << 20
WS = 64.0
SPAN = CH + 1


class Steps:

    def __init__(self, engine, sem, per):
        self.engine, self.sem, self.per = engine, sem, per

    def begin(self, n):
        self.base, self.done = n * self.per, 0

    def step(self, instruction):
        instruction.then_inc(self.sem, 1)
        self.done += 1

    def settle(self, hold=lambda engine, value: value):
        self.engine.wait_ge(self.sem, hold(self.engine, self.base + self.done))

    def end(self):
        assert self.done == self.per, (self.done, self.per)


def build(nc, x, tok_W, tok_b, tok_gamma, tok_beta, W_q, W_k, W_v, W_aw, W_ab, W_o,
          w_red, wg, W1, b1, W2, b2, out):
    with ExitStack() as ctx:
        def sb(name, shape, dt=F32):
            return ctx.enter_context(nc.sbuf_tensor(name, shape, dt))

        def sem(name):
            return ctx.enter_context(nc.semaphore(name))

        routed = nc.dram_tensor("routed_rows", [SLOTS * P, ROWC], F32, kind="Internal").ap()
        routed_tiles = routed.rearrange("(i p) c -> i p c", p=P)
        lam_by_chunk = nc.dram_tensor("lam_by_chunk", [B, NCH, HEADS, SPAN], F32, kind="Internal").ap()
        lam_by_head = nc.dram_tensor("lam_by_head", [B * HEADS, 2 * P], F32, kind="Internal").ap()
        out_rows = out.rearrange("b n d -> (b n) d")

        banks = ctx.enter_context(nc.psum_tensor("banks", [P, 8, 512], F32))

        rows = sb("rows", [P, TILES, ROWC])
        vo = sb("vo", [P, TILES, D])
        w1h = sb("w1h", [P, E * DC, FF], F16)
        w1l = sb("w1l", [P, E * DC, FF], F16)
        w2h = sb("w2h", [P, E * FC, D], F16)
        w2l = sb("w2l", [P, E * FC, D], F16)
        bsum = sb("bsum", [P, 2, B * HEADS])
        asum = sb("asum", [P, 2, B * HEADS])
        wrg = sb("wrg", [P, DC, E])
        ident = sb("ident", [P, P])
        shift = sb("shift", [P, P])
        corner = sb("corner", [P, P])
        ones = sb("ones", [P, P])
        before = sb("before", [P, P])
        chunk_mask = sb("chunk_mask", [P, CT, CH])
        mask4 = sb("mask4", [P, CT, HEADS])
        last_row = sb("last_row", [P, 1])
        decay_in = sb("decay_in", [P, HEADS, SPAN])
        head_state_in = sb("head_state_in", [P, 2 * P])
        one_col = sb("one_col", [P, 1])
        minus_half = sb("minus_half", [P, 1])
        plus_half = sb("plus_half", [E, 1])
        minus_veps = sb("minus_veps", [P, 1])
        init_rows = sb("init_rows", [P, ROWC])
        colsum = sb("colsum", [P, D])
        tok_bias = sb("tok_bias", [P, D])
        alpha_bias = sb("alpha_bias", [P, HD])
        bias_hl = sb("bias_hl", [2 * E, FF + D], F16)
        minus_low = sb("minus_low", [2 * E, 1])
        pick_expert = sb("pick_expert", [2 * E, E, P], F16)

        early = sb("early", [P, 6272])
        wtok = early[:, 0:2048].rearrange("p (k d) -> p k d", k=KC)
        gT = early[:, 2048:3076].rearrange("p (k g) -> p k g", k=KG)
        xg = early[:, 3076:4100].rearrange("p (j r) -> p j r", j=2)
        q_sb = early[:, 4100:4612]
        qk = early[:, 4612:5124]
        al = early[:, 5124:5636]
        sp = early[:, 5636:6148]
        beta_wide = early[:, 4100:5124].rearrange("p (k m) -> p k m", k=KC)
        proj = sb("proj", [P, 3072])
        wqka_h = proj[:, 0:1536].bitcast(F16).rearrange("p (c o) -> p c o", c=DC)
        wqka_l = proj[:, 1536:3072].bitcast(F16).rearrange("p (c o) -> p c o", c=DC)
        wv_h = sb("wv_h", [P, DC, D], F16)
        wv_l = sb("wv_l", [P, DC, D], F16)
        wo_h = sb("wo_h", [P, DC, D], F16)
        wo_l = sb("wo_l", [P, DC, D], F16)
        xn = sb("xn", [P, 2, D])
        xnT_h = sb("xnT_h", [P, DC, 2 * P], F16)
        xnT_l = sb("xnT_l", [P, DC, 2 * P], F16)
        u = sb("u", [P, DC, 2 * P])
        vT_h = sb("vT_h", [P, DC, 2 * P], F16)
        vT_l = sb("vT_l", [P, DC, 2 * P], F16)
        bias_in = early[0:2 * E, 5124:5124 + FF + D]
        bias_hi = u[0:2 * E].rearrange("p c t -> p (c t)")[:, 0:(FF + D) // 2].bitcast(F16)
        gst6 = sb("gst6", [P, 2, 6])
        gst = sb("gst", [P, 2, 2])
        lst6 = sb("lst6", [P, 6])
        sm = sb("sm", [P, 12])
        stage1 = sb("stage1", [P, 512])
        stage2 = sb("stage2", [P, 512])
        gam_raw = sb("gam_raw", [P, PATCH])
        bet_raw = sb("bet_raw", [P, PATCH])
        gam = sb("gam", [P, KC])
        bet = sb("bet", [P, KC])

        late = {}
        at = 0
        for name, cols in (("bT", 256), ("aT", 256), ("m", 257), ("ea", 256), ("eb", 256), ("r", 257), ("lam", 256)):
            late[name] = proj[:, at:at + cols]
            at += cols
        lam_slots = proj[:, at:at + NCH * SPAN].rearrange("p (c s) -> p c s", c=NCH)
        lam_tile = early[:, 0:4 * HEADS * SPAN].rearrange("p (k f) -> p k f", k=4)
        lam_head = early[:, 4 * HEADS * SPAN:4 * HEADS * SPAN + 2 * P]
        resp = sb("resp", [P, HEADS + 1, SPAN])
        wsum = sb("wsum", [P, CH])
        wbd = sb("wbd", [P, 4, P])
        ends = sb("ends", [P, 4, P])
        qst = sb("qst", [P, 2 * P])
        lst = sb("lst", [P, D])
        xn2 = xn
        xT2 = u

        flat = vo[:].rearrange("p t d -> p (t d)")
        at = 0

        def over(cols):
            nonlocal at
            at += cols
            assert at <= TILES * D
            return flat[:, at - cols:at]

        lg = over(256).rearrange("p (t e) -> p t e", e=E)
        oh = over(256).rearrange("p (t e) -> p t e", e=E)
        t8 = over(256).rearrange("p (t e) -> p t e", e=E)
        tot = over(256).rearrange("p (t e) -> p t e", e=E)
        cum = over(256).rearrange("p (t e) -> p t e", e=E)
        zer = over(256)
        cmp8 = over(SLOTS * E).rearrange("p (i e) -> p i e", e=E)
        rt = over(32 * 4)
        mx, mw, sumexp, posf = (rt[:, 32 * i:32 * i + 32] for i in range(4))
        r8 = over(8 * 4)
        ntile, tend, tstart, _ = (r8[:, 8 * i:8 * i + 8] for i in range(4))
        slotf = over(SLOTS)
        posi = over(32).bitcast(I32)
        sloti = over(SLOTS).bitcast(I32)
        xr = over(RING * ROWC).rearrange("p (w c) -> p w c", w=RING)
        xnD = over(D)
        xh = over(D // 2).bitcast(F16).rearrange("p (c t) -> p c t", c=DC)
        xl = over(D // 2).bitcast(F16).rearrange("p (c t) -> p c t", c=DC)
        gel = over(FF)
        gh = over(FF).bitcast(F16).rearrange("p (w f t) -> p w f t", w=2, f=FC)
        gl = over(FF).bitcast(F16).rearrange("p (w f t) -> p w f t", w=2, f=FC)
        yo = proj[:, 0:RING * D].rearrange("p (w d) -> p w d", w=RING)
        valid = sb("valid", [P, TILES])
        pad_pos = sb("pad_pos", [P, TILES])
        rank_w = sb("rank_w", [P, E])
        thr = sb("thr", [P, 32])
        slot_no = sb("slot_no", [P, SLOTS])
        ii = sb("ii", [P, 64], I32)
        oid = sb("oid", [P, RING], I32)
        wred_sb = sb("wred_sb", [P, DC, 16])
        wg_sb = sb("wg_sb", [E, 16])
        wg_sq = sb("wg_sq", [E, 16])
        wg_norm = sb("wg_norm", [E, 2])
        wbd_flat = wbd[:].rearrange("p k s -> p (k s)")
        router_T = wbd_flat[0:16, 0:D + E]
        tokc = wbd_flat[:, D:2 * D]
        tok_b_wide = lst

        raw = flat[:, 0:16 * D].rearrange("p (o c) -> p o c", c=D)

        names = """consts consts2 const_steps_p init_out wload wraw_ready misc_in tok_w_in wsplit_hi wsplit_lo
            beta_wide_ready bias_ready gamma_done colsum_ready tokprep
            router_norm router_root router_steps router_prep router_t router_weights router_mm
            x_in xt_ready xt_evac gst_done gst_steps tok_done h_done ln_steps var_ready rstd_ready xn_ready
            xnt_ready xhi_done xlo_done q_ready k_ready al_ready q_copied qk_done al_copied act_steps
            ln_done sp_steps sp_done vt_ready u_steps u_done vh_done vl_done vo_ready vo_copied
            w_in w_hi w_lo
            ba_ready gate_steps gate_exp gate_args lam_done lam_slots_done lam_out
            lam_in_0 lam_in_1 lam_in_2 lam_in_3 lam_used es_steps es_ready l_ready l_copied out_ready h2_done h2_steps var2_ready rstd2_ready
            xn2_ready t2_ready t2_evac lg_done lam_head_in q_done
            r_steps r_args r_exp oh_ready counts route_ready scattered bias_split bias_done
            row_in_0 row_in_1 row_in_2 row_in_3 row_in_4 row_in_5 xd_ready xdt_ready xdh_done xdl_done m1_ready gelu_done gt_ready gh_done g_done
            m2_ready y_steps y_done y_out_0 y_out_1 y_out_2 y_out_3 y_out_4 y_out_5""".split()
        s = {n: sem(n) for n in names}

        def bank(i, n=512):
            return banks[:, i, 0:n]

        def apart(engine, value):
            if not isinstance(value, int):
                value = engine.snap(engine.to_reg(value))
            engine.wait_ge(s["consts"], 1)
            return value

        block = ctx.enter_context(nc.Block())

        @block.sync
        def _(sp_):
            for m, w in enumerate((W_q, W_k, W_aw)):
                sp_.dma_start(raw[:, 4 * m:4 * m + 4, :], w.rearrange("(o p) c -> p o c", p=P)).then_inc(s["wraw_ready"], 16)
            sp_.dma_start(raw[:, 12:14, :], W_v.rearrange("(o p) c -> p o c", p=P)).then_inc(s["wraw_ready"], 16)
            sp_.dma_start(raw[:, 14:16, :], W_o.rearrange("(o p) c -> p o c", p=P)).then_inc(s["wraw_ready"], 16)

            def load_x(b):
                if not (isinstance(b, int) and b == 0):
                    sp_.wait_ge(s["xt_ready"], 2 * b)
                    sp_.wait_ge(s["gst_done"], b)
                sp_.dma_start(xg, x[b].rearrange("(j g r) c -> g j (r c)", j=2, r=STRIDE)).then_inc(s["x_in"], 16)

            def load_expert_part(n):
                if not (isinstance(n, int) and n == 0):
                    sp_.wait_ge(s["w_lo"], 2 * n)
                sp_.dma_start(stage1[:], W1.rearrange("e (c p) f -> (e c) p f", p=P)[n]).then_inc(s["w_in"], 16)
                sp_.dma_start(stage2[:].rearrange("p (q d) -> p q d", q=2),
                              W2.rearrange("e (n q p) d -> (e n) p q d", q=2, p=P)[n]).then_inc(s["w_in"], 16)

            for t2 in range(2):
                half = slice(DIN * t2, DIN * t2 + DIN)
                sp_.dma_start(wtok[half], tok_W.rearrange("(d k t) o -> t d k o", k=KC, t=2)[t2]).then_inc(s["tok_w_in"], 16)
                sp_.dma_start(gam_raw[half, :], tok_gamma.rearrange("(d t) -> d t", t=PATCH)).then_inc(s["tok_w_in"], 16)
                sp_.dma_start(bet_raw[half, :], tok_beta.rearrange("(d t) -> d t", t=PATCH)).then_inc(s["tok_w_in"], 16)
            sp_.dma_start(tok_b_wide[:], tok_b.partition_broadcast(P)).then_inc(s["misc_in"], 16)
            sp_.dma_start(alpha_bias[:], W_ab.partition_broadcast(P)).then_inc(s["misc_in"], 16)
            sp_.dma_start(wred_sb[:], w_red.rearrange("(c p) g -> p c g", p=P)).then_inc(s["misc_in"], 16)
            sp_.dma_start(wg_sb[:], wg).then_inc(s["misc_in"], 16)
            for half in range(2):
                two = slice(E * half, E * half + E)
                sp_.dma_start(bias_in[two, 0:FF], b1).then_inc(s["misc_in"], 16)
                sp_.dma_start(bias_in[two, FF:FF + D], b2).then_inc(s["misc_in"], 16)

            load_x(0)
            load_expert_part(0)
            load_x(1)
            load_x(2)
            sp_.wait_ge(s["consts2"], 1)
            per = SLOTS // (B - 3)
            assert per * (B - 3) == SLOTS
            with sp_.Fori(3, B) as b:
                load_expert_part(b - 2)
                load_x(b)
                for n in range(per):
                    sp_.dma_start(routed_tiles[per * (b - 3) + n], init_rows[:]).then_inc(s["init_out"], 16)
            load_expert_part(B - 2)
            load_expert_part(B - 1)

            sp_.wait_ge(s["lam_done"], 1)
            sp_.dma_start(lam_by_head, late["lam"]).then_inc(s["lam_out"], 16)
            sp_.wait_ge(s["lam_slots_done"], 1)
            for c in range(0, NCH, 2):
                sp_.dma_start(lam_by_chunk[:, c], lam_slots[:, c, :]).then_inc(s["lam_out"], 16)
            sp_.wait_ge(s["lam_out"], 16 * (1 + NCH))

            def load_tile_decays(p, k, first=False):
                if not first:
                    sp_.wait_ge(s["lam_used"], 4 * p + k - 3)
                sp_.dma_start(lam_tile[:, k, :], lam_by_chunk[2 * p + k // 2, CT * (k % 2):CT * (k % 2) + CT]
                              .rearrange("c h s -> c (h s)").unsqueeze(1).to_broadcast([CT, CH, HEADS * SPAN])
                              ).then_inc(s[f"lam_in_{k}"], 16)

            def load_head_decays(p, first=False):
                if not first:
                    sp_.wait_ge(s["q_done"], p)
                for half in range(2):
                    sp_.dma_start(lam_head[64 * half:64 * half + 64, :],
                                  lam_by_head.rearrange("(b h) t -> b h t", h=HEADS)[2 * p + half]
                                  .unsqueeze(0).to_broadcast([NCH, HEADS, 2 * P])).then_inc(s["lam_head_in"], 16)

            for k in range(4):
                load_tile_decays(0, k, True)
            load_head_decays(0, True)
            with sp_.Fori(1, TILES // 4) as p:
                for k in range(4):
                    load_tile_decays(p, k)
                load_head_decays(p)

            sp_.wait_ge(s["scattered"], 16 * TILES)

            def load_rows(i, w, first=False):
                if not first:
                    sp_.wait_ge(s["y_done"], i - RING + 1)
                sp_.dma_start(xr[:, w, :], routed_tiles[i]).then_inc(s[f"row_in_{w}"], 16)

            for w in range(RING):
                load_rows(w, w, True)
            with sp_.Fori(1, ROUNDS) as g:
                for w in range(RING):
                    load_rows(RING * g + w, w)
            for w in range(REST):
                load_rows(RING * ROUNDS + w, w)

        @block.tensor
        def _(pe):
            mm, tr = nc.tensor.matmul, nc.tensor.transpose

            pe.wait_ge(s["consts"], 1)
            pe.wait_ge(s["wraw_ready"], 80)
            for m in range(3):
                for c in range(DC):
                    for o in range(4):
                        last = tr(bank(2 * m + c)[:, o * P:o * P + P], raw[:, 4 * m + o, c * P:c * P + P], ident[:])
                    last.then_inc(s["wload"], 1)
            for m in range(2):
                for c in range(DC):
                    for o in range(2):
                        last = tr(bank(6 + m)[:, c * D + o * P:c * D + o * P + P], raw[:, 12 + 2 * m + o, c * P:c * P + P], ident[:])
                last.then_inc(s["wload"], 1)

            pe.wait_ge(s["beta_wide_ready"], 1)
            pe.wait_ge(s["wsplit_lo"], 2)
            for k in range(KC):
                last = mm(bank(1, D), beta_wide[:, k, :], wtok[:, k, :], start=(k == 0), stop=(k == KC - 1))
            last.then_inc(s["bias_ready"], 1)

            def column_sums():
                pe.wait_ge(s["gamma_done"], 1)
                for k in range(KC):
                    last = mm(bank(4, D), ones[:], wtok[:, k, :], start=(k == 0), stop=(k == KC - 1))
                last.then_inc(s["colsum_ready"], 1)

            def transpose_router():
                pe.wait_ge(s["router_prep"], 1)
                for c in range(DC):
                    tr(banks[0:16, 5, c * P:c * P + P], wred_sb[:, c, :], ident[:])
                tr(banks[0:16, 5, D:D + E], wg_sb[:, :], ident[0:E, 0:E]).then_inc(s["router_t"], 1)

            def multiply_router():
                pe.wait_ge(s["router_weights"], 1)
                for c in range(DC):
                    last = mm(banks[:, 6, c * E:c * E + E], router_T[:, c * P:c * P + P], router_T[:, D:D + E],
                              start=True, stop=True)
                last.then_inc(s["router_mm"], 1)

            def transpose_x(b, j):
                if j == 0:
                    pe.wait_ge(s["x_in"], 16 * (b + 1))
                if isinstance(b, int) and b == 0 and j == 0:
                    pe.wait_ge(s["wsplit_lo"], 8)
                else:
                    pe.wait_ge(s["xt_evac"], 2 * b + j)
                for k in range(KG):
                    last = tr(bank(0)[:, k * P:k * P + P], xg[:, j, k * P:k * P + P], ident[:])
                last.then_inc(s["xt_ready"], 1)

            def tokenise(b, j):
                if j == 0:
                    pe.wait_ge(s["xt_evac"], 2 * b + 2)
                if not (isinstance(b, int) and b == 0):
                    pe.wait_ge(s["h_done"], 2 * b + j - 1)
                for k in range(KG):
                    mm(bank(2 + j, D), gT[:, k, j * P:j * P + P], wtok[:, k, :], start=(k == 0), stop=False)
                for k in range(KG):
                    mm(bank(2 + j, D), gT[:, k, j * P + 1:j * P + 1 + P], wtok[:, KG + k, :], start=False, stop=(k == KG - 1))
                if j == 0:
                    pe.wait_ge(s["gst_done"], b + 1)
                last = mm(banks[:, 2 + j, D:D + 2], shift[:], gst[:, j, :], start=True, stop=(j == 1))
                if j == 0:
                    last = mm(banks[:, 2 + j, D:D + 2], corner[:], gst[:, 1, :], start=False, stop=True)
                last.then_inc(s["tok_done"], 1)

            def transpose_xn(b):
                if not (isinstance(b, int) and b == 0):
                    pe.wait_ge(s["xlo_done"], b)
                for j in range(2):
                    pe.wait_ge(s["xn_ready"], 2 * b + j + 1)
                    for c in range(DC):
                        last = tr(bank(1)[:, c * D + j * P:c * D + j * P + P], xn[:, j, c * P:c * P + P], ident[:])
                last.then_inc(s["xnt_ready"], 1)

            def three(dst, pairs):
                n = 3 * len(pairs)
                i = 0
                for lh, ll, rh, rl in pairs:
                    for a, c in ((lh, rh), (lh, rl), (ll, rh)):
                        last = mm(dst, a, c, start=(i == 0), stop=(i == n - 1))
                        i += 1
                return last

            def project(b, j, first=False):
                if j == 0:
                    pe.wait_ge(s["xlo_done"], b + 1)
                for m in ((1, 2, 0), (2, 0, 1))[j]:
                    rdy, free = (("q_ready", "q_copied"), ("k_ready", "qk_done"), ("al_ready", "al_copied"))[m]
                    if m == 0 and j == 0 and not first:
                        pe.wait_ge(s["vo_copied"], b)
                    if not (first and j == 0):
                        pe.wait_ge(s[free], 2 * b + j)
                    three(bank(4 + m), [(xnT_h[:, c, j * P:j * P + P], xnT_l[:, c, j * P:j * P + P],
                                         wqka_h[:, c, m * HD:m * HD + HD], wqka_l[:, c, m * HD:m * HD + HD])
                                        for c in range(DC)]).then_inc(s[rdy], 1)

            def project_v(b, first=False):
                if not first:
                    pe.wait_ge(s["u_done"], b)
                for o in range(DC):
                    last = three(bank(7)[:, o * D:o * D + D],
                                 [(wv_h[:, c, o * P:o * P + P], wv_l[:, c, o * P:o * P + P], xnT_h[:, c, :], xnT_l[:, c, :])
                                  for c in range(DC)])
                last.then_inc(s["vt_ready"], 1)

            def project_out(b):
                pe.wait_ge(s["vl_done"], b + 1)
                pe.wait_ge(s["q_copied"], 2 * b + 2)
                for j in range(2):
                    last = three(bank(4)[:, j * D:j * D + D],
                                 [(vT_h[:, c, j * P:j * P + P], vT_l[:, c, j * P:j * P + P], wo_h[:, c, :], wo_l[:, c, :])
                                  for c in range(DC)])
                last.then_inc(s["vo_ready"], 1)

            def step(b, first=False, ahead=2):
                if ahead >= 1:
                    tokenise(b + 1, 0)
                    if first:
                        transpose_xn(b)
                    tokenise(b + 1, 1)
                if not first:
                    project_out(b - 1)
                project(b, 0, first)
                if ahead >= 2:
                    transpose_x(b + 2, 0)
                project(b, 1, first)
                if ahead >= 2:
                    transpose_x(b + 2, 1)
                project_v(b, first)
                if ahead >= 1:
                    transpose_xn(b + 1)

            transpose_x(0, 0)
            transpose_x(0, 1)
            column_sums()
            transpose_router()
            tokenise(0, 0)
            multiply_router()
            tokenise(0, 1)
            transpose_x(1, 0)
            transpose_x(1, 1)
            step(0, first=True)
            with pe.Fori(1, B - 2) as b:
                step(b)
            step(B - 2, ahead=1)
            step(B - 1, ahead=0)
            project_out(B - 1)

            pe.wait_ge(s["sp_done"], TILES)
            pe.wait_ge(s["xt_evac"], TILES)
            pe.wait_ge(s["xlo_done"], B)
            for k, src in enumerate((bsum, asum)):
                for j in range(2):
                    last = tr(banks[:, k, j * P:j * P + P], src[:, j, :], ident[:])
            last.then_inc(s["ba_ready"], 1)

            def chunk_end(p, k):
                pe.wait_ge(s["es_ready"], apart(pe, 4 * p + k + 1))
                if k == 0 and not (isinstance(p, int) and p == 0):
                    pe.wait_ge(s["l_copied"], p)
                last = mm(bank(4, D), ends[:, k, :], vo[:, 4 * p + k, :], start=(k == 0), stop=(k == 3))
                if k == 3:
                    last.then_inc(s["l_ready"], 1)

            def mix(p, k):
                t = 4 * p + k
                b2_, j = k // 2, k % 2
                if not (isinstance(p, int) and t < 2):
                    pe.wait_ge(s["h2_done"], t - 1)
                mm(bank(2 + k % 2, D), wbd[:, k, :], vo[:, t, :], start=True, stop=False)
                if k == 0:
                    pe.wait_ge(s["q_done"], p + 1)
                    pe.wait_ge(s["l_copied"], p + 1)
                mm(bank(2 + k % 2, D), qst[64 * b2_:64 * b2_ + 64, j * P:j * P + P], lst[64 * b2_:64 * b2_ + 64, :],
                   start=False, stop=True).then_inc(s["out_ready"], 1)

            def transpose_xn2(t, w):
                pe.wait_ge(s["xn2_ready"], t + 1)
                if not (isinstance(t, int) and t == 0):
                    pe.wait_ge(s["t2_evac"], t)
                for c in range(DC):
                    last = tr(bank(6)[:, c * P:c * P + P], xn2[:, w, c * P:c * P + P], ident[:])
                last.then_inc(s["t2_ready"], 1)

            def logits(t, w):
                pe.wait_ge(s["t2_evac"], t + 1)
                for c in range(DC):
                    last = mm(banks[:, 7, bass.ds(t * E, E)], xT2[:, w, c * P:c * P + P], wrg[:, c, :],
                              start=(c == 0), stop=(c == DC - 1))
                last.then_inc(s["lg_done"], 1)

            def pair(p, ahead=True):
                for k in range(4):
                    mix(p, k)
                    t = 4 * p + k
                    if not (isinstance(p, int) and t < 3):
                        logits(t - 3, (k + 1) % 2)
                    if not (isinstance(p, int) and t < 2):
                        transpose_xn2(t - 2, k % 2)
                    if ahead and k > 0:
                        chunk_end(p + 1, k - 1)
                if ahead:
                    chunk_end(p + 1, 3)

            pe.wait_ge(s["consts2"], 1)
            pe.wait_ge(s["gate_steps"], 2)
            pe.wait_ge(s["vo_copied"], B)
            pe.wait_ge(s["qk_done"], TILES)
            pe.wait_ge(s["al_copied"], TILES)
            pe.wait_ge(s["u_done"], B)
            for k in range(4):
                chunk_end(0, k)
            pair(0)
            with pe.Fori(1, 7) as p:
                pair(p)
            pair(7, ahead=False)
            logits(TILES - 3, 1)
            transpose_xn2(TILES - 2, 0)
            logits(TILES - 2, 0)
            transpose_xn2(TILES - 1, 1)
            logits(TILES - 1, 1)

            pe.wait_ge(s["oh_ready"], 1)
            ohf = oh.rearrange("p t e -> p (t e)")
            mm(bank(0, 256), before[:], ohf, start=True, stop=True)
            mm(bank(1, 256), ones[:], ohf, start=True, stop=True).then_inc(s["counts"], 1)

            def transpose_rows(i):
                pe.wait_ge(s["xd_ready"], i + 1)
                if not (isinstance(i, int) and i == 0):
                    pe.wait_ge(s["xdl_done"], i)
                for c in range(DC):
                    last = tr(bank(2)[:, c * P:c * P + P], xnD[:, c * P:c * P + P], ident[:])
                last.then_inc(s["xdt_ready"], 1)

            def expert_of(i):
                return pe.value_load(sloti[0:1, bass.ds(i, 1)], min_val=0, max_val=E - 1)

            def up(i, e):
                pe.wait_ge(s["xdl_done"], i + 1)
                if not (isinstance(i, int) and i == 0):
                    pe.wait_ge(s["gelu_done"], i)
                for c in range(DC):
                    for x_, w in ((xh, w1h), (xh, w1l), (xl, w1h)):
                        mm(bank(0), x_[:, c, :], w[:, bass.ds(e * DC + c, 1), :].rearrange("p a b -> p (a b)"),
                           start=(c == 0 and w is w1h and x_ is xh), stop=False)
                mm(bank(0), pick_expert[:, bass.ds(e, 1), :].rearrange("p a b -> p (a b)"), bias_hl[:, 0:FF],
                   start=False, stop=True).then_inc(s["m1_ready"], 1)

            def transpose_gelu(i, w):
                pe.wait_ge(s["gelu_done"], i + 1)
                if not (isinstance(i, int) and i < 2):
                    pe.wait_ge(s["g_done"], i - 1)
                for f in range(FC):
                    last = tr(bank(4 + w)[:, f * P:f * P + P], gel[:, f * P:f * P + P], ident[:])
                last.then_inc(s["gt_ready"], 1)

            def down(i, w, e):
                pe.wait_ge(s["g_done"], i + 1)
                if not (isinstance(i, int) and i == 0):
                    pe.wait_ge(s["y_steps"], i)
                for f in range(FC):
                    for a, w_ in ((gh, w2h), (gh, w2l), (gl, w2h)):
                        mm(bank(3, D), a[:, w, f, :], w_[:, bass.ds(e * FC + f, 1), :].rearrange("p a b -> p (a b)"),
                           start=(f == 0 and w_ is w2h and a is gh), stop=False)
                mm(bank(3, D), pick_expert[:, bass.ds(e, 1), :].rearrange("p a b -> p (a b)"), bias_hl[:, FF:FF + D],
                   start=False, stop=True).then_inc(s["m2_ready"], 1)

            def slots(g, count=RING, first=False, last=False):
                i0 = RING * g
                experts = {0: expert_of(i0)}
                for w in range(count):
                    up(i0 + w, experts[w])
                    if w + 1 < count:
                        experts[w + 1] = expert_of(i0 + w + 1)
                    if w < 2 and not first:
                        experts[w - 2] = expert_of(i0 + w - 2)
                    if not (last and w == count - 1):
                        transpose_rows(i0 + w + 1)
                    if not (first and w == 0):
                        transpose_gelu(i0 + w - 1, (w - 1) % 2)
                    if not (first and w < 2):
                        down(i0 + w - 2, w % 2, experts[w - 2])
                return experts

            pe.wait_ge(s["route_ready"], 1)
            pe.wait_ge(s["bias_done"], 1)
            transpose_rows(0)
            slots(0, first=True)
            with pe.Fori(1, ROUNDS) as g:
                slots(g)
            experts = slots(ROUNDS, REST, last=True)
            transpose_gelu(SLOTS - 1, (REST - 1) % 2)
            down(SLOTS - 2, (REST - 2) % 2, experts[REST - 2])
            down(SLOTS - 1, (REST - 1) % 2, experts[REST - 1])

        @block.scalar
        def _(act):
            af = nc.scalar.activation
            act.wait_ge(s["consts"], 1)
            for m in range(3):
                for c in range(DC):
                    act.wait_ge(s["wload"], 2 * m + c + 1)
                    af(wqka_h[:, c, m * HD:m * HD + HD], bank(2 * m + c), ACT.Copy, scale=WS).then_inc(s["wsplit_hi"], 1)
            for m, dst in enumerate((wv_h, wo_h)):
                act.wait_ge(s["wload"], 7 + m)
                af(dst[:].rearrange("p c o -> p (c o)"), bank(6 + m), ACT.Copy, scale=WS).then_inc(s["wsplit_hi"], 1)

            act.preload_act_table_set("natural_log_exp_and_others")
            act.wait_ge(s["misc_in"], 16 * 8)
            af(bias_hi, bias_in, ACT.Copy).then_inc(s["bias_split"], 1)
            steps = Steps(act, s["act_steps"], 2)

            def keep_xT(b, j):
                act.wait_ge(s["xt_ready"], 2 * b + j + 1)
                if not (isinstance(b, int) and b == 0):
                    act.wait_ge(s["tok_done"], 2 * b)
                af(gT[:, :, j * P:j * P + P], bank(0).rearrange("p (k g) -> p k g", k=KG), ACT.Copy).then_inc(s["xt_evac"], 1)

            def split_xn(b):
                act.wait_ge(s["xnt_ready"], b + 1)
                if not (isinstance(b, int) and b == 0):
                    act.wait_ge(s["vt_ready"], b)
                af(xnT_h[:].rearrange("p c t -> p (c t)"), bank(1), ACT.Copy).then_inc(s["xhi_done"], 1)

            def copy_q(b, j, first=False):
                act.wait_ge(s["q_ready"], 2 * b + j + 1)
                if not (first and j == 0):
                    act.wait_ge(s["qk_done"], 2 * b + j)
                af(q_sb, bank(4), ACT.Copy).then_inc(s["q_copied"], 1)

            def log_part(b, j, first=False):
                t = 2 * b + j
                steps.begin(t)
                act.wait_ge(s["al_copied"], t + 1)
                if not (first and j == 0):
                    act.wait_ge(s["sp_done"], t)
                steps.step(af(sp, al, ACT.Abs))
                steps.settle()
                steps.step(af(sp, sp, ACT.Exp, scale=-1.0))
                steps.settle()
                steps.end()
                af(sp, sp, ACT.Ln, bias=one_col[:]).then_inc(s["ln_done"], 1)

            def split_v(b):
                act.wait_ge(s["u_done"], b + 1)
                if not (isinstance(b, int) and b == 0):
                    act.wait_ge(s["vo_ready"], b)
                af(vT_h[:].rearrange("p c t -> p (c t)"), u[:].rearrange("p c t -> p (c t)"), ACT.Identity,
                   bias=minus_veps[:]).then_inc(s["vh_done"], 1)

            def keep_vo(b):
                act.wait_ge(s["vo_ready"], b + 1)
                if isinstance(b, int) and b == 0:
                    act.wait_ge(s["wsplit_lo"], 8)
                af(vo[:, bass.ds(2 * b, 2), :].rearrange("p t d -> p (t d)"), bank(4), ACT.Copy,
                   scale=1.0 / WS).then_inc(s["vo_copied"], 1)

            def split_expert(n):
                act.wait_ge(s["w_in"], 32 * n + 32)
                af(w1h[:, n, :], stage1[:], ACT.Copy).then_inc(s["w_hi"], 1)
                af(w2h[:, bass.ds(2 * n, 2), :].rearrange("p q d -> p (q d)"), stage2[:], ACT.Copy).then_inc(s["w_hi"], 1)

            def step(b, first=False, ahead=2):
                if not first:
                    split_v(b - 1)
                    keep_vo(b - 1)
                copy_q(b, 0, first)
                log_part(b, 0, first)
                if ahead >= 2:
                    keep_xT(b + 2, 0)
                copy_q(b, 1)
                if ahead >= 2:
                    keep_xT(b + 2, 1)
                log_part(b, 1)
                split_expert(b)
                if ahead >= 1:
                    split_xn(b + 1)

            for j in range(2):
                keep_xT(0, j)
            for j in range(2):
                keep_xT(1, j)
            split_xn(0)
            step(0, first=True)
            with act.Fori(1, B - 2) as b:
                step(b)
            step(B - 2, ahead=1)
            step(B - 1, ahead=0)
            split_v(B - 1)
            keep_vo(B - 1)

            act.wait_ge(s["gate_args"], 1)
            af(late["ea"], late["ea"], ACT.Exp).then_inc(s["gate_exp"], 1)
            act.wait_ge(s["gate_args"], 2)
            af(late["eb"], late["eb"], ACT.Exp).then_inc(s["gate_exp"], 1)
            act.wait_ge(s["lam_slots_done"], 1)
            for c in range(1, NCH, 2):
                act.dma_start(lam_by_chunk[:, c], lam_slots[:, c, :]).then_inc(s["lam_out"], 16)

            def keep_ends(p):
                act.wait_ge(s["l_ready"], p + 1)
                af(lst[:], bank(4, D), ACT.Copy).then_inc(s["l_copied"], 1)

            def keep_xT2(t, w):
                act.wait_ge(s["t2_ready"], t + 1)
                if not (isinstance(t, int) and t < 2):
                    act.wait_ge(s["lg_done"], t - 1)
                af(xT2[:, w, :], bank(6, D), ACT.Copy).then_inc(s["t2_evac"], 1)

            keep_ends(0)
            for k in range(2, 4):
                keep_xT2(k - 2, k % 2)
            with act.Fori(1, TILES // 4) as p:
                keep_ends(p)
                for k in range(4):
                    keep_xT2(4 * p + k - 2, k % 2)
            for k in range(2):
                keep_xT2(TILES - 2 + k, k)

            act.wait_ge(s["r_args"], 1)
            af(t8.rearrange("p t e -> p (t e)"), t8.rearrange("p t e -> p (t e)"), ACT.Exp).then_inc(s["r_exp"], 1)
            act.wait_ge(s["route_ready"], 1)

            def split_rows(i):
                act.wait_ge(s["xdt_ready"], i + 1)
                if not (isinstance(i, int) and i == 0):
                    act.wait_ge(s["m1_ready"], i)
                af(xh.rearrange("p c t -> p (c t)"), bank(2, D), ACT.Copy).then_inc(s["xdh_done"], 1)

            def gelu(i):
                act.wait_ge(s["m1_ready"], i + 1)
                if not (isinstance(i, int) and i == 0):
                    act.wait_ge(s["gt_ready"], i)
                af(gel, bank(0), ACT.Gelu).then_inc(s["gelu_done"], 1)

            def split_gelu(i, w):
                act.wait_ge(s["gt_ready"], i + 1)
                if not (isinstance(i, int) and i < 2):
                    act.wait_ge(s["m2_ready"], i - 1)
                af(gh[:, w].rearrange("p f t -> p (f t)"), bank(4 + w), ACT.Copy).then_inc(s["gh_done"], 1)

            def slots(g, count=RING, first=False, last=False):
                for w in range(count):
                    i = RING * g + w
                    if not (last and w == count - 1):
                        split_rows(i + 1)
                    gelu(i)
                    if not (first and w == 0):
                        split_gelu(i - 1, (w - 1) % 2)

            split_rows(0)
            slots(0, first=True)
            with act.Fori(1, ROUNDS) as g:
                slots(g)
            slots(ROUNDS, REST, last=True)
            split_gelu(SLOTS - 1, (REST - 1) % 2)

        @block.vector
        def _(dve):
            tt, ts, stt = nc.vector.tensor_tensor, nc.vector.tensor_scalar, nc.vector.scalar_tensor_tensor
            copy, reduce, scan = nc.vector.tensor_copy, nc.vector.tensor_reduce, nc.vector.tensor_tensor_scan

            def wide(ap, shape):
                return ap.unsqueeze(2).to_broadcast(shape)

            def repeated(ap, shape):
                return ap.unsqueeze(1).to_broadcast(shape)

            def weights_lo(n, dst):
                dve.wait_ge(s["wsplit_hi"], n + 1)
                hi, lo = dst
                stt(lo, bank(n), WS, hi, ALU.mult, ALU.subtract).then_inc(s["wsplit_lo"], 1)

            dve.wait_ge(s["consts"], 1)
            dve.wait_ge(s["tok_w_in"], 96)
            prep = Steps(dve, s["router_steps"], 7)
            prep.begin(0)
            nc.vector.memset(gT[:, :, 2 * P:2 * P + 1], 0.0)
            for t2 in range(2):
                half = slice(DIN * t2, DIN * t2 + DIN)
                prep.step(copy(gam[half, :], gam_raw[half, t2::2]))
                prep.step(copy(bet[half, :], bet_raw[half, t2::2]))
            prep.settle()
            copy(beta_wide, wide(bet[:], [P, KC, P])).then_inc(s["beta_wide_ready"], 1)
            dve.wait_ge(s["misc_in"], 16 * 8)
            prep.step(tt(wg_sq[:], wg_sb[:], wg_sb[:], ALU.mult))
            prep.settle()
            reduce(wg_norm[:, 0:1], wg_sq[:], AX, ALU.add).then_inc(s["router_norm"], 1)
            for n in range(8):
                m, c = n // 2, n % 2
                if n < 6:
                    weights_lo(n, (wqka_h[:, c, m * HD:m * HD + HD], wqka_l[:, c, m * HD:m * HD + HD]))
                else:
                    hi, lo = ((wv_h, wv_l), (wo_h, wo_l))[n - 6]
                    weights_lo(n, (hi[:].rearrange("p c o -> p (c o)"), lo[:].rearrange("p c o -> p (c o)")))
            dve.wait_ge(s["bias_ready"], 1)
            tt(wtok, wtok, wide(gam[:], [P, KC, D]), ALU.mult).then_inc(s["gamma_done"], 1)
            tt(tok_bias[:], bank(1, D), tok_b_wide[:], ALU.add)
            dve.wait_ge(s["router_root"], 1)
            prep.step(ts(wg_norm[:, 1:2], wg_norm[:, 1:2], 1e-4, None, ALU.max))
            prep.settle()
            prep.step(nc.vector.reciprocal(wg_norm[:, 0:1], wg_norm[:, 1:2]))
            prep.settle()
            prep.end()
            ts(wg_sb[:], wg_sb[:], wg_norm[:, 0:1], None, ALU.mult).then_inc(s["router_prep"], 1)

            def prologue_rest():
                dve.wait_ge(s["router_t"], 1)
                copy(router_T, banks[0:16, 5, 0:D + E]).then_inc(s["router_weights"], 1)
                copy(colsum[:], bank(4, D))
                dve.wait_ge(s["bias_split"], 1)
                stt(bias_hl[:], bias_hi, minus_low[:], bias_in, ALU.mult, ALU.add).then_inc(s["bias_done"], 1)
                dve.wait_ge(s["router_mm"], 1)
                copy(wrg[:].rearrange("p c e -> p (c e)"), banks[:, 6, 0:DC * E]).then_inc(s["tokprep"], 1)
                dve.wait_ge(s["bias_done"], 1)
                dve.wait_ge(s["tokprep"], 1)

            gsteps = Steps(dve, s["gst_steps"], 3)
            lsteps = Steps(dve, s["ln_steps"], 7)
            ssteps = Steps(dve, s["sp_steps"], 1)
            usteps = Steps(dve, s["u_steps"], 1)

            def group_stats(b):
                gsteps.begin(b)
                dve.wait_ge(s["x_in"], 16 * (b + 1))
                if not (isinstance(b, int) and b == 0):
                    dve.wait_ge(s["tok_done"], 2 * b)
                for j in range(2):
                    gsteps.step(nc.vector.bn_stats(gst6[:, j, :], xg[:, j, :]))
                gsteps.settle(apart)
                gsteps.step(nc.vector.bn_aggr(gst[:, 0, :], gst6[:, 0, :]))
                nc.vector.bn_aggr(gst[:, 1, :], gst6[:, 1, :]).then_inc(s["gst_done"], 1)
                gsteps.end()

            def normalise(b, j):
                t = 2 * b + j
                lsteps.begin(t)
                dve.wait_ge(s["tok_done"], t + 1)
                nxt = banks[:, 2 + j, D:D + 2]
                lsteps.step(tt(sm[:, 0:2], gst[:, j, :], nxt, ALU.add))
                lsteps.settle()
                lsteps.step(stt(sm[:, 3:4], sm[:, 0:1], -0.5, gst[:, j, 0:1], ALU.mult, ALU.add))
                lsteps.step(ts(sm[:, 2:3], sm[:, 1:2], 0.5, LN_EPS, ALU.mult, ALU.add))
                lsteps.settle()
                stt(sm[:, 4:5], sm[:, 3:4], sm[:, 3:4], sm[:, 2:3], ALU.mult, ALU.add).then_inc(s["var_ready"], 1)
                dve.wait_ge(s["rstd_ready"], 2 * t + 1)
                lsteps.step(stt(sm[:, 6:7], sm[:, 0:1], -0.5, sm[:, 5:6], ALU.mult, ALU.mult))
                lsteps.settle()
                lsteps.step(stt(tokc, colsum[:], sm[:, 6:7], tok_bias[:], ALU.mult, ALU.add))
                lsteps.settle()
                h = rows[:, bass.ds(t, 1), 0:D].rearrange("p a b -> p (a b)")
                stt(h, bank(2 + j, D), sm[:, 5:6], tokc, ALU.mult, ALU.add).then_inc(s["h_done"], 1)
                dve.wait_ge(s["h_done"], apart(dve, t + 1))
                lsteps.step(nc.vector.bn_stats(lst6[:], h))
                lsteps.settle(apart)
                lsteps.step(nc.vector.bn_aggr(sm[:, 9:11], lst6[:]))
                lsteps.settle()
                lsteps.end()
                ts(sm[:, 7:8], sm[:, 10:11], LN_EPS, None, ALU.add).then_inc(s["var_ready"], 1)
                dve.wait_ge(s["rstd_ready"], 2 * t + 2)
                if not (isinstance(b, int) and b == 0):
                    dve.wait_ge(s["xnt_ready"], b)
                ts(xn[:, j, :], h, sm[:, 9:10], sm[:, 8:9], ALU.subtract, ALU.mult).then_inc(s["xn_ready"], 1)

            def split_xn(b):
                dve.wait_ge(s["xhi_done"], b + 1)
                if not (isinstance(b, int) and b == 0):
                    dve.wait_ge(s["vt_ready"], b)
                tt(xnT_l[:].rearrange("p c t -> p (c t)"), bank(1), xnT_h[:].rearrange("p c t -> p (c t)"),
                   ALU.subtract).then_inc(s["xlo_done"], 1)

            def gate_b(b, j):
                t = 2 * b + j
                dve.wait_ge(s["k_ready"], t + 1)
                dve.wait_ge(s["q_copied"], t + 1)
                stt(qk, bank(5), DH ** -0.5 / (WS * WS), q_sb, ALU.mult, ALU.mult).then_inc(s["qk_done"], 1)
                dve.wait_ge(s["qk_done"], t + 1)
                reduce(bsum[:, j, bass.ds(b * HEADS, HEADS)], qk.rearrange("p (h d) -> p h d", h=HEADS), AX, ALU.add)

            def alpha(b, j, first=False):
                t = 2 * b + j
                dve.wait_ge(s["al_ready"], t + 1)
                if not (first and j == 0):
                    dve.wait_ge(s["sp_done"], t)
                stt(al, bank(6), 1.0 / WS, alpha_bias[:], ALU.mult, ALU.add).then_inc(s["al_copied"], 1)

            def gate_a(b, j):
                t = 2 * b + j
                ssteps.begin(t)
                dve.wait_ge(s["ln_done"], t + 1)
                dve.wait_ge(s["al_copied"], t + 1)
                ssteps.step(stt(al, al, 0.0, sp, ALU.max, ALU.add))
                ssteps.settle()
                ssteps.end()
                reduce(asum[:, j, bass.ds(b * HEADS, HEADS)], al.rearrange("p (h d) -> p h d", h=HEADS), AX,
                       ALU.add).then_inc(s["sp_done"], 1)

            flat_u = u[:].rearrange("p c t -> p (c t)")

            def guard_v(b):
                usteps.begin(b)
                dve.wait_ge(s["vt_ready"], b + 1)
                if not (isinstance(b, int) and b == 0):
                    dve.wait_ge(s["vh_done"], b)
                usteps.step(ts(flat_u, bank(7), 0.0, 2 * V_EPS, ALU.is_ge, ALU.mult))
                usteps.settle()
                usteps.end()
                stt(flat_u, bank(7), 1.0 / WS, flat_u, ALU.mult, ALU.add).then_inc(s["u_done"], 1)

            def split_v(b):
                dve.wait_ge(s["vh_done"], b + 1)
                dve.wait_ge(s["u_done"], b + 1)
                if not (isinstance(b, int) and b == 0):
                    dve.wait_ge(s["vo_ready"], b)
                stt(vT_l[:].rearrange("p c t -> p (c t)"), flat_u, V_EPS, vT_h[:].rearrange("p c t -> p (c t)"),
                    ALU.subtract, ALU.subtract).then_inc(s["vl_done"], 1)

            def step(b, first=False, ahead=2):
                if not first:
                    split_v(b - 1)
                if ahead >= 1:
                    normalise(b + 1, 0)
                    normalise(b + 1, 1)
                alpha(b, 0, first)
                if ahead >= 2:
                    group_stats(b + 2)
                gate_b(b, 0)
                gate_a(b, 0)
                alpha(b, 1)
                gate_b(b, 1)
                guard_v(b)
                gate_a(b, 1)
                if ahead >= 1:
                    split_xn(b + 1)

            group_stats(0)
            prologue_rest()
            normalise(0, 0)
            normalise(0, 1)
            group_stats(1)
            split_xn(0)
            step(0, first=True)
            with dve.Fori(1, B - 2) as b:
                step(b)
            step(B - 2, ahead=1)
            step(B - 1, ahead=0)
            split_v(B - 1)

            T = 2 * P
            gate = Steps(dve, s["gate_steps"], 10)
            gate.begin(0)
            dve.wait_ge(s["ba_ready"], 1)
            dve.wait_ge(s["tok_done"], TILES)
            dve.wait_ge(s["al_ready"], TILES)
            gate.step(copy(late["bT"], bank(0, T)))
            gate.step(ts(late["aT"], bank(1, T), -1.0, None, ALU.mult))
            gate.step(nc.vector.memset(late["m"][:, 0:1], NEG))
            gate.step(nc.vector.memset(late["r"][:, 0:1], 0.0))
            gate.step(nc.vector.memset(lam_slots[:, :, 0:1], 0.0))
            gate.settle()
            gate.step(scan(late["m"][:, 1:T + 1], late["aT"], late["bT"], NEG, ALU.add, ALU.max))
            gate.settle()
            gate.step(tt(late["ea"], late["aT"], late["m"][:, 0:T], ALU.add))
            gate.settle()
            tt(late["ea"], late["ea"], late["m"][:, 1:T + 1], ALU.subtract).then_inc(s["gate_args"], 1)
            tt(late["eb"], late["bT"], late["m"][:, 1:T + 1], ALU.subtract).then_inc(s["gate_args"], 1)
            dve.wait_ge(s["gate_exp"], 2)
            gate.step(scan(late["r"][:, 1:T + 1], late["ea"], late["eb"], 0.0, ALU.mult, ALU.add))
            gate.settle()
            gate.step(nc.vector.reciprocal(late["bT"], late["r"][:, 1:T + 1]))
            gate.step(tt(late["ea"], late["ea"], late["r"][:, 0:T], ALU.mult))
            gate.settle()
            gate.end()
            tt(late["lam"], late["ea"], late["bT"], ALU.mult).then_inc(s["lam_done"], 1)
            tt(lam_slots[:, :, 1:SPAN], late["ea"].rearrange("p (c s) -> p c s", c=NCH),
               late["bT"].rearrange("p (c s) -> p c s", c=NCH), ALU.mult).then_inc(s["lam_slots_done"], 1)

            esteps = Steps(dve, s["es_steps"], 2)
            hsteps = Steps(dve, s["h2_steps"], 3)

            class Chunk:

                def __init__(self, p, k):
                    self.p, self.k, self.t = p, k, 4 * p + k
                    self.first = isinstance(p, int) and p == 0

                def scan(self):
                    esteps.begin(self.t)
                    dve.wait_ge(s[f"lam_in_{self.k}"], 16 * self.p + 16)
                    scan(resp[:, 0:HEADS, :].rearrange("p h s -> p (h s)"), decay_in[:].rearrange("p h s -> p (h s)"),
                         lam_tile[:, self.k, :], 0.0, ALU.add, ALU.mult).then_inc(s["lam_used"], 1)

                def sum_heads(self):
                    dve.wait_ge(s["lam_used"], self.t + 1)
                    esteps.step(reduce(wsum[:], resp[:, :, 1:SPAN].rearrange("p h s -> p s h"), AX, ALU.add))

                def keep_ends(self):
                    k = self.k
                    if not self.first:
                        dve.wait_ge(s["l_ready"], self.p)
                    col = 64 * (k // 2) + CH * (k % 2)
                    end = resp[:, 0:HEADS, CH:SPAN].rearrange("p h s -> p (h s)")
                    esteps.step(stt(ends[:, k, col:col + CH].rearrange("p (c h) -> p c h", c=CT),
                                    repeated(end, [P, CT, HEADS]), last_row[:], mask4[:], ALU.add, ALU.mult))

                def spread(self):
                    esteps.settle()
                    esteps.end()
                    tt(wbd[:, self.k, :].rearrange("p (c s) -> p c s", c=CT), repeated(wsum[:], [P, CT, CH]),
                       chunk_mask[:], ALU.mult).then_inc(s["es_ready"], 1)

            def head_decays(p):
                dve.wait_ge(s["lam_head_in"], 32 * p + 32)
                scan(qst[:], head_state_in[:], lam_head, 0.0, ALU.add, ALU.mult).then_inc(s["q_done"], 1)

            def normalise2(t, k):
                row = rows[:, bass.ds(t, 1), :].rearrange("p a b -> p (a b)")
                stats = sm[:, 2 * (k % 2):2 * (k % 2) + 2]
                dve.wait_ge(s["rstd2_ready"], t + 1)
                if not (isinstance(t, int) and t < 2):
                    dve.wait_ge(s["t2_ready"], t - 1)
                ts(xn2[:, k % 2, :], row[:, 0:D], stats[:, 0:1], stats[:, 1:2], ALU.subtract,
                   ALU.mult).then_inc(s["xn2_ready"], 1)
                copy(row[:, D + 1:D + 3], stats)

            def slot(p, k, ahead):
                t = 4 * p + k
                chunk = Chunk(p + 1, k)
                hsteps.begin(t)
                row = rows[:, bass.ds(t, 1), :].rearrange("p a b -> p (a b)")
                stats = sm[:, 2 * (k % 2):2 * (k % 2) + 2]
                mean, rstd = stats[:, 0:1], stats[:, 1:2]
                if ahead:
                    chunk.scan()
                dve.wait_ge(s["out_ready"], t + 1)
                tt(row[:, 0:D], bank(2 + k % 2, D), row[:, 0:D], ALU.add).then_inc(s["h2_done"], 1)
                if ahead and k == 3:
                    head_decays(p + 1)
                if not (isinstance(p, int) and t == 0):
                    normalise2(t - 1, (k + 1) % 2)
                if ahead:
                    chunk.sum_heads()
                dve.wait_ge(s["h2_done"], apart(dve, t + 1))
                hsteps.step(nc.vector.bn_stats(lst6[:], row[:, 0:D]))
                if ahead:
                    chunk.keep_ends()
                hsteps.settle(apart)
                hsteps.step(nc.vector.bn_aggr(stats, lst6[:]))
                if ahead:
                    chunk.spread()
                hsteps.settle()
                hsteps.step(ts(rstd, rstd, LN_EPS, None, ALU.add))
                hsteps.end()

            def pair(p, ahead=True):
                for k in range(4):
                    slot(p, k, ahead)

            dve.wait_ge(s["consts2"], 1)
            head_decays(0)
            for k in range(4):
                chunk = Chunk(0, k)
                chunk.scan()
                chunk.sum_heads()
                chunk.keep_ends()
                chunk.spread()
            pair(0)
            with dve.Fori(1, 7) as p:
                pair(p)
            pair(7, ahead=False)
            normalise2(TILES - 1, 1)

            T8 = [P, TILES, E]
            r = Steps(dve, s["r_steps"], 32)
            r.begin(0)
            dve.wait_ge(s["lg_done"], TILES)
            r.step(copy(lg.rearrange("p t e -> p (t e)"), bank(7, TILES * E)))
            r.step(nc.vector.memset(zer, 0.0))
            r.settle()
            r.step(reduce(mx, lg, AX, ALU.max))
            r.settle()
            tt(t8, lg, wide(mx, T8), ALU.subtract).then_inc(s["r_args"], 1)
            r.step(tt(oh, lg, wide(mx, T8), ALU.is_ge))
            r.settle()
            r.step(tt(oh, oh, repeated(rank_w[:], T8), ALU.mult))
            r.settle()
            r.step(reduce(mw, oh, AX, ALU.max))
            r.settle()
            r.step(tt(oh, repeated(rank_w[:], T8), wide(mw, T8), ALU.is_equal))
            r.settle()
            tt(oh, oh, wide(valid[:], T8), ALU.mult).then_inc(s["oh_ready"], 1)
            dve.wait_ge(s["r_exp"], 1)
            r.step(reduce(sumexp, t8, AX, ALU.add))
            r.settle()
            r.step(nc.vector.reciprocal(rows[:, :, D:D + 1].rearrange("p t c -> p (t c)"), sumexp))
            dve.wait_ge(s["counts"], 1)
            r.step(copy(tot.rearrange("p t e -> p (t e)"), bank(1, TILES * E)))
            r.settle()
            for e in range(E):
                r.step(scan(cum[:, :, e], tot[:, :, e], zer[:, 0:TILES], 0.0, ALU.add, ALU.add))
            r.settle()
            r.step(tt(t8, cum, tot, ALU.subtract))
            over_thr = lg.rearrange("p t e -> p (t e)").rearrange("p (e t) -> p e t", e=E)
            r.step(tt(over_thr, wide(cum[:, TILES - 1, :], [P, E, 32]), repeated(thr[:], [P, E, 32]), ALU.is_gt))
            r.settle()
            r.step(reduce(ntile, over_thr, AX, ALU.add))
            r.settle()
            r.step(scan(tend, ntile, zer[:, 0:E], 0.0, ALU.add, ALU.add))
            r.settle()
            r.step(tt(tstart, tend, ntile, ALU.subtract))
            r.settle()
            r.step(ts(tstart, tstart, float(P), None, ALU.mult))
            flat8 = t8.rearrange("p t e -> p (t e)")
            r.step(tt(flat8, bank(0, TILES * E), flat8, ALU.add))
            r.settle()
            r.step(tt(t8, t8, repeated(tstart, T8), ALU.add))
            r.settle()
            r.step(tt(t8, t8, oh, ALU.mult))
            r.settle()
            r.step(reduce(posf, t8, AX, ALU.add))
            r.settle()
            r.step(tt(posf, posf, pad_pos[:], ALU.add))
            r.settle()
            r.step(copy(posi, posf))
            S7 = [P, SLOTS, E - 1]
            r.step(tt(cmp8[:, :, 0:E - 1], wide(slot_no[:], S7), repeated(tend[:, 0:E - 1], S7), ALU.is_ge))
            r.settle()
            r.step(reduce(slotf, cmp8[:, :, 0:E - 1], AX, ALU.add))
            r.settle()
            r.end()
            copy(sloti, slotf).then_inc(s["route_ready"], 1)
            dve.wait_ge(s["route_ready"], 1)

            def norm_rows(i, w, g):
                dve.wait_ge(s[f"row_in_{w}"], 16 * g + 16)
                if not (isinstance(i, int) and i == 0):
                    dve.wait_ge(s["xdt_ready"], i)
                ts(xnD, xr[:, w, 0:D], xr[:, w, D + 1:D + 2], xr[:, w, D + 2:D + 3], ALU.subtract,
                   ALU.mult).then_inc(s["xd_ready"], 1)

            def split_rows(i):
                dve.wait_ge(s["xdh_done"], i + 1)
                if not (isinstance(i, int) and i == 0):
                    dve.wait_ge(s["m1_ready"], i)
                tt(xl.rearrange("p c t -> p (c t)"), bank(2, D), xh.rearrange("p c t -> p (c t)"),
                   ALU.subtract).then_inc(s["xdl_done"], 1)

            def split_gelu(i, w):
                dve.wait_ge(s["gh_done"], i + 1)
                if not (isinstance(i, int) and i < 2):
                    dve.wait_ge(s["m2_ready"], i - 1)
                tt(gl[:, w].rearrange("p f t -> p (f t)"), bank(4 + w), gh[:, w].rearrange("p f t -> p (f t)"),
                   ALU.subtract).then_inc(s["g_done"], 1)

            def finish(i, w, g):
                dve.wait_ge(s["m2_ready"], i + 1)
                if not (isinstance(i, int) and i < RING):
                    dve.wait_ge(s[f"y_out_{w}"], 16 * g)
                stt(yo[:, w, :], bank(3, D), xr[:, w, D:D + 1], xr[:, w, 0:D], ALU.mult, ALU.add).then_inc(s["y_steps"], 1)
                copy(oid[:, w:w + 1], xr[:, w, D + 3:D + 4].bitcast(I32)).then_inc(s["y_done"], 1)

            def slots(g, count=RING, first=False, last=False):
                for w in range(count):
                    i = RING * g + w
                    if not (last and w == count - 1):
                        split_rows(i + 1)
                    if not (last and w >= count - 2):
                        norm_rows(i + 2, (w + 2) % RING, g if w + 2 < RING else g + 1)
                    if not (first and w == 0):
                        split_gelu(i - 1, (w - 1) % 2)
                    if not (first and w < 2):
                        finish(i - 2, (w - 2) % RING, g - 1 if w < 2 else g)

            norm_rows(0, 0, 0)
            split_rows(0)
            norm_rows(1, 1, 0)
            slots(0, first=True)
            with dve.Fori(1, ROUNDS) as g:
                slots(g)
            slots(ROUNDS, REST, last=True)
            split_gelu(SLOTS - 1, (REST - 1) % 2)
            finish(SLOTS - 2, REST - 2, ROUNDS)
            finish(SLOTS - 1, REST - 1, ROUNDS)

        @block.gpsimd
        def _(pool):
            g = nc.gpsimd
            ptt = g.tensor_tensor
            made = Steps(pool, s["const_steps_p"], 1000)
            made.begin(0)

            def clear(ap, value=0.0):
                made.step(g.memset(ap, value))

            def select(ap, pattern, base, cm, op, fill):
                made.settle()
                made.step(g.affine_select(out=ap, in_=ap, pattern=pattern, compare_op=op, fill=fill, base=base,
                                          channel_multiplier=cm))

            NE, GE = ALU.not_equal, ALU.is_ge
            for ap in (ident, shift, corner):
                clear(ap[:])
            select(ident[:], [[-1, P]], 0, 1, NE, 1.0)
            select(shift[:], [[-1, P]], -1, 1, NE, 1.0)
            for ap in (ones, one_col):
                clear(ap[:], 1.0)
            clear(minus_half[:], -0.5)
            clear(plus_half[:], 0.5)
            clear(minus_veps[:], -V_EPS)
            clear(minus_low[:])
            select(minus_low[:], [[0, 1]], E - 1, -1, GE, -1.0)
            made.settle()
            g.memset(corner[0:1, P - 1:P], 1.0).then_inc(s["consts"], 1)

            pool.wait_ge(s["router_norm"], 1)
            ptt(wg_norm[:, 1:2], wg_norm[:, 0:1], plus_half[:], ALU.pow).then_inc(s["router_root"], 1)

            for ap in (chunk_mask, mask4, last_row, decay_in, resp, init_rows, pad_pos,
                       head_state_in, wsum, pick_expert, ends):
                clear(ap[:])
            for ap in (before, valid):
                clear(ap[:], 1.0)
            for e in range(E):
                clear(rank_w[:, e:e + 1], float(E - e))
            select(before[:], [[1, P]], -1, -1, GE, 0.0)
            for half in range(2):
                select(pick_expert[:], [[-1, E], [0, P]], -E * half, 1, NE, 1.0)
            for q in range(CT):
                quad = slice(CH * q, CH * q + CH)
                clear(chunk_mask[quad, q, :], 1.0)
                clear(mask4[quad, q, :], 1.0)
                select(last_row[quad, :], [[0, 1]], -(CH - 1), 1, NE, 1.0)
                select(decay_in[quad], [[0, HEADS], [-1, SPAN]], 1, 1, NE, -1.0)
                select(decay_in[quad], [[0, HEADS], [-1, SPAN]], 2, 1, NE, 1.0)
                select(resp[quad, HEADS, :], [[-1, SPAN]], 1, 1, NE, float(HEADS))
            made.settle()
            for q in range(2):
                half = head_state_in[64 * q:64 * q + 64, CH::CH]
                clear(half, 1.0)
                select(half, [[-HEADS, NCH - 1]], 0, 1, GE, 0.0)
                select(half, [[HEADS, NCH - 1]], HEADS - 1, -1, GE, 0.0)
            select(valid[:], [[0, B], [1, 2]], -P, 1, NE, 0.0)
            select(pad_pos[:], [[0, B], [1, 2]], -P, 1, NE, float(OUT_OF_RANGE))
            made.step(g.iota(ii[:, 0:32], pattern=[[P, 32]], base=0, channel_multiplier=0))
            made.settle()
            made.step(g.tensor_copy(thr[:], ii[:, 0:32]))
            made.settle()
            made.step(g.iota(ii[:, 0:SLOTS], pattern=[[1, SLOTS]], base=0, channel_multiplier=0))
            made.settle()
            made.step(g.tensor_copy(slot_no[:], ii[:, 0:SLOTS]))
            made.step(g.iota(rows[:, :, D + 3:D + 4].bitcast(I32), pattern=[[NTOK, B], [P, 2]], base=0, channel_multiplier=1))
            made.settle()
            g.iota(init_rows[:, D + 3:D + 4].bitcast(I32), pattern=[[0, 1]], base=OUT_OF_RANGE,
                   channel_multiplier=0).then_inc(s["consts2"], 1)

            def roots(b, j):
                t = 2 * b + j
                for n, (src, dst) in enumerate(((4, 5), (7, 8))):
                    pool.wait_ge(s["var_ready"], 2 * t + n + 1)
                    ptt(sm[:, dst:dst + 1], sm[:, src:src + 1], minus_half[:], ALU.pow).then_inc(s["rstd_ready"], 1)

            def expert_lo(n):
                pool.wait_ge(s["w_hi"], apart(pool, 2 * n + 1))
                ptt(w1l[:, n, :], stage1[:], w1h[:, n, :], ALU.subtract).then_inc(s["w_lo"], 1)
                pool.wait_ge(s["w_hi"], apart(pool, 2 * n + 2))
                two = lambda w: w[:, bass.ds(2 * n, 2), :].rearrange("p q d -> p (q d)")
                ptt(two(w2l), stage2[:], two(w2h), ALU.subtract).then_inc(s["w_lo"], 1)

            roots(0, 0)
            roots(0, 1)
            with pool.Fori(0, B - 1) as b:
                roots(b + 1, 0)
                roots(b + 1, 1)
                expert_lo(b)
            expert_lo(B - 1)

            def root2(t, w):
                pool.wait_ge(s["h2_steps"], 3 * t + 3)
                ptt(sm[:, 2 * w + 1:2 * w + 2], sm[:, 2 * w + 1:2 * w + 2], minus_half[:], ALU.pow).then_inc(s["rstd2_ready"], 1)

            with pool.Fori(0, TILES // 2) as h:
                root2(2 * h, 0)
                root2(2 * h + 1, 1)

            pool.wait_ge(s["route_ready"], 1)
            pool.wait_ge(s["init_out"], 16 * SLOTS)
            for t in range(TILES):
                pool.indirect_dma_start(routed, bass.IndirectOffsetOnAxis(ap=posi[:, t:t + 1].bitcast(U32), axis=0),
                                        rows[:, t, :], None, bounds_check=SLOTS * P - 1,
                                        oob_is_err=False).then_inc(s["scattered"], 16)
            def store(i, w):
                pool.wait_ge(s["y_done"], apart(pool, i + 1))
                pool.indirect_dma_start(out_rows, bass.IndirectOffsetOnAxis(ap=oid[:, w:w + 1].bitcast(U32), axis=0),
                                        yo[:, w, :], None, bounds_check=B * NTOK - 1,
                                        oob_is_err=False).then_inc(s[f"y_out_{w}"], 16)

            with pool.Fori(0, ROUNDS) as g_:
                for w in range(RING):
                    store(RING * g_ + w, w)
            for w in range(REST):
                store(RING * ROUNDS + w, w)
            for w in range(RING):
                pool.wait_ge(s[f"y_out_{w}"], 16 * (ROUNDS + (w < REST)))


def kernel(x, L0_tok_W, L0_tok_b, L0_tok_gamma, L0_tok_beta, L0_attn_W_q, L0_attn_W_k, L0_attn_W_v,
           L0_attn_W_alpha_w, L0_attn_W_alpha_b, L0_attn_W_o, L0_ffn_w_red, L0_ffn_wg, L0_ffn_W1,
           L0_ffn_b1, L0_ffn_W2, L0_ffn_b2):
    import concourse.bacc as bacc
    from concourse.bass_utils import run_bass_kernel_spmd

    given = dict(x=x, tok_W=L0_tok_W, tok_b=L0_tok_b, tok_gamma=L0_tok_gamma, tok_beta=L0_tok_beta,
                 W_q=L0_attn_W_q, W_k=L0_attn_W_k, W_v=L0_attn_W_v, W_aw=L0_attn_W_alpha_w,
                 W_ab=L0_attn_W_alpha_b, W_o=L0_attn_W_o, w_red=L0_ffn_w_red, wg=L0_ffn_wg,
                 W1=L0_ffn_W1, b1=L0_ffn_b1, W2=L0_ffn_W2, b2=L0_ffn_b2)
    nc = bacc.Bacc("TRN2", target_bir_lowering=False, num_devices=1)
    arrays, args = {}, []
    for name, value in given.items():
        a = np.ascontiguousarray(value)
        arrays["in_" + name] = a
        args.append(nc.dram_tensor("in_" + name, a.shape, mybir.dt.from_np(a.dtype), kind="ExternalInput").ap())
    args.append(nc.dram_tensor("out", (B, NTOK, D), F32, kind="ExternalOutput").ap())
    build(nc, *args)
    return run_bass_kernel_spmd(nc, [arrays], core_ids=[0]).results[0]["out"]
```

```python
from contextlib import ExitStack

import numpy as np

import concourse.bass as bass
from concourse import mybir

F32 = mybir.dt.float32
F16 = mybir.dt.float16
I32 = mybir.dt.int32
U32 = mybir.dt.uint32
ALU = mybir.AluOpType
ACT = mybir.ActivationFunctionType
AX = mybir.AxisListType.X

P = 128
B, L, DIN = 16, 2048, 64
STRIDE, PATCH = 8, 16
GROUP = STRIDE * DIN
NG = L // STRIDE
NTOK = (L - PATCH) // STRIDE + 1
KG = GROUP // P
KC = 2 * KG
D = 256
DC = D // P
HEADS, DH = 8, 64
HD = HEADS * DH
E, FF = 8, 512
FC = FF // P
TILES = 2 * B
PAIRS = B // 2
CH = 32
NCH = 2 * P // CH
CT = P // CH
ROWC = D + 2
SLOTS = (B * NTOK + E * (P - 1)) // P
RING = 6
ROUNDS, REST = divmod(SLOTS, RING)
LN_EPS = 1e-5
V_EPS = 1e-8
NEG = -1.0e30
OUT_OF_RANGE = 1 << 20
ROUND = 1.5 * 2 ** 23
WS = 64.0
SPAN = CH + 1


class Steps:

    def __init__(self, engine, sem, per):
        self.engine, self.sem, self.per = engine, sem, per

    def begin(self, n):
        self.base, self.done = n * self.per, 0

    def step(self, instruction):
        instruction.then_inc(self.sem, 1)
        self.done += 1

    def settle(self, hold=lambda engine, value: value):
        self.engine.wait_ge(self.sem, hold(self.engine, self.base + self.done))

    def end(self):
        assert self.done == self.per, (self.done, self.per)


def build(nc, x, tok_W, tok_b, tok_gamma, tok_beta, W_q, W_k, W_v, W_aw, W_ab, W_o,
          w_red, wg, W1, b1, W2, b2, out):
    with ExitStack() as ctx:
        def sb(name, shape, dt=F32):
            return ctx.enter_context(nc.sbuf_tensor(name, shape, dt))

        def sem(name):
            return ctx.enter_context(nc.semaphore(name))

        token_rows = nc.dram_tensor("token_rows", [B, NTOK, ROWC], F32, kind="Internal").ap()
        lam_by_chunk = nc.dram_tensor("lam_by_chunk", [NCH, B, HEADS, SPAN], F32, kind="Internal").ap()
        lam_by_head = nc.dram_tensor("lam_by_head", [B * HEADS, 2 * P], F32, kind="Internal").ap()
        out_rows = out.rearrange("b n d -> (b n) d")

        banks = ctx.enter_context(nc.psum_tensor("banks", [P, 8, 512], F32))

        rows = sb("rows", [P, TILES, ROWC])
        vo = sb("vo", [P, TILES, D])
        w1h = sb("w1h", [P, E * DC, FF], F16)
        w1l = sb("w1l", [P, E * DC, FF], F16)
        w2h = sb("w2h", [P, E * FC, D], F16)
        w2l = sb("w2l", [P, E * FC, D], F16)
        bsum = sb("bsum", [P, 2, B * HEADS])
        asum = sb("asum", [P, 2, B * HEADS])
        wrg = sb("wrg", [P, DC, E])
        ident = sb("ident", [P, P])
        shift = sb("shift", [P, P])
        corner = sb("corner", [P, P])
        ones = sb("ones", [P, P])
        before = sb("before", [P, P])
        chunk_mask = sb("chunk_mask", [P, CT, CH])
        mask4 = sb("mask4", [P, CT, HEADS])
        last_row = sb("last_row", [P, 1])
        decay_in = sb("decay_in", [P, HEADS, SPAN])
        head_state_in = sb("head_state_in", [P, 2 * P])
        one_col = sb("one_col", [P, 1])
        minus_half = sb("minus_half", [P, 1])
        plus_half = sb("plus_half", [E, 1])
        minus_veps = sb("minus_veps", [P, 1])
        colsum = sb("colsum", [P, D])
        tok_bias = sb("tok_bias", [P, D])
        alpha_bias = sb("alpha_bias", [P, HD])
        bias_hl = sb("bias_hl", [2 * E, FF + D], F16)
        minus_low = sb("minus_low", [2 * E, 1])
        pick_expert = sb("pick_expert", [2 * E, E, P], F16)

        early = sb("early", [P, 6272])
        wtok = early[:, 0:2048].rearrange("p (k d) -> p k d", k=KC)
        gT = early[:, 2048:3076].rearrange("p (k g) -> p k g", k=KG)
        xg = early[:, 3076:4100].rearrange("p (j r) -> p j r", j=2)
        q_sb = early[:, 4100:4612]
        qk = early[:, 4612:5124]
        al = early[:, 5124:5636]
        sp = early[:, 5636:6148]
        beta_wide = early[:, 4100:5124].rearrange("p (k m) -> p k m", k=KC)
        proj = sb("proj", [P, 3072])
        wqka_h = proj[:, 0:1536].bitcast(F16).rearrange("p (c o) -> p c o", c=DC)
        wqka_l = proj[:, 1536:3072].bitcast(F16).rearrange("p (c o) -> p c o", c=DC)
        wv_h = sb("wv_h", [P, DC, D], F16)
        wv_l = sb("wv_l", [P, DC, D], F16)
        wo_h = sb("wo_h", [P, DC, D], F16)
        wo_l = sb("wo_l", [P, DC, D], F16)
        xn = sb("xn", [P, 2, D])
        xnT_h = sb("xnT_h", [P, DC, 2 * P], F16)
        xnT_l = sb("xnT_l", [P, DC, 2 * P], F16)
        u = sb("u", [P, DC, 2 * P])
        vT_h = sb("vT_h", [P, DC, 2 * P], F16)
        vT_l = sb("vT_l", [P, DC, 2 * P], F16)
        bias_in = early[0:2 * E, 5124:5124 + FF + D]
        bias_hi = u[0:2 * E].rearrange("p c t -> p (c t)")[:, 0:(FF + D) // 2].bitcast(F16)
        gst6 = sb("gst6", [P, 2, 6])
        gst = sb("gst", [P, 2, 2])
        lst6 = sb("lst6", [P, 6])
        sm = sb("sm", [P, 12])
        stage1 = sb("stage1", [P, 512])
        stage2 = sb("stage2", [P, 512])
        gam_raw = sb("gam_raw", [P, PATCH])
        bet_raw = sb("bet_raw", [P, PATCH])
        gam = sb("gam", [P, KC])
        bet = sb("bet", [P, KC])

        late = {}
        at = 0
        for name, cols in (("bT", 256), ("aT", 256), ("m", 257), ("ea", 256), ("eb", 256), ("r", 257), ("lam", 256)):
            late[name] = proj[:, at:at + cols]
            at += cols
        lam_slots = proj[:, at:at + NCH * SPAN].rearrange("p (c s) -> p c s", c=NCH)
        lam_tile = early[:, 0:4 * HEADS * SPAN].rearrange("p (k f) -> p k f", k=4)
        lam_head = early[:, 4 * HEADS * SPAN:4 * HEADS * SPAN + 2 * P]
        resp = sb("resp", [P, HEADS + 1, SPAN])
        wsum = sb("wsum", [P, 2, CH])
        wbd = sb("wbd", [P, 4, P])
        ends = sb("ends", [P, 4, P])
        qst = sb("qst", [P, 2 * P])
        lgT = early[0:E, 1536:1536 + P]
        lst = sb("lst", [P, D])
        xn2 = xn
        xT2 = u

        flat = vo[:].rearrange("p t d -> p (t d)")
        at = 0

        def over(cols):
            nonlocal at
            at += cols
            assert at <= TILES * D
            return flat[:, at - cols:at]

        lg = over(256).rearrange("p (t e) -> p t e", e=E)
        oh = over(256).rearrange("p (t e) -> p t e", e=E)
        t8 = over(256).rearrange("p (t e) -> p t e", e=E)
        tot = over(256).rearrange("p (t e) -> p t e", e=E)
        cum = over(256).rearrange("p (t e) -> p t e", e=E)
        cmp8 = over(SLOTS * E).rearrange("p (i e) -> p i e", e=E)
        rt = over(32 * 4)
        mx, mw, sumexp, posf = (rt[:, 32 * i:32 * i + 32] for i in range(4))
        r8 = over(8 * 4)
        ntile, tend, tstart, _ = (r8[:, 8 * i:8 * i + 8] for i in range(4))
        slotf = over(SLOTS)
        posd, magic = over(32), over(32)
        slot_of, place_of = (over(16).bitcast(F16) for _ in range(2))
        score = over(32)
        score_parts = over(32).bitcast(F16).rearrange("p (h t) -> p h t", h=2)
        in_slot = early[:, 4096:4096 + TILES * SLOTS // 2].bitcast(F16).rearrange("p (t i) -> p t i", t=TILES)
        carried = early[:, 1536:1536 + 2 * TILES * SLOTS].bitcast(F16).rearrange("p (t v i) -> p t v i", t=TILES, v=4)
        at_place = proj[:, 0:TILES * P // 2].bitcast(F16).rearrange("p (t j) -> p t j", t=TILES)
        found = over(4 * SLOTS).rearrange("p (v i) -> p v i", v=4)
        id1, empty, slot_id = over(SLOTS), over(SLOTS), over(SLOTS)
        slot_score = over(SLOTS)
        gather_id = over(SLOTS).bitcast(I32)
        slot_ids = over(2 * SLOTS).bitcast(I32).rearrange("p (i v) -> p i v", v=2)
        ring_ids = over(2 * RING).bitcast(I32).rearrange("p (w v) -> p w v", v=2)
        sloti = over(SLOTS).bitcast(I32)
        xr = over(RING * ROWC).rearrange("p (w c) -> p w c", w=RING)
        xnD = over(D)
        xh = over(D // 2).bitcast(F16).rearrange("p (c t) -> p c t", c=DC)
        xl = over(D // 2).bitcast(F16).rearrange("p (c t) -> p c t", c=DC)
        gel = over(FF)
        gh = over(FF).bitcast(F16).rearrange("p (w f t) -> p w f t", w=2, f=FC)
        gl = over(FF).bitcast(F16).rearrange("p (w f t) -> p w f t", w=2, f=FC)
        yo = proj[:, 0:RING * D].rearrange("p (w d) -> p w d", w=RING)
        valid = sb("valid", [P, TILES])
        zeros = sb("zeros", [P, TILES])
        pad_pos = sb("pad_pos", [P, TILES])
        rank_w = sb("rank_w", [P, E])
        thr = sb("thr", [P, 32])
        slot_no = sb("slot_no", [P, SLOTS])
        slot_no16 = sb("slot_no16", [P, SLOTS], F16)
        ii = sb("ii", [P, P], I32)
        place = sb("place", [P, P], F16)
        id_parts = sb("id_parts", [P, 2, TILES], F16)
        wred_sb = sb("wred_sb", [P, DC, 16])
        wg_sb = sb("wg_sb", [E, 16])
        wg_sq = sb("wg_sq", [E, 16])
        wg_norm = sb("wg_norm", [E, 2])
        wbd_flat = wbd[:].rearrange("p k s -> p (k s)")
        router_T = wbd_flat[0:16, 0:D + E]
        tokc = wbd_flat[:, D:2 * D]
        tok_b_wide = lst

        raw = flat[:, 0:16 * D].rearrange("p (o c) -> p o c", c=D)

        names = """consts consts2 const_steps_p wload raw_in_0 raw_in_1 raw_in_2 raw_in_3 raw_in_4 misc_in tok_w_in wsplit_hi wsplit_lo
            beta_wide_ready bias_ready gamma_done colsum_ready tokprep
            router_norm router_root router_steps router_prep router_t router_weights router_mm
            x_in xt_ready xt_evac gst_done gst_steps tok_done h_done ln_steps var_ready rstd_ready xn_ready
            xnt_ready xhi_done xlo_done q_ready k_ready al_ready q_copied qk_done al_copied act_steps
            ln_done sp_steps sp_done vt_ready u_steps u_done vh_done vl_done vo_ready vo_copied
            w_in w_hi w_lo
            ba_ready gate_steps gate_exp gate_args lam_done lam_slots_done lam_out
            lam_in_0 lam_in_1 lam_in_2 lam_in_3 lam_used wsum_ready ends_ready es_ready l_ready l_copied out_ready h2_done h2_steps rstd2_ready
            xn2_ready t2_ready t2_evac lg_ready lg_copied lg_turned lg_done lam_head_in q_done
            r_steps r_args r_exp oh_ready counts route_ready slot_ids_ready experts_ready in_slot_ready ids_ready places_ready found_ready row_done table_in bias_split bias_done
            row_in_0 row_in_1 row_in_2 row_in_3 row_in_4 row_in_5 xd_ready xdt_ready xdh_done xdl_done m1_ready gelu_done gt_ready gh_done g_done
            m2_ready y_steps y_done y_out_0 y_out_1 y_out_2 y_out_3 y_out_4 y_out_5""".split()
        s = {n: sem(n) for n in names}

        def bank(i, n=512):
            return banks[:, i, 0:n]

        def apart(engine, value):
            if not isinstance(value, int):
                value = engine.snap(engine.to_reg(value))
            engine.wait_ge(s["consts"], 1)
            return value

        block = ctx.enter_context(nc.Block())

        @block.sync
        def _(sp_):
            def load_raw(m, w):
                rows_ = 4 if m < 3 else 2
                at = 4 * m if m < 3 else 12 + 2 * (m - 3)
                sp_.dma_start(raw[:, at:at + rows_, :], w.rearrange("(o p) c -> p o c", p=P)).then_inc(s[f"raw_in_{m}"], 16)

            for m, w in enumerate((W_q, W_k, W_aw)):
                load_raw(m, w)

            def load_x(b):
                if not (isinstance(b, int) and b == 0):
                    sp_.wait_ge(s["xt_ready"], 2 * b)
                    sp_.wait_ge(s["gst_done"], b)
                sp_.dma_start(xg, x[b].rearrange("(j g r) c -> g j (r c)", j=2, r=STRIDE)).then_inc(s["x_in"], 16)

            def load_expert_part(n):
                if not (isinstance(n, int) and n == 0):
                    sp_.wait_ge(s["w_lo"], 2 * n)
                sp_.dma_start(stage1[:], W1.rearrange("e (c p) f -> (e c) p f", p=P)[n]).then_inc(s["w_in"], 16)
                sp_.dma_start(stage2[:].rearrange("p (q d) -> p q d", q=2),
                              W2.rearrange("e (n q p) d -> (e n) p q d", q=2, p=P)[n]).then_inc(s["w_in"], 16)

            for t2 in range(2):
                half = slice(DIN * t2, DIN * t2 + DIN)
                sp_.dma_start(wtok[half], tok_W.rearrange("(d k t) o -> t d k o", k=KC, t=2)[t2]).then_inc(s["tok_w_in"], 16)
                sp_.dma_start(gam_raw[half, :], tok_gamma.rearrange("(d t) -> d t", t=PATCH)).then_inc(s["tok_w_in"], 16)
                sp_.dma_start(bet_raw[half, :], tok_beta.rearrange("(d t) -> d t", t=PATCH)).then_inc(s["tok_w_in"], 16)
            load_raw(3, W_v)
            load_raw(4, W_o)
            load_x(0)
            sp_.dma_start(tok_b_wide[:], tok_b.partition_broadcast(P)).then_inc(s["misc_in"], 16)
            sp_.dma_start(alpha_bias[:], W_ab.partition_broadcast(P)).then_inc(s["misc_in"], 16)
            sp_.dma_start(wred_sb[:], w_red.rearrange("(c p) g -> p c g", p=P)).then_inc(s["misc_in"], 16)
            sp_.dma_start(wg_sb[:], wg).then_inc(s["misc_in"], 16)
            for half in range(2):
                two = slice(E * half, E * half + E)
                sp_.dma_start(bias_in[two, 0:FF], b1).then_inc(s["misc_in"], 16)
                sp_.dma_start(bias_in[two, FF:FF + D], b2).then_inc(s["misc_in"], 16)

            load_expert_part(0)
            load_x(1)
            load_x(2)
            with sp_.Fori(3, B) as b:
                load_expert_part(b - 2)
                load_x(b)
            load_expert_part(B - 2)
            load_expert_part(B - 1)

            sp_.wait_ge(s["lam_done"], 1)
            sp_.dma_start(lam_by_head, late["lam"]).then_inc(s["lam_out"], 16)
            sp_.wait_ge(s["lam_slots_done"], 1)
            sp_.dma_start(lam_by_chunk.rearrange("c b h s -> (b h) c s"), lam_slots).then_inc(s["lam_out"], 16)
            sp_.wait_ge(s["lam_out"], 32)

            def load_tile_decays(p, k, first=False):
                if not first:
                    sp_.wait_ge(s["lam_used"], 4 * p + k - 3)
                sp_.dma_start(lam_tile[:, k, :], lam_by_chunk[CT * (k % 2):CT * (k % 2) + CT, 2 * p + k // 2]
                              .rearrange("c h s -> c (h s)").unsqueeze(1).to_broadcast([CT, CH, HEADS * SPAN])
                              ).then_inc(s[f"lam_in_{k}"], 16)

            def load_head_decays(p, first=False):
                if not first:
                    sp_.wait_ge(s["q_done"], p)
                for half in range(2):
                    sp_.dma_start(lam_head[64 * half:64 * half + 64, :],
                                  lam_by_head.rearrange("(b h) t -> b h t", h=HEADS)[2 * p + half]
                                  .unsqueeze(0).to_broadcast([NCH, HEADS, 2 * P])).then_inc(s["lam_head_in"], 16)

            for k in range(4):
                load_tile_decays(0, k, True)
            load_head_decays(0, True)
            with sp_.Fori(1, PAIRS) as p:
                for k in range(4):
                    load_tile_decays(p, k)
                load_head_decays(p)

        @block.tensor
        def _(pe):
            mm, tr = nc.tensor.matmul, nc.tensor.transpose

            pe.wait_ge(s["consts"], 1)
            for m in range(3):
                pe.wait_ge(s[f"raw_in_{m}"], 16)
                for c in range(DC):
                    for o in range(4):
                        last = tr(bank(2 * m + c)[:, o * P:o * P + P], raw[:, 4 * m + o, c * P:c * P + P], ident[:])
                    last.then_inc(s["wload"], 1)

            pe.wait_ge(s["beta_wide_ready"], 1)
            pe.wait_ge(s["wsplit_lo"], 2)
            for k in range(KC):
                last = mm(bank(1, D), beta_wide[:, k, :], wtok[:, k, :], start=(k == 0), stop=(k == KC - 1))
            last.then_inc(s["bias_ready"], 1)
            for m in range(2):
                pe.wait_ge(s[f"raw_in_{3 + m}"], 16)
                for c in range(DC):
                    for o in range(2):
                        last = tr(bank(6 + m)[:, c * D + o * P:c * D + o * P + P], raw[:, 12 + 2 * m + o, c * P:c * P + P], ident[:])
                last.then_inc(s["wload"], 1)

            def column_sums():
                pe.wait_ge(s["gamma_done"], 1)
                for k in range(KC):
                    last = mm(bank(4, D), ones[:], wtok[:, k, :], start=(k == 0), stop=(k == KC - 1))
                last.then_inc(s["colsum_ready"], 1)

            def transpose_router():
                pe.wait_ge(s["router_prep"], 1)
                for c in range(DC):
                    tr(banks[0:16, 5, c * P:c * P + P], wred_sb[:, c, :], ident[:])
                tr(banks[0:16, 5, D:D + E], wg_sb[:, :], ident[0:E, 0:E]).then_inc(s["router_t"], 1)

            def multiply_router():
                pe.wait_ge(s["router_weights"], 1)
                pe.wait_ge(s["wsplit_lo"], 8)
                for c in range(DC):
                    last = mm(banks[:, 6, c * E:c * E + E], router_T[:, c * P:c * P + P], router_T[:, D:D + E],
                              start=True, stop=True)
                last.then_inc(s["router_mm"], 1)

            def transpose_x(b, j):
                if j == 0:
                    pe.wait_ge(s["x_in"], 16 * (b + 1))
                if isinstance(b, int) and b == 0 and j == 0:
                    pe.wait_ge(s["wsplit_lo"], 6)
                else:
                    pe.wait_ge(s["xt_evac"], 2 * b + j)
                for k in range(KG):
                    last = tr(bank(0)[:, k * P:k * P + P], xg[:, j, k * P:k * P + P], ident[:])
                last.then_inc(s["xt_ready"], 1)

            def tokenise(b, j):
                if j == 0:
                    pe.wait_ge(s["xt_evac"], 2 * b + 2)
                if not (isinstance(b, int) and b == 0):
                    pe.wait_ge(s["h_done"], 2 * b + j - 1)
                for k in range(KG):
                    mm(bank(2 + j, D), gT[:, k, j * P:j * P + P], wtok[:, k, :], start=(k == 0), stop=False)
                for k in range(KG):
                    mm(bank(2 + j, D), gT[:, k, j * P + 1:j * P + 1 + P], wtok[:, KG + k, :], start=False, stop=(k == KG - 1))
                if j == 0:
                    pe.wait_ge(s["gst_done"], b + 1)
                last = mm(banks[:, 2 + j, D:D + 2], shift[:], gst[:, j, :], start=True, stop=(j == 1))
                if j == 0:
                    last = mm(banks[:, 2 + j, D:D + 2], corner[:], gst[:, 1, :], start=False, stop=True)
                last.then_inc(s["tok_done"], 1)

            def transpose_xn(b):
                if not (isinstance(b, int) and b == 0):
                    pe.wait_ge(s["xlo_done"], b)
                for j in range(2):
                    pe.wait_ge(s["xn_ready"], 2 * b + j + 1)
                    for c in range(DC):
                        last = tr(bank(1)[:, c * D + j * P:c * D + j * P + P], xn[:, j, c * P:c * P + P], ident[:])
                last.then_inc(s["xnt_ready"], 1)

            def three(dst, pairs):
                n = 3 * len(pairs)
                i = 0
                for lh, ll, rh, rl in pairs:
                    for a, c in ((lh, rh), (lh, rl), (ll, rh)):
                        last = mm(dst, a, c, start=(i == 0), stop=(i == n - 1))
                        i += 1
                return last

            def project(b, j, first=False):
                if j == 0:
                    pe.wait_ge(s["xlo_done"], b + 1)
                for m in ((1, 2, 0), (2, 0, 1))[j]:
                    rdy, free = (("q_ready", "q_copied"), ("k_ready", "qk_done"), ("al_ready", "al_copied"))[m]
                    if m == 0 and j == 0 and not first:
                        pe.wait_ge(s["vo_copied"], b)
                    if not (first and j == 0):
                        pe.wait_ge(s[free], 2 * b + j)
                    three(bank(4 + m), [(xnT_h[:, c, j * P:j * P + P], xnT_l[:, c, j * P:j * P + P],
                                         wqka_h[:, c, m * HD:m * HD + HD], wqka_l[:, c, m * HD:m * HD + HD])
                                        for c in range(DC)]).then_inc(s[rdy], 1)

            def project_v(b, first=False):
                if not first:
                    pe.wait_ge(s["u_done"], b)
                for o in range(DC):
                    last = three(bank(7)[:, o * D:o * D + D],
                                 [(wv_h[:, c, o * P:o * P + P], wv_l[:, c, o * P:o * P + P], xnT_h[:, c, :], xnT_l[:, c, :])
                                  for c in range(DC)])
                last.then_inc(s["vt_ready"], 1)

            def project_out(b):
                pe.wait_ge(s["vl_done"], b + 1)
                pe.wait_ge(s["q_copied"], 2 * b + 2)
                for j in range(2):
                    last = three(bank(4)[:, j * D:j * D + D],
                                 [(vT_h[:, c, j * P:j * P + P], vT_l[:, c, j * P:j * P + P], wo_h[:, c, :], wo_l[:, c, :])
                                  for c in range(DC)])
                last.then_inc(s["vo_ready"], 1)

            def step(b, first=False, ahead=2):
                if ahead >= 1:
                    tokenise(b + 1, 0)
                    if first:
                        transpose_xn(b)
                    tokenise(b + 1, 1)
                if not first:
                    project_out(b - 1)
                project(b, 0, first)
                if ahead >= 2:
                    transpose_x(b + 2, 0)
                project(b, 1, first)
                if ahead >= 2:
                    transpose_x(b + 2, 1)
                project_v(b, first)
                if ahead >= 1:
                    transpose_xn(b + 1)

            transpose_x(0, 0)
            transpose_x(0, 1)
            column_sums()
            transpose_router()
            tokenise(0, 0)
            multiply_router()
            tokenise(0, 1)
            transpose_x(1, 0)
            transpose_x(1, 1)
            step(0, first=True)
            with pe.Fori(1, B - 2) as b:
                step(b)
            step(B - 2, ahead=1)
            step(B - 1, ahead=0)

            pe.wait_ge(s["sp_done"], TILES)
            pe.wait_ge(s["xt_evac"], TILES)
            pe.wait_ge(s["xlo_done"], B)
            for k, src in enumerate((bsum, asum)):
                for j in range(2):
                    last = tr(banks[:, k, j * P:j * P + P], src[:, j, :], ident[:])
            last.then_inc(s["ba_ready"], 1)
            project_out(B - 1)

            def chunk_end(p, k):
                pe.wait_ge(s["ends_ready"], apart(pe, 4 * p + k + 1))
                if k == 0 and not (isinstance(p, int) and p == 0):
                    pe.wait_ge(s["l_copied"], p)
                last = mm(bank(4, D), ends[:, k, :], vo[:, 4 * p + k, :], start=(k == 0), stop=(k == 3))
                if k == 3:
                    last.then_inc(s["l_ready"], 1)

            def mix(p, k):
                t = 4 * p + k
                b2_, j = k // 2, k % 2
                if not (isinstance(p, int) and t < 2):
                    pe.wait_ge(s["h2_done"], t - 1)
                pe.wait_ge(s["es_ready"], t + 1)
                mm(bank(2 + k % 2, D), wbd[:, k, :], vo[:, t, :], start=True, stop=False)
                if k == 0:
                    pe.wait_ge(s["q_done"], p + 1)
                    pe.wait_ge(s["l_copied"], p + 1)
                mm(bank(2 + k % 2, D), qst[64 * b2_:64 * b2_ + 64, j * P:j * P + P], lst[64 * b2_:64 * b2_ + 64, :],
                   start=False, stop=True).then_inc(s["out_ready"], 1)

            def transpose_xn2(t, w):
                pe.wait_ge(s["xn2_ready"], t + 1)
                if not (isinstance(t, int) and t == 0):
                    pe.wait_ge(s["t2_evac"], t)
                for c in range(DC):
                    last = tr(bank(6)[:, c * P:c * P + P], xn2[:, w, c * P:c * P + P], ident[:])
                last.then_inc(s["t2_ready"], 1)

            def logits(t, w):
                pe.wait_ge(s["t2_evac"], t + 1)
                for c in range(DC):
                    last = mm(banks[0:E, 0, 0:P], wrg[:, c, :], xT2[:, w, c * P:c * P + P], start=(c == 0), stop=(c == DC - 1))
                last.then_inc(s["lg_ready"], 1)

            def turn_logits(t):
                pe.wait_ge(s["lg_copied"], apart(pe, t + 1))
                tr(banks[:, 1, 0:E], lgT, ident[0:E, 0:E]).then_inc(s["lg_turned"], 1)

            def pair(p, ahead=True):
                for k in range(4):
                    mix(p, k)
                    if ahead:
                        chunk_end(p + 1, k)
                    t = 4 * p + k
                    if not (isinstance(p, int) and t < 4):
                        turn_logits(t - 4)
                    if not (isinstance(p, int) and t < 3):
                        logits(t - 3, (k + 1) % 2)
                    if not (isinstance(p, int) and t < 2):
                        transpose_xn2(t - 2, k % 2)

            pe.wait_ge(s["consts2"], 1)
            pe.wait_ge(s["gate_steps"], 2)
            pe.wait_ge(s["vo_copied"], B)
            pe.wait_ge(s["qk_done"], TILES)
            pe.wait_ge(s["al_copied"], TILES)
            pe.wait_ge(s["u_done"], B)
            for k in range(4):
                chunk_end(0, k)
            pair(0)
            with pe.Fori(1, PAIRS - 1) as p:
                pair(p)
            pair(PAIRS - 1, ahead=False)
            for t in range(TILES - 4, TILES):
                turn_logits(t)
                if t < TILES - 1:
                    logits(t + 1, (t + 1) % 2)
                if t < TILES - 2:
                    transpose_xn2(t + 2, t % 2)

            pe.wait_ge(s["oh_ready"], 1)
            ohf = oh.rearrange("p t e -> p (t e)")
            mm(bank(0, 256), before[:], ohf, start=True, stop=True)
            mm(bank(1, 256), ones[:], ohf, start=True, stop=True).then_inc(s["counts"], 1)

            pe.wait_ge(s["ids_ready"], 1)
            for q in range(4):
                pe.wait_ge(s["places_ready"], q + 1)
                for t in range(8 * q, 8 * q + 8):
                    last = mm(banks[:, 5, 0:4 * SLOTS], at_place[:, t, :], carried[:, t, :, :].rearrange("p v i -> p (v i)"),
                              start=(t == 0), stop=(t == TILES - 1))
            last.then_inc(s["found_ready"], 1)

            def transpose_rows(i):
                pe.wait_ge(s["xd_ready"], i + 1)
                if not (isinstance(i, int) and i == 0):
                    pe.wait_ge(s["xdl_done"], i)
                for c in range(DC):
                    last = tr(bank(2)[:, c * P:c * P + P], xnD[:, c * P:c * P + P], ident[:])
                last.then_inc(s["xdt_ready"], 1)

            def expert_of(i):
                return pe.value_load(sloti[0:1, bass.ds(i, 1)], min_val=0, max_val=E - 1)

            def up(i, e):
                pe.wait_ge(s["xdl_done"], i + 1)
                if not (isinstance(i, int) and i == 0):
                    pe.wait_ge(s["gelu_done"], i)
                for c in range(DC):
                    for x_, w in ((xh, w1h), (xh, w1l), (xl, w1h)):
                        mm(bank(0), x_[:, c, :], w[:, bass.ds(e * DC + c, 1), :].rearrange("p a b -> p (a b)"),
                           start=(c == 0 and w is w1h and x_ is xh), stop=False)
                mm(bank(0), pick_expert[:, bass.ds(e, 1), :].rearrange("p a b -> p (a b)"), bias_hl[:, 0:FF],
                   start=False, stop=True).then_inc(s["m1_ready"], 1)

            def transpose_gelu(i, w):
                pe.wait_ge(s["gelu_done"], i + 1)
                if not (isinstance(i, int) and i < 2):
                    pe.wait_ge(s["g_done"], i - 1)
                for f in range(FC):
                    last = tr(bank(4 + w)[:, f * P:f * P + P], gel[:, f * P:f * P + P], ident[:])
                last.then_inc(s["gt_ready"], 1)

            def down(i, w, e):
                pe.wait_ge(s["g_done"], i + 1)
                if not (isinstance(i, int) and i == 0):
                    pe.wait_ge(s["y_steps"], i)
                for f in range(FC):
                    for a, w_ in ((gh, w2h), (gh, w2l), (gl, w2h)):
                        mm(bank(3, D), a[:, w, f, :], w_[:, bass.ds(e * FC + f, 1), :].rearrange("p a b -> p (a b)"),
                           start=(f == 0 and w_ is w2h and a is gh), stop=False)
                mm(bank(3, D), pick_expert[:, bass.ds(e, 1), :].rearrange("p a b -> p (a b)"), bias_hl[:, FF:FF + D],
                   start=False, stop=True).then_inc(s["m2_ready"], 1)

            def slots(g, count=RING, first=False, last=False):
                i0 = RING * g
                experts = {0: expert_of(i0)}
                for w in range(count):
                    up(i0 + w, experts[w])
                    if w + 1 < count:
                        experts[w + 1] = expert_of(i0 + w + 1)
                    if w < 2 and not first:
                        experts[w - 2] = expert_of(i0 + w - 2)
                    if not (last and w == count - 1):
                        transpose_rows(i0 + w + 1)
                    if not (first and w == 0):
                        transpose_gelu(i0 + w - 1, (w - 1) % 2)
                    if not (first and w < 2):
                        down(i0 + w - 2, w % 2, experts[w - 2])
                return experts

            pe.wait_ge(s["experts_ready"], 1)
            pe.wait_ge(s["bias_done"], 1)
            transpose_rows(0)
            slots(0, first=True)
            with pe.Fori(1, ROUNDS) as g:
                slots(g)
            experts = slots(ROUNDS, REST, last=True)
            transpose_gelu(SLOTS - 1, (REST - 1) % 2)
            down(SLOTS - 2, (REST - 2) % 2, experts[REST - 2])
            down(SLOTS - 1, (REST - 1) % 2, experts[REST - 1])

        @block.scalar
        def _(act):
            af = nc.scalar.activation
            act.preload_act_table_set("natural_log_exp_and_others")
            act.wait_ge(s["consts"], 1)
            for m in range(3):
                for c in range(DC):
                    act.wait_ge(s["wload"], 2 * m + c + 1)
                    af(wqka_h[:, c, m * HD:m * HD + HD], bank(2 * m + c), ACT.Copy, scale=WS).then_inc(s["wsplit_hi"], 1)
            for m, dst in enumerate((wv_h, wo_h)):
                act.wait_ge(s["wload"], 7 + m)
                af(dst[:].rearrange("p c o -> p (c o)"), bank(6 + m), ACT.Copy, scale=WS).then_inc(s["wsplit_hi"], 1)

            act.wait_ge(s["misc_in"], 16 * 8)
            af(bias_hi, bias_in, ACT.Copy).then_inc(s["bias_split"], 1)
            steps = Steps(act, s["act_steps"], 2)

            def keep_xT(b, j):
                act.wait_ge(s["xt_ready"], 2 * b + j + 1)
                if not (isinstance(b, int) and b == 0):
                    act.wait_ge(s["tok_done"], 2 * b)
                af(gT[:, :, j * P:j * P + P], bank(0).rearrange("p (k g) -> p k g", k=KG), ACT.Copy).then_inc(s["xt_evac"], 1)

            def split_xn(b):
                act.wait_ge(s["xnt_ready"], b + 1)
                if not (isinstance(b, int) and b == 0):
                    act.wait_ge(s["vt_ready"], b)
                af(xnT_h[:].rearrange("p c t -> p (c t)"), bank(1), ACT.Copy).then_inc(s["xhi_done"], 1)

            def copy_q(b, j, first=False):
                act.wait_ge(s["q_ready"], 2 * b + j + 1)
                if not (first and j == 0):
                    act.wait_ge(s["qk_done"], 2 * b + j)
                af(q_sb, bank(4), ACT.Copy).then_inc(s["q_copied"], 1)

            def log_part(b, j, first=False):
                t = 2 * b + j
                steps.begin(t)
                act.wait_ge(s["al_copied"], t + 1)
                if not (first and j == 0):
                    act.wait_ge(s["sp_done"], t)
                steps.step(af(sp, al, ACT.Abs))
                steps.settle()
                steps.step(af(sp, sp, ACT.Exp, scale=-1.0))
                steps.settle()
                steps.end()
                af(sp, sp, ACT.Ln, bias=one_col[:]).then_inc(s["ln_done"], 1)

            def split_v(b):
                act.wait_ge(s["u_done"], b + 1)
                if not (isinstance(b, int) and b == 0):
                    act.wait_ge(s["vo_ready"], b)
                af(vT_h[:].rearrange("p c t -> p (c t)"), u[:].rearrange("p c t -> p (c t)"), ACT.Identity,
                   bias=minus_veps[:]).then_inc(s["vh_done"], 1)

            def keep_vo(b):
                act.wait_ge(s["vo_ready"], b + 1)
                if isinstance(b, int) and b == 0:
                    act.wait_ge(s["wsplit_lo"], 8)
                af(vo[:, bass.ds(2 * b, 2), :].rearrange("p t d -> p (t d)"), bank(4), ACT.Copy,
                   scale=1.0 / WS).then_inc(s["vo_copied"], 1)

            def split_expert(n):
                act.wait_ge(s["w_in"], 32 * n + 32)
                af(w1h[:, n, :], stage1[:], ACT.Copy).then_inc(s["w_hi"], 1)
                af(w2h[:, bass.ds(2 * n, 2), :].rearrange("p q d -> p (q d)"), stage2[:], ACT.Copy).then_inc(s["w_hi"], 1)

            def step(b, first=False, ahead=2):
                if not first:
                    split_v(b - 1)
                    keep_vo(b - 1)
                if ahead == 0:
                    split_expert(b - 1)
                copy_q(b, 0, first)
                log_part(b, 0, first)
                if ahead >= 2:
                    keep_xT(b + 2, 0)
                copy_q(b, 1)
                if ahead >= 2:
                    keep_xT(b + 2, 1)
                log_part(b, 1)
                if ahead == 2:
                    split_expert(b)
                if ahead >= 1:
                    split_xn(b + 1)

            for j in range(2):
                keep_xT(0, j)
            for j in range(2):
                keep_xT(1, j)
            split_xn(0)
            step(0, first=True)
            with act.Fori(1, B - 2) as b:
                step(b)
            step(B - 2, ahead=1)
            step(B - 1, ahead=0)
            act.wait_ge(s["gate_args"], 1)
            af(late["ea"], late["ea"], ACT.Exp).then_inc(s["gate_exp"], 1)
            act.wait_ge(s["gate_args"], 2)
            af(late["eb"], late["eb"], ACT.Exp).then_inc(s["gate_exp"], 1)
            split_v(B - 1)
            keep_vo(B - 1)
            split_expert(B - 1)
            def keep_ends(p):
                act.wait_ge(s["l_ready"], p + 1)
                if not (isinstance(p, int) and p == 0):
                    act.wait_ge(s["out_ready"], 4 * p)
                af(lst[:], bank(4, D), ACT.Copy).then_inc(s["l_copied"], 1)

            def keep_xT2(t, w):
                act.wait_ge(s["t2_ready"], t + 1)
                if not (isinstance(t, int) and t < 2):
                    act.wait_ge(s["lg_ready"], t - 1)
                af(xT2[:, w, :], bank(6, D), ACT.Copy).then_inc(s["t2_evac"], 1)

            def keep_logits(t):
                act.wait_ge(s["lg_ready"], t + 1)
                af(lgT, banks[0:E, 0, 0:P], ACT.Copy).then_inc(s["lg_copied"], 1)

            def collect_logits(t):
                act.wait_ge(s["lg_turned"], t + 1)
                af(lg[:, bass.ds(t, 1), :].rearrange("p a e -> p (a e)"), banks[:, 1, 0:E], ACT.Copy).then_inc(s["lg_done"], 1)

            def store_rows(b, j):
                act.wait_ge(s["row_done"], 2 * b + j + 1)
                n = min(P, NTOK - j * P)
                act.dma_start(token_rows[b, j * P:j * P + n], rows[0:n, bass.ds(2 * b + j, 1), :].rearrange("p a b -> p (a b)")
                              ).then_inc(s["table_in"], 16)

            keep_ends(0)
            for k in range(2, 4):
                if k == 3:
                    keep_logits(0)
                keep_xT2(k - 2, k % 2)
                store_rows(0, k % 2)
            with act.Fori(1, PAIRS) as p:
                keep_ends(p)
                for k in range(4):
                    collect_logits(4 * p + k - 4)
                    keep_logits(4 * p + k - 3)
                    keep_xT2(4 * p + k - 2, k % 2)
                    store_rows(2 * p - 1 if k < 2 else 2 * p, k % 2)
            for k in range(2):
                collect_logits(TILES - 4 + k)
                keep_logits(TILES - 3 + k)
                keep_xT2(TILES - 2 + k, k)
                store_rows(B - 1, k)
            collect_logits(TILES - 2)
            keep_logits(TILES - 1)
            collect_logits(TILES - 1)

            act.wait_ge(s["r_args"], 1)
            af(t8.rearrange("p t e -> p (t e)"), t8.rearrange("p t e -> p (t e)"), ACT.Exp).then_inc(s["r_exp"], 1)
            act.preload_act_table_set("gelu_and_others")
            def split_rows(i):
                act.wait_ge(s["xdt_ready"], i + 1)
                if not (isinstance(i, int) and i == 0):
                    act.wait_ge(s["m1_ready"], i)
                af(xh.rearrange("p c t -> p (c t)"), bank(2, D), ACT.Copy).then_inc(s["xdh_done"], 1)

            def gelu(i):
                act.wait_ge(s["m1_ready"], i + 1)
                if not (isinstance(i, int) and i == 0):
                    act.wait_ge(s["gt_ready"], i)
                af(gel, bank(0), ACT.Gelu).then_inc(s["gelu_done"], 1)

            def split_gelu(i, w):
                act.wait_ge(s["gt_ready"], i + 1)
                if not (isinstance(i, int) and i < 2):
                    act.wait_ge(s["m2_ready"], i - 1)
                af(gh[:, w].rearrange("p f t -> p (f t)"), bank(4 + w), ACT.Copy).then_inc(s["gh_done"], 1)

            def slots(g, count=RING, first=False, last=False):
                for w in range(count):
                    i = RING * g + w
                    if not (last and w == count - 1):
                        split_rows(i + 1)
                    gelu(i)
                    if not (first and w == 0):
                        split_gelu(i - 1, (w - 1) % 2)

            split_rows(0)
            slots(0, first=True)
            with act.Fori(1, ROUNDS) as g:
                slots(g)
            slots(ROUNDS, REST, last=True)
            split_gelu(SLOTS - 1, (REST - 1) % 2)

        @block.vector
        def _(dve):
            tt, ts, stt = nc.vector.tensor_tensor, nc.vector.tensor_scalar, nc.vector.scalar_tensor_tensor
            copy, reduce, scan = nc.vector.tensor_copy, nc.vector.tensor_reduce, nc.vector.tensor_tensor_scan

            def wide(ap, shape):
                return ap.unsqueeze(2).to_broadcast(shape)

            def repeated(ap, shape):
                return ap.unsqueeze(1).to_broadcast(shape)

            def weights_lo(n, dst):
                dve.wait_ge(s["wsplit_hi"], n + 1)
                hi, lo = dst
                stt(lo, bank(n), WS, hi, ALU.mult, ALU.subtract).then_inc(s["wsplit_lo"], 1)

            def keep_low_parts(start, stop):
                for n in range(start, stop):
                    m, c = n // 2, n % 2
                    if n < 6:
                        weights_lo(n, (wqka_h[:, c, m * HD:m * HD + HD], wqka_l[:, c, m * HD:m * HD + HD]))
                    else:
                        hi, lo = ((wv_h, wv_l), (wo_h, wo_l))[n - 6]
                        weights_lo(n, (hi[:].rearrange("p c o -> p (c o)"), lo[:].rearrange("p c o -> p (c o)")))

            dve.wait_ge(s["consts"], 1)
            keep_low_parts(0, 2)
            dve.wait_ge(s["tok_w_in"], 96)
            prep = Steps(dve, s["router_steps"], 7)
            prep.begin(0)
            nc.vector.memset(gT[:, :, 2 * P:2 * P + 1], 0.0)
            for t2 in range(2):
                half = slice(DIN * t2, DIN * t2 + DIN)
                prep.step(copy(gam[half, :], gam_raw[half, t2::2]))
                prep.step(copy(bet[half, :], bet_raw[half, t2::2]))
            prep.settle()
            copy(beta_wide, wide(bet[:], [P, KC, P])).then_inc(s["beta_wide_ready"], 1)
            keep_low_parts(2, 6)
            dve.wait_ge(s["bias_ready"], 1)
            tt(wtok, wtok, wide(gam[:], [P, KC, D]), ALU.mult).then_inc(s["gamma_done"], 1)
            keep_low_parts(6, 8)
            dve.wait_ge(s["misc_in"], 16 * 8)
            prep.step(tt(wg_sq[:], wg_sb[:], wg_sb[:], ALU.mult))
            prep.settle()
            reduce(wg_norm[:, 0:1], wg_sq[:], AX, ALU.add).then_inc(s["router_norm"], 1)
            tt(tok_bias[:], bank(1, D), tok_b_wide[:], ALU.add)
            dve.wait_ge(s["router_root"], 1)
            prep.step(ts(wg_norm[:, 1:2], wg_norm[:, 1:2], 1e-4, None, ALU.max))
            prep.settle()
            prep.step(nc.vector.reciprocal(wg_norm[:, 0:1], wg_norm[:, 1:2]))
            prep.settle()
            prep.end()
            ts(wg_sb[:], wg_sb[:], wg_norm[:, 0:1], None, ALU.mult).then_inc(s["router_prep"], 1)

            def prologue_rest():
                dve.wait_ge(s["router_t"], 1)
                copy(router_T, banks[0:16, 5, 0:D + E]).then_inc(s["router_weights"], 1)
                copy(colsum[:], bank(4, D))
                dve.wait_ge(s["bias_split"], 1)
                stt(bias_hl[:], bias_hi, minus_low[:], bias_in, ALU.mult, ALU.add).then_inc(s["bias_done"], 1)
                dve.wait_ge(s["router_mm"], 1)
                copy(wrg[:].rearrange("p c e -> p (c e)"), banks[:, 6, 0:DC * E]).then_inc(s["tokprep"], 1)
                dve.wait_ge(s["bias_done"], 1)
                dve.wait_ge(s["tokprep"], 1)

            gsteps = Steps(dve, s["gst_steps"], 3)
            lsteps = Steps(dve, s["ln_steps"], 7)
            ssteps = Steps(dve, s["sp_steps"], 1)
            usteps = Steps(dve, s["u_steps"], 1)

            def group_sums(b, j):
                if j == 0:
                    gsteps.begin(b)
                    dve.wait_ge(s["x_in"], 16 * (b + 1))
                gsteps.step(nc.vector.bn_stats(gst6[:, j, :], xg[:, j, :]))

            def group_aggregates(b):
                if not (isinstance(b, int) and b == 0):
                    dve.wait_ge(s["tok_done"], apart(dve, 2 * b))
                gsteps.settle(apart)
                gsteps.step(nc.vector.bn_aggr(gst[:, 0, :], gst6[:, 0, :]))
                nc.vector.bn_aggr(gst[:, 1, :], gst6[:, 1, :]).then_inc(s["gst_done"], 1)
                gsteps.end()

            def group_stats(b):
                group_sums(b, 0)
                group_sums(b, 1)
                group_aggregates(b)

            def normalise(b, j, fill=()):
                at_root, at_h, at_root2 = fill or (lambda: None,) * 3
                t = 2 * b + j
                lsteps.begin(t)
                dve.wait_ge(s["tok_done"], t + 1)
                nxt = banks[:, 2 + j, D:D + 2]
                lsteps.step(tt(sm[:, 0:2], gst[:, j, :], nxt, ALU.add))
                lsteps.settle()
                lsteps.step(stt(sm[:, 3:4], sm[:, 0:1], -0.5, gst[:, j, 0:1], ALU.mult, ALU.add))
                lsteps.step(ts(sm[:, 2:3], sm[:, 1:2], 0.5, LN_EPS, ALU.mult, ALU.add))
                lsteps.settle()
                stt(sm[:, 4:5], sm[:, 3:4], sm[:, 3:4], sm[:, 2:3], ALU.mult, ALU.add).then_inc(s["var_ready"], 1)
                at_root()
                dve.wait_ge(s["rstd_ready"], 2 * t + 1)
                lsteps.step(stt(sm[:, 6:7], sm[:, 0:1], -0.5, sm[:, 5:6], ALU.mult, ALU.mult))
                lsteps.settle()
                lsteps.step(stt(tokc, colsum[:], sm[:, 6:7], tok_bias[:], ALU.mult, ALU.add))
                lsteps.settle()
                h = rows[:, bass.ds(t, 1), 0:D].rearrange("p a b -> p (a b)")
                stt(h, bank(2 + j, D), sm[:, 5:6], tokc, ALU.mult, ALU.add).then_inc(s["h_done"], 1)
                at_h()
                dve.wait_ge(s["h_done"], apart(dve, t + 1))
                lsteps.step(nc.vector.bn_stats(lst6[:], h))
                lsteps.settle(apart)
                lsteps.step(nc.vector.bn_aggr(sm[:, 9:11], lst6[:]))
                lsteps.settle()
                lsteps.end()
                ts(sm[:, 7:8], sm[:, 10:11], LN_EPS, None, ALU.add).then_inc(s["var_ready"], 1)
                at_root2()
                dve.wait_ge(s["rstd_ready"], 2 * t + 2)
                if not (isinstance(b, int) and b == 0):
                    dve.wait_ge(s["xnt_ready"], b)
                ts(xn[:, j, :], h, sm[:, 9:10], sm[:, 8:9], ALU.subtract, ALU.mult).then_inc(s["xn_ready"], 1)

            def split_xn(b):
                dve.wait_ge(s["xhi_done"], b + 1)
                if not (isinstance(b, int) and b == 0):
                    dve.wait_ge(s["vt_ready"], b)
                tt(xnT_l[:].rearrange("p c t -> p (c t)"), bank(1), xnT_h[:].rearrange("p c t -> p (c t)"),
                   ALU.subtract).then_inc(s["xlo_done"], 1)

            def gate_b_products(b, j):
                t = 2 * b + j
                dve.wait_ge(s["k_ready"], t + 1)
                dve.wait_ge(s["q_copied"], t + 1)
                stt(qk, bank(5), DH ** -0.5 / (WS * WS), q_sb, ALU.mult, ALU.mult).then_inc(s["qk_done"], 1)

            def gate_b(b, j):
                dve.wait_ge(s["qk_done"], 2 * b + j + 1)
                reduce(bsum[:, j, bass.ds(b * HEADS, HEADS)], qk.rearrange("p (h d) -> p h d", h=HEADS), AX, ALU.add)

            def alpha(b, j, first=False):
                t = 2 * b + j
                dve.wait_ge(s["al_ready"], t + 1)
                if not (first and j == 0):
                    dve.wait_ge(s["sp_done"], t)
                stt(al, bank(6), 1.0 / WS, alpha_bias[:], ALU.mult, ALU.add).then_inc(s["al_copied"], 1)

            def gate_a_terms(b, j):
                t = 2 * b + j
                ssteps.begin(t)
                dve.wait_ge(s["ln_done"], t + 1)
                dve.wait_ge(s["al_copied"], t + 1)
                ssteps.step(stt(al, al, 0.0, sp, ALU.max, ALU.add))

            def gate_a_sum(b, j):
                ssteps.settle()
                ssteps.end()
                reduce(asum[:, j, bass.ds(b * HEADS, HEADS)], al.rearrange("p (h d) -> p h d", h=HEADS), AX,
                       ALU.add).then_inc(s["sp_done"], 1)

            flat_u = u[:].rearrange("p c t -> p (c t)")

            def guard_v(b):
                usteps.begin(b)
                dve.wait_ge(s["vt_ready"], b + 1)
                if not (isinstance(b, int) and b == 0):
                    dve.wait_ge(s["vh_done"], b)
                usteps.step(ts(flat_u, bank(7), 0.0, 2 * V_EPS, ALU.is_ge, ALU.mult))
                usteps.settle()
                usteps.end()
                stt(flat_u, bank(7), 1.0 / WS, flat_u, ALU.mult, ALU.add).then_inc(s["u_done"], 1)

            def split_v(b):
                dve.wait_ge(s["vh_done"], b + 1)
                dve.wait_ge(s["u_done"], b + 1)
                if not (isinstance(b, int) and b == 0):
                    dve.wait_ge(s["vo_ready"], b)
                stt(vT_l[:].rearrange("p c t -> p (c t)"), flat_u, V_EPS, vT_h[:].rearrange("p c t -> p (c t)"),
                    ALU.subtract, ALU.subtract).then_inc(s["vl_done"], 1)

            def step(b, first=False, ahead=2):
                if not first:
                    split_v(b - 1)
                nothing = lambda: None
                last_sums = (lambda: gate_b(b - 1, 1), lambda: gate_a_terms(b - 1, 1), lambda: gate_a_sum(b - 1, 1))
                if first:
                    last_sums = (nothing,) * 3
                first_products = (lambda: alpha(b, 0, first), lambda: gate_b_products(b, 0))
                if ahead >= 1:
                    normalise(b + 1, 0, (last_sums[0], nothing, last_sums[1]))
                    normalise(b + 1, 1, (last_sums[2], *first_products))
                else:
                    for work in last_sums + first_products:
                        work()
                if ahead >= 2:
                    group_stats(b + 2)
                gate_b(b, 0)
                gate_a_terms(b, 0)
                gate_a_sum(b, 0)
                alpha(b, 1)
                gate_b_products(b, 1)
                if ahead >= 1:
                    guard_v(b)
                if ahead >= 1:
                    split_xn(b + 1)

            group_stats(0)
            prologue_rest()
            nothing = lambda: None
            normalise(0, 0, (nothing, nothing, lambda: group_sums(1, 0)))
            normalise(0, 1, (lambda: group_sums(1, 1), nothing, nothing))
            group_aggregates(1)
            split_xn(0)
            step(0, first=True)
            with dve.Fori(1, B - 2) as b:
                step(b)
            step(B - 2, ahead=1)
            step(B - 1, ahead=0)
            gate_b(B - 1, 1)
            gate_a_terms(B - 1, 1)
            gate_a_sum(B - 1, 1)

            T = 2 * P
            gate = Steps(dve, s["gate_steps"], 10)
            gate.begin(0)
            dve.wait_ge(s["ba_ready"], 1)
            dve.wait_ge(s["tok_done"], TILES)
            dve.wait_ge(s["al_ready"], TILES)
            gate.step(copy(late["bT"], bank(0, T)))
            gate.step(ts(late["aT"], bank(1, T), -1.0, None, ALU.mult))
            gate.step(nc.vector.memset(late["m"][:, 0:1], NEG))
            gate.step(nc.vector.memset(late["r"][:, 0:1], 0.0))
            gate.step(nc.vector.memset(lam_slots[:, :, 0:1], 0.0))
            gate.settle()
            gate.step(scan(late["m"][:, 1:T + 1], late["aT"], late["bT"], NEG, ALU.add, ALU.max))
            gate.settle()
            gate.step(tt(late["ea"], late["aT"], late["m"][:, 0:T], ALU.add))
            gate.settle()
            tt(late["ea"], late["ea"], late["m"][:, 1:T + 1], ALU.subtract).then_inc(s["gate_args"], 1)
            tt(late["eb"], late["bT"], late["m"][:, 1:T + 1], ALU.subtract).then_inc(s["gate_args"], 1)
            guard_v(B - 1)
            dve.wait_ge(s["gate_exp"], 2)
            gate.step(scan(late["r"][:, 1:T + 1], late["ea"], late["eb"], 0.0, ALU.mult, ALU.add))
            gate.settle()
            gate.step(nc.vector.reciprocal(late["bT"], late["r"][:, 1:T + 1]))
            gate.step(tt(late["ea"], late["ea"], late["r"][:, 0:T], ALU.mult))
            gate.settle()
            gate.end()
            tt(late["lam"], late["ea"], late["bT"], ALU.mult).then_inc(s["lam_done"], 1)
            tt(lam_slots[:, :, 1:SPAN], late["ea"].rearrange("p (c s) -> p c s", c=NCH),
               late["bT"].rearrange("p (c s) -> p c s", c=NCH), ALU.mult).then_inc(s["lam_slots_done"], 1)
            split_v(B - 1)

            hsteps = Steps(dve, s["h2_steps"], 3)

            class Chunk:

                def __init__(self, p, k):
                    self.p, self.k, self.t = p, k, 4 * p + k

                def scan(self):
                    if not (isinstance(self.t, int) and self.t == 0):
                        dve.wait_ge(s["ends_ready"], self.t)
                    dve.wait_ge(s[f"lam_in_{self.k}"], 16 * self.p + 16)
                    scan(resp[:, 0:HEADS, :].rearrange("p h s -> p (h s)"), decay_in[:].rearrange("p h s -> p (h s)"),
                         lam_tile[:, self.k, :], 0.0, ALU.add, ALU.mult).then_inc(s["lam_used"], 1)

                def sum_heads(self):
                    dve.wait_ge(s["lam_used"], self.t + 1)
                    if not (isinstance(self.t, int) and self.t < 2):
                        dve.wait_ge(s["es_ready"], self.t - 1)
                    reduce(wsum[:, self.k % 2], resp[:, :, 1:SPAN].rearrange("p h s -> p s h"), AX,
                           ALU.add).then_inc(s["wsum_ready"], 1)

                def keep_ends(self):
                    k = self.k
                    col = 64 * (k // 2) + CH * (k % 2)
                    end = resp[:, 0:HEADS, CH:SPAN].rearrange("p h s -> p (h s)")
                    stt(ends[:, k, col:col + CH].rearrange("p (c h) -> p c h", c=CT), repeated(end, [P, CT, HEADS]),
                        last_row[:], mask4[:], ALU.add, ALU.mult).then_inc(s["ends_ready"], 1)

                def spread(self):
                    dve.wait_ge(s["wsum_ready"], self.t + 1)
                    tt(wbd[:, self.k, :].rearrange("p (c s) -> p c s", c=CT), repeated(wsum[:, self.k % 2], [P, CT, CH]),
                       chunk_mask[:], ALU.mult).then_inc(s["es_ready"], 1)

            def head_decays(p):
                dve.wait_ge(s["lam_head_in"], 32 * p + 32)
                scan(qst[:], head_state_in[:], lam_head, 0.0, ALU.add, ALU.mult).then_inc(s["q_done"], 1)

            def normalise2(t, k):
                row = rows[:, bass.ds(t, 1), :].rearrange("p a b -> p (a b)")
                stats = sm[:, 2 * (k % 2):2 * (k % 2) + 2]
                dve.wait_ge(s["rstd2_ready"], t + 1)
                if not (isinstance(t, int) and t < 2):
                    dve.wait_ge(s["t2_ready"], t - 1)
                ts(xn2[:, k % 2, :], row[:, 0:D], stats[:, 0:1], stats[:, 1:2], ALU.subtract,
                   ALU.mult).then_inc(s["xn2_ready"], 1)
                copy(row[:, D:D + 2], stats).then_inc(s["row_done"], 1)

            def slot(p, k, left):
                t = 4 * p + k
                coming = Chunk(p + 1, k + 1) if k < 3 else Chunk(p + 2, 0)
                if left < 5:
                    coming = None
                hsteps.begin(t)
                row = rows[:, bass.ds(t, 1), :].rearrange("p a b -> p (a b)")
                stats = sm[:, 2 * (k % 2):2 * (k % 2) + 2]
                mean, rstd = stats[:, 0:1], stats[:, 1:2]
                if coming:
                    coming.scan()
                dve.wait_ge(s["out_ready"], t + 1)
                tt(row[:, 0:D], bank(2 + k % 2, D), row[:, 0:D], ALU.add).then_inc(s["h2_done"], 1)
                if left >= 4 and k == 3:
                    head_decays(p + 1)
                if not (isinstance(p, int) and t == 0):
                    normalise2(t - 1, (k + 1) % 2)
                if coming:
                    coming.sum_heads()
                dve.wait_ge(s["h2_done"], apart(dve, t + 1))
                hsteps.step(nc.vector.bn_stats(lst6[:], row[:, 0:D]))
                if coming:
                    coming.keep_ends()
                hsteps.settle(apart)
                hsteps.step(nc.vector.bn_aggr(stats, lst6[:]))
                if left >= 4:
                    Chunk(p + 1, k).spread()
                hsteps.settle()
                hsteps.step(ts(rstd, rstd, LN_EPS, None, ALU.add))
                hsteps.end()

            def pair(p, left=TILES):
                for k in range(4):
                    slot(p, k, left - k)

            dve.wait_ge(s["consts2"], 1)
            for t in range(5):
                chunk = Chunk(t // 4, t % 4)
                chunk.scan()
                chunk.sum_heads()
                if t == 4:
                    dve.wait_ge(s["l_ready"], 1)
                chunk.keep_ends()
                if t < 4:
                    chunk.spread()
                if t == 3:
                    head_decays(0)
            pair(0)
            with dve.Fori(1, PAIRS - 2) as p:
                pair(p)
            pair(PAIRS - 2, left=7)
            pair(PAIRS - 1, left=3)
            normalise2(TILES - 1, 1)

            T8 = [P, TILES, E]
            r = Steps(dve, s["r_steps"], 45)
            r.begin(0)
            dve.wait_ge(s["lg_done"], TILES)
            r.step(reduce(mx, lg, AX, ALU.max))
            r.settle()
            tt(t8, lg, wide(mx, T8), ALU.subtract).then_inc(s["r_args"], 1)
            r.step(tt(oh, lg, wide(mx, T8), ALU.is_ge))
            r.settle()
            r.step(tt(oh, oh, repeated(rank_w[:], T8), ALU.mult))
            r.settle()
            r.step(reduce(mw, oh, AX, ALU.max))
            r.settle()
            r.step(tt(oh, repeated(rank_w[:], T8), wide(mw, T8), ALU.is_equal))
            r.settle()
            tt(oh, oh, wide(valid[:], T8), ALU.mult).then_inc(s["oh_ready"], 1)
            dve.wait_ge(s["r_exp"], 1)
            r.step(reduce(sumexp, t8, AX, ALU.add))
            r.settle()
            r.step(nc.vector.reciprocal(score, sumexp))
            r.settle()
            r.step(copy(score_parts[:, 0], score))
            r.settle()
            r.step(tt(score_parts[:, 1], score, score_parts[:, 0], ALU.subtract))
            dve.wait_ge(s["counts"], 1)
            r.step(copy(tot.rearrange("p t e -> p (t e)"), bank(1, TILES * E)))
            r.settle()
            for e in range(E):
                r.step(scan(cum[:, :, e], tot[:, :, e], zeros[:], 0.0, ALU.add, ALU.add))
            r.settle()
            r.step(tt(t8, cum, tot, ALU.subtract))
            over_thr = lg.rearrange("p t e -> p (t e)").rearrange("p (e t) -> p e t", e=E)
            r.step(tt(over_thr, wide(cum[:, TILES - 1, :], [P, E, 32]), repeated(thr[:], [P, E, 32]), ALU.is_gt))
            r.settle()
            r.step(reduce(ntile, over_thr, AX, ALU.add))
            r.settle()
            r.step(scan(tend, ntile, zeros[:, 0:E], 0.0, ALU.add, ALU.add))
            r.settle()
            r.step(tt(tstart, tend, ntile, ALU.subtract))
            r.settle()
            r.step(ts(tstart, tstart, float(P), None, ALU.mult))
            flat8 = t8.rearrange("p t e -> p (t e)")
            r.step(tt(flat8, bank(0, TILES * E), flat8, ALU.add))
            r.settle()
            r.step(tt(t8, t8, repeated(tstart, T8), ALU.add))
            r.settle()
            r.step(tt(t8, t8, oh, ALU.mult))
            r.settle()
            r.step(reduce(posf, t8, AX, ALU.add))
            r.settle()
            r.step(tt(posf, posf, pad_pos[:], ALU.add))
            r.settle()
            r.step(ts(posd, posf, 1.0 / P, -(P - 1) / (2 * P), ALU.mult, ALU.add))
            r.settle()
            r.step(ts(magic, posd, ROUND, None, ALU.add))
            r.settle()
            r.step(ts(posd, magic, ROUND, None, ALU.subtract))
            r.settle()
            r.step(copy(slot_of, posd))
            r.step(stt(place_of, posd, -float(P), posf, ALU.mult, ALU.add))
            r.settle()
            TS = [P, TILES, SLOTS]
            tt(in_slot, wide(slot_of, TS), repeated(slot_no16[:], TS), ALU.is_equal).then_inc(s["in_slot_ready"], 1)
            dve.wait_ge(s["in_slot_ready"], 1)
            for h in range(2):
                r.step(tt(carried[:, :, 2 + h, :], in_slot, wide(score_parts[:, h], TS), ALU.mult))
            r.settle()
            for q in range(4):
                eight = slice(8 * q, 8 * q + 8)
                tt(at_place[:, eight], wide(place_of[:, eight], [P, 8, P]), repeated(place[:], [P, 8, P]),
                   ALU.is_equal).then_inc(s["places_ready"], 1)
            S7 = [P, SLOTS, E - 1]
            r.step(tt(cmp8[:, :, 0:E - 1], wide(slot_no[:], S7), repeated(tend[:, 0:E - 1], S7), ALU.is_ge))
            r.settle()
            r.step(reduce(slotf, cmp8[:, :, 0:E - 1], AX, ALU.add))
            r.settle()
            copy(sloti, slotf).then_inc(s["experts_ready"], 1)
            dve.wait_ge(s["found_ready"], 1)
            r.step(copy(found.rearrange("p v i -> p (v i)"), banks[:, 5, 0:4 * SLOTS]))
            r.settle()
            r.step(stt(id1, found[:, 0], 64.0, found[:, 1], ALU.mult, ALU.add))
            r.step(tt(slot_score, found[:, 2], found[:, 3], ALU.add))
            r.settle()
            r.step(ts(slot_id, id1, -1.0, 0.0, ALU.add, ALU.max))
            r.step(nc.vector.memset(slot_ids[:, SLOTS - RING:SLOTS, 1], 0))
            r.step(ts(empty, id1, 0.0, float(OUT_OF_RANGE), ALU.is_equal, ALU.mult))
            r.settle()
            copy(gather_id, slot_id).then_inc(s["route_ready"], 1)
            r.step(stt(id1, id1, -1.0, empty, ALU.add, ALU.add))
            r.settle()
            r.end()
            copy(slot_ids[:, :, 0], id1)
            copy(slot_ids[:, 0:SLOTS - RING, 1], slot_id[:, RING:SLOTS]).then_inc(s["slot_ids_ready"], 1)
            dve.wait_ge(s["slot_ids_ready"], 1)

            def norm_rows(i, w, g):
                dve.wait_ge(s[f"row_in_{w}"], 16 * g + 16)
                if not (isinstance(i, int) and i == 0):
                    dve.wait_ge(s["xdt_ready"], i)
                ts(xnD, xr[:, w, 0:D], xr[:, w, D:D + 1], xr[:, w, D + 1:D + 2], ALU.subtract,
                   ALU.mult).then_inc(s["xd_ready"], 1)

            def split_rows(i):
                dve.wait_ge(s["xdh_done"], i + 1)
                if not (isinstance(i, int) and i == 0):
                    dve.wait_ge(s["m1_ready"], i)
                tt(xl.rearrange("p c t -> p (c t)"), bank(2, D), xh.rearrange("p c t -> p (c t)"),
                   ALU.subtract).then_inc(s["xdl_done"], 1)

            def split_gelu(i, w):
                dve.wait_ge(s["gh_done"], i + 1)
                if not (isinstance(i, int) and i < 2):
                    dve.wait_ge(s["m2_ready"], i - 1)
                tt(gl[:, w].rearrange("p f t -> p (f t)"), bank(4 + w), gh[:, w].rearrange("p f t -> p (f t)"),
                   ALU.subtract).then_inc(s["g_done"], 1)

            def finish(i, w, g):
                dve.wait_ge(s["m2_ready"], i + 1)
                if not (isinstance(i, int) and i < RING):
                    dve.wait_ge(s[f"y_out_{w}"], 16 * g)
                stt(yo[:, w, :], bank(3, D), slot_score[:, bass.ds(i, 1)], xr[:, w, 0:D], ALU.mult,
                    ALU.add).then_inc(s["y_steps"], 1)
                copy(ring_ids[:, w, :], slot_ids[:, bass.ds(i, 1), :].rearrange("p a v -> p (a v)")).then_inc(s["y_done"], 1)

            def slots(g, count=RING, first=False, last=False):
                for w in range(count):
                    i = RING * g + w
                    if not (last and w == count - 1):
                        split_rows(i + 1)
                    if not (last and w >= count - 2):
                        norm_rows(i + 2, (w + 2) % RING, g if w + 2 < RING else g + 1)
                    if not (first and w == 0):
                        split_gelu(i - 1, (w - 1) % 2)
                    if not (first and w < 2):
                        finish(i - 2, (w - 2) % RING, g - 1 if w < 2 else g)

            norm_rows(0, 0, 0)
            split_rows(0)
            norm_rows(1, 1, 0)
            slots(0, first=True)
            with dve.Fori(1, ROUNDS) as g:
                slots(g)
            slots(ROUNDS, REST, last=True)
            split_gelu(SLOTS - 1, (REST - 1) % 2)
            finish(SLOTS - 2, REST - 2, ROUNDS)
            finish(SLOTS - 1, REST - 1, ROUNDS)

        @block.gpsimd
        def _(pool):
            g = nc.gpsimd
            ptt = g.tensor_tensor
            made = Steps(pool, s["const_steps_p"], 1000)
            made.begin(0)

            def clear(ap, value=0.0):
                made.step(g.memset(ap, value))

            def select(ap, pattern, base, cm, op, fill):
                made.settle()
                made.step(g.affine_select(out=ap, in_=ap, pattern=pattern, compare_op=op, fill=fill, base=base,
                                          channel_multiplier=cm))

            NE, GE = ALU.not_equal, ALU.is_ge
            for ap in (ident, shift, corner):
                clear(ap[:])
            select(ident[:], [[-1, P]], 0, 1, NE, 1.0)
            select(shift[:], [[-1, P]], -1, 1, NE, 1.0)
            for ap in (ones, one_col):
                clear(ap[:], 1.0)
            clear(minus_half[:], -0.5)
            clear(plus_half[:], 0.5)
            clear(minus_veps[:], -V_EPS)
            clear(minus_low[:])
            select(minus_low[:], [[0, 1]], E - 1, -1, GE, -1.0)
            made.settle()
            g.memset(corner[0:1, P - 1:P], 1.0).then_inc(s["consts"], 1)

            for ap in (chunk_mask, mask4, last_row, decay_in, resp, zeros, pad_pos,
                       head_state_in, wsum, pick_expert, ends):
                clear(ap[:])
            for ap in (before, valid):
                clear(ap[:], 1.0)
            for e in range(E):
                clear(rank_w[:, e:e + 1], float(E - e))
            select(before[:], [[1, P]], -1, -1, GE, 0.0)
            for half in range(2):
                select(pick_expert[:], [[-1, E], [0, P]], -E * half, 1, NE, 1.0)
            for q in range(CT):
                quad = slice(CH * q, CH * q + CH)
                clear(chunk_mask[quad, q, :], 1.0)
                clear(mask4[quad, q, :], 1.0)
                select(last_row[quad, :], [[0, 1]], -(CH - 1), 1, NE, 1.0)
                select(decay_in[quad], [[0, HEADS], [-1, SPAN]], 1, 1, NE, -1.0)
                select(decay_in[quad], [[0, HEADS], [-1, SPAN]], 2, 1, NE, 1.0)
                select(resp[quad, HEADS, :], [[-1, SPAN]], 1, 1, NE, float(HEADS))
            def roots(b, j):
                t = 2 * b + j
                for n, (src, dst) in enumerate(((4, 5), (7, 8))):
                    pool.wait_ge(s["var_ready"], 2 * t + n + 1)
                    ptt(sm[:, dst:dst + 1], sm[:, src:src + 1], minus_half[:], ALU.pow).then_inc(s["rstd_ready"], 1)

            def expert_lo(n):
                pool.wait_ge(s["w_hi"], apart(pool, 2 * n + 1))
                ptt(w1l[:, n, :], stage1[:], w1h[:, n, :], ALU.subtract).then_inc(s["w_lo"], 1)
                pool.wait_ge(s["w_hi"], apart(pool, 2 * n + 2))
                two = lambda w: w[:, bass.ds(2 * n, 2), :].rearrange("p q d -> p (q d)")
                ptt(two(w2l), stage2[:], two(w2h), ALU.subtract).then_inc(s["w_lo"], 1)

            made.settle()
            pool.wait_ge(s["router_norm"], 1)
            ptt(wg_norm[:, 1:2], wg_norm[:, 0:1], plus_half[:], ALU.pow).then_inc(s["router_root"], 1)
            pool.wait_ge(s["router_root"], 1)

            made.settle()
            for q in range(2):
                half = head_state_in[64 * q:64 * q + 64, CH::CH]
                clear(half, 1.0)
                select(half, [[-HEADS, NCH - 1]], 0, 1, GE, 0.0)
                select(half, [[HEADS, NCH - 1]], HEADS - 1, -1, GE, 0.0)
            select(valid[:], [[0, B], [1, 2]], -P, 1, NE, 0.0)
            select(pad_pos[:], [[0, B], [1, 2]], -P, 1, NE, float(OUT_OF_RANGE))
            made.step(g.iota(ii[:, 0:32], pattern=[[P, 32]], base=0, channel_multiplier=0))
            made.settle()
            made.step(g.tensor_copy(thr[:], ii[:, 0:32]))
            made.settle()
            made.step(g.iota(ii[:, 0:SLOTS], pattern=[[1, SLOTS]], base=0, channel_multiplier=0))
            made.settle()
            made.step(g.tensor_copy(slot_no[:], ii[:, 0:SLOTS]))
            made.settle()
            made.step(g.tensor_copy(slot_no16[:], ii[:, 0:SLOTS]))
            made.settle()
            made.step(g.iota(ii[:, 0:P], pattern=[[1, P]], base=0, channel_multiplier=0))
            made.settle()
            made.step(g.tensor_copy(place[:], ii[:, 0:P]))
            assert NTOK == 2 * P - 1
            for half, (pattern, base, cm) in enumerate((([[4, B], [2, 2]], 0, 0), ([[-1, B], [0, 2]], 1, 1))):
                made.settle()
                made.step(g.iota(ii[:, 0:TILES], pattern=pattern, base=base, channel_multiplier=cm))
                made.settle()
                last = g.tensor_copy(id_parts[:, half], ii[:, 0:TILES])
                if half == 0:
                    made.step(last)
            last.then_inc(s["consts2"], 1)
            pool.wait_ge(s["consts2"], 1)

            roots(0, 0)
            roots(0, 1)
            with pool.Fori(0, B - 1) as b:
                roots(b + 1, 0)
                roots(b + 1, 1)
                expert_lo(b)
            expert_lo(B - 1)

            def root2(t, w):
                pool.wait_ge(s["h2_steps"], 3 * t + 3)
                ptt(sm[:, 2 * w + 1:2 * w + 2], sm[:, 2 * w + 1:2 * w + 2], minus_half[:], ALU.pow).then_inc(s["rstd2_ready"], 1)

            with pool.Fori(0, TILES // 2) as h:
                root2(2 * h, 0)
                root2(2 * h + 1, 1)

            TS = [P, TILES, SLOTS]
            pool.wait_ge(s["in_slot_ready"], 1)
            ptt(carried[:, :, 0, :], in_slot, id_parts[:, 0].unsqueeze(2).to_broadcast(TS), ALU.mult)
            ptt(carried[:, :, 1, :], in_slot, id_parts[:, 1].unsqueeze(2).to_broadcast(TS), ALU.mult).then_inc(s["ids_ready"], 1)

            def load(w, ids):
                pool.indirect_dma_start(xr[:, w, :], None, token_rows.rearrange("b n c -> (b n) c"),
                                        bass.IndirectOffsetOnAxis(ap=ids.bitcast(U32), axis=0),
                                        bounds_check=B * NTOK - 1, oob_is_err=False).then_inc(s[f"row_in_{w}"], 16)

            def store(i, w):
                pool.wait_ge(s["y_done"], apart(pool, i + 1))
                pool.indirect_dma_start(out_rows, bass.IndirectOffsetOnAxis(ap=ring_ids[:, w, 0:1].bitcast(U32), axis=0),
                                        yo[:, w, :], None, bounds_check=B * NTOK - 1,
                                        oob_is_err=False).then_inc(s[f"y_out_{w}"], 16)

            pool.wait_ge(s["table_in"], 16 * TILES)
            pool.wait_ge(s["route_ready"], 1)
            for w in range(RING):
                load(w, gather_id[:, w:w + 1])
            with pool.Fori(0, ROUNDS - 1) as g_:
                for w in range(RING):
                    store(RING * g_ + w, w)
                    load(w, ring_ids[:, w, 1:2])
            for w in range(RING + REST):
                store(RING * (ROUNDS - 1) + w, w % RING)
                if w < REST:
                    load(w, ring_ids[:, w, 1:2])
            for w in range(RING):
                pool.wait_ge(s[f"y_out_{w}"], 16 * (ROUNDS + (w < REST)))


def kernel(x, L0_tok_W, L0_tok_b, L0_tok_gamma, L0_tok_beta, L0_attn_W_q, L0_attn_W_k, L0_attn_W_v,
           L0_attn_W_alpha_w, L0_attn_W_alpha_b, L0_attn_W_o, L0_ffn_w_red, L0_ffn_wg, L0_ffn_W1,
           L0_ffn_b1, L0_ffn_W2, L0_ffn_b2):
    import concourse.bacc as bacc
    from concourse.bass_utils import run_bass_kernel_spmd

    given = dict(x=x, tok_W=L0_tok_W, tok_b=L0_tok_b, tok_gamma=L0_tok_gamma, tok_beta=L0_tok_beta,
                 W_q=L0_attn_W_q, W_k=L0_attn_W_k, W_v=L0_attn_W_v, W_aw=L0_attn_W_alpha_w,
                 W_ab=L0_attn_W_alpha_b, W_o=L0_attn_W_o, w_red=L0_ffn_w_red, wg=L0_ffn_wg,
                 W1=L0_ffn_W1, b1=L0_ffn_b1, W2=L0_ffn_W2, b2=L0_ffn_b2)
    nc = bacc.Bacc("TRN2", target_bir_lowering=False, num_devices=1)
    arrays, args = {}, []
    for name, value in given.items():
        a = np.ascontiguousarray(value)
        arrays["in_" + name] = a
        args.append(nc.dram_tensor("in_" + name, a.shape, mybir.dt.from_np(a.dtype), kind="ExternalInput").ap())
    args.append(nc.dram_tensor("out", (B, NTOK, D), F32, kind="ExternalOutput").ap())
    build(nc, *args)
    return run_bass_kernel_spmd(nc, [arrays], core_ids=[0]).results[0]["out"]
```
